# Optimizing a Trainium2 kernel written in Bass

```python
import numpy as np
import jax
import jax.numpy as jnp

def _softmax(x, axis=-1):
    return jax.nn.softmax(x, axis=axis)

def _gelu(x):
    return jax.nn.gelu(x, approximate=True)

def _silu(x):
    return jax.nn.silu(x)

def _sigmoid(x):
    return jax.nn.sigmoid(x)

def _layernorm(x, axis=-1, eps=1e-05):
    m = jnp.mean(x, axis=axis, keepdims=True)
    v = jnp.var(x, axis=axis, keepdims=True)
    return (x - m) / jnp.sqrt(v + eps)

def _scatter_add(tgt, idx, src, axis=0):
    return tgt.at[idx].add(src)

def _segment_sum(src, seg, n):
    return jax.ops.segment_sum(src, seg, n)
kernel_name = 'mk_recurrent_d2_jaxref_r8_80c78b'

def setup_inputs(seed: int=0):
    np.random.seed(seed)
    _w = jnp.asarray

    def _L0_attn_setup():
        import jax, jax.numpy as jnp
        import numpy as np
        import math
        D_MODEL = 256
        NUM_HEADS = 16
        D_K = D_MODEL // NUM_HEADS
        SEQ_LEN = 256
        BATCH = 2

        def _rope_cache(s):
            half = D_K // 2
            inv_freq = 1.0 / 10000.0 ** (jnp.arange(half, dtype=jnp.float32) / half)
            angles = jnp.arange(s, dtype=jnp.float32)[:, None] * inv_freq[None, :]
            return (jnp.cos(angles), jnp.sin(angles))

        def _apply_rope(x, cos, sin):
            x_even = x[..., 0::2]
            x_odd = x[..., 1::2]
            rot_even = x_even * cos - x_odd * sin
            rot_odd = x_even * sin + x_odd * cos
            return jnp.stack((rot_even, rot_odd), axis=-1).reshape(x.shape)
        key = jax.random.key(seed)
        ks = jax.random.split(key, 9)
        sc = 1.0 / math.sqrt(D_MODEL)
        return {'x': jax.random.normal(ks[0], (BATCH, SEQ_LEN, D_MODEL), jnp.float32), 'Wq': jax.random.normal(ks[1], (D_MODEL, D_MODEL), jnp.float32) * sc, 'bq': jax.random.normal(ks[2], (D_MODEL,), jnp.float32) * 0.01, 'Wk': jax.random.normal(ks[3], (D_MODEL, D_MODEL), jnp.float32) * sc, 'bk': jax.random.normal(ks[4], (D_MODEL,), jnp.float32) * 0.01, 'Wv': jax.random.normal(ks[5], (D_MODEL, D_MODEL), jnp.float32) * sc, 'bv': jax.random.normal(ks[6], (D_MODEL,), jnp.float32) * 0.01, 'Wo': jax.random.normal(ks[7], (D_MODEL, D_MODEL), jnp.float32) * sc, 'bo': jax.random.normal(ks[8], (D_MODEL,), jnp.float32) * 0.01}
    _L0_attn_in = _L0_attn_setup()

    def _L0_ffn_setup():
        import jax, jax.numpy as jnp
        import numpy as np
        DIM = 256
        HID = 704
        ZERO_POINT = 128.0

        def _qlinear(x, wq, scale):
            W = (wq.astype(jnp.float32) - ZERO_POINT) * scale[:, None]
            return jnp.einsum('bsd,hd->bsh', x, W)
        key = jax.random.key(seed)
        ks = jax.random.split(key, 7)
        B, S = (4, 256)
        sg = jax.random.uniform(ks[1], (HID,)) * (0.02 / np.sqrt(DIM)) + 0.0001
        su = jax.random.uniform(ks[3], (HID,)) * (0.02 / np.sqrt(DIM)) + 0.0001
        sd = jax.random.uniform(ks[5], (DIM,)) * (0.02 / np.sqrt(HID)) + 0.0001
        return {'x': jax.random.normal(ks[0], (B, S, DIM), dtype=jnp.float32), 'wq_gate': jax.random.randint(ks[2], (HID, DIM), 0, 32, dtype=jnp.int32), 's_gate': sg, 'wq_up': jax.random.randint(ks[4], (HID, DIM), 0, 32, dtype=jnp.int32), 's_up': su, 'wq_down': jax.random.randint(ks[6], (DIM, HID), 0, 32, dtype=jnp.int32), 's_down': sd}
    _L0_ffn_in = _L0_ffn_setup()

    def _L1_attn_setup():
        import jax, jax.numpy as jnp
        import numpy as np
        H = 16
        KVH = 4
        G = H // KVH
        HD = 128
        D = 256
        BASE = 10000.0

        def _rope(x, cos, sin):
            half = HD // 2
            x1, x2 = (x[..., :half], x[..., half:])
            return jnp.concatenate([x1 * cos - x2 * sin, x1 * sin + x2 * cos], axis=-1)
        key = jax.random.key(seed)
        ks = jax.random.split(key, 5)
        B, S = (2, 256)
        x = jax.random.normal(ks[0], (B, S, D), dtype=jnp.float32)
        Wq = jax.random.normal(ks[1], (D, H * HD), dtype=jnp.float32) * 0.02
        Wk = jax.random.normal(ks[2], (D, KVH * HD), dtype=jnp.float32) * 0.02
        Wv = jax.random.normal(ks[3], (D, KVH * HD), dtype=jnp.float32) * 0.02
        Wo = jax.random.normal(ks[4], (H * HD, D), dtype=jnp.float32) * 0.02
        return {'x': x, 'Wq': Wq, 'Wk': Wk, 'Wv': Wv, 'Wo': Wo}
    _L1_attn_in = _L1_attn_setup()

    def _L1_ffn_setup():
        import jax, jax.numpy as jnp
        import numpy as np
        D = 256
        F = 176
        E = 8
        K = 2
        FS = 352
        B, S = (2, 128)
        key = jax.random.key(seed)
        ks = jax.random.split(key, 9)
        sc = 0.02
        return {'x': jax.random.normal(ks[0], (B, S, D), dtype=jnp.float32), 'Wr': jax.random.normal(ks[1], (E, D), dtype=jnp.float32) * sc, 'Wg': jax.random.normal(ks[2], (E, F, D), dtype=jnp.float32) * sc, 'Wu': jax.random.normal(ks[3], (E, F, D), dtype=jnp.float32) * sc, 'Wd': jax.random.normal(ks[4], (E, D, F), dtype=jnp.float32) * sc, 'Wsg': jax.random.normal(ks[5], (FS, D), dtype=jnp.float32) * sc, 'Wsu': jax.random.normal(ks[6], (FS, D), dtype=jnp.float32) * sc, 'Wsd': jax.random.normal(ks[7], (D, FS), dtype=jnp.float32) * sc}
    _L1_ffn_in = _L1_ffn_setup()
    _d = {'L0_attn_x': _L0_attn_in['x'], 'L0_attn_Wq': _L0_attn_in['Wq'], 'L0_attn_bq': _L0_attn_in['bq'], 'L0_attn_Wk': _L0_attn_in['Wk'], 'L0_attn_bk': _L0_attn_in['bk'], 'L0_attn_Wv': _L0_attn_in['Wv'], 'L0_attn_bv': _L0_attn_in['bv'], 'L0_attn_Wo': _L0_attn_in['Wo'], 'L0_attn_bo': _L0_attn_in['bo'], 'L0_ffn_wq_gate': _L0_ffn_in['wq_gate'], 'L0_ffn_s_gate': _L0_ffn_in['s_gate'], 'L0_ffn_wq_up': _L0_ffn_in['wq_up'], 'L0_ffn_s_up': _L0_ffn_in['s_up'], 'L0_ffn_wq_down': _L0_ffn_in['wq_down'], 'L0_ffn_s_down': _L0_ffn_in['s_down'], 'L1_attn_Wq': _L1_attn_in['Wq'], 'L1_attn_Wk': _L1_attn_in['Wk'], 'L1_attn_Wv': _L1_attn_in['Wv'], 'L1_attn_Wo': _L1_attn_in['Wo'], 'L1_ffn_Wr': _L1_ffn_in['Wr'], 'L1_ffn_Wg': _L1_ffn_in['Wg'], 'L1_ffn_Wu': _L1_ffn_in['Wu'], 'L1_ffn_Wd': _L1_ffn_in['Wd'], 'L1_ffn_Wsg': _L1_ffn_in['Wsg'], 'L1_ffn_Wsu': _L1_ffn_in['Wsu'], 'L1_ffn_Wsd': _L1_ffn_in['Wsd']}
    _x0 = _d['L0_attn_x']
    _d['L0_attn_x'] = jax.random.normal(jax.random.fold_in(jax.random.key(seed), 1), (1, 1024, 256), dtype=_x0.dtype)
    del _x0
    return _d

def reference(L0_attn_x, L0_attn_Wq, L0_attn_bq, L0_attn_Wk, L0_attn_bk, L0_attn_Wv, L0_attn_bv, L0_attn_Wo, L0_attn_bo, L0_ffn_wq_gate, L0_ffn_s_gate, L0_ffn_wq_up, L0_ffn_s_up, L0_ffn_wq_down, L0_ffn_s_down, L1_attn_Wq, L1_attn_Wk, L1_attn_Wv, L1_attn_Wo, L1_ffn_Wr, L1_ffn_Wg, L1_ffn_Wu, L1_ffn_Wd, L1_ffn_Wsg, L1_ffn_Wsu, L1_ffn_Wsd):

    def _L0_attn_ref(x, Wq, bq, Wk, bk, Wv, bv, Wo, bo):
        import jax, jax.numpy as jnp
        import numpy as np
        import math
        D_MODEL = 256
        NUM_HEADS = 16
        D_K = D_MODEL // NUM_HEADS
        SEQ_LEN = 256
        BATCH = 2

        def _rope_cache(s):
            half = D_K // 2
            inv_freq = 1.0 / 10000.0 ** (jnp.arange(half, dtype=jnp.float32) / half)
            angles = jnp.arange(s, dtype=jnp.float32)[:, None] * inv_freq[None, :]
            return (jnp.cos(angles), jnp.sin(angles))

        def _apply_rope(x, cos, sin):
            x_even = x[..., 0::2]
            x_odd = x[..., 1::2]
            rot_even = x_even * cos - x_odd * sin
            rot_odd = x_even * sin + x_odd * cos
            return jnp.stack((rot_even, rot_odd), axis=-1).reshape(x.shape)
        b, s, d = x.shape

        def proj(W, bias):
            y = jnp.einsum('bsd,ed->bse', x, W) + bias
            return y.reshape(b, s, NUM_HEADS, D_K).transpose(0, 2, 1, 3)
        Q, K, V = (proj(Wq, bq), proj(Wk, bk), proj(Wv, bv))
        cos, sin = _rope_cache(s)
        Q = _apply_rope(Q, cos, sin)
        K = _apply_rope(K, cos, sin)
        scores = jnp.einsum('bhqd,bhkd->bhqk', Q, K) * (1.0 / math.sqrt(D_K))
        causal = jnp.tril(jnp.ones((s, s), bool))
        scores = jnp.where(causal[None, None], scores, -jnp.inf)
        probs = jax.nn.softmax(scores, axis=-1)
        att = jnp.einsum('bhqk,bhkd->bhqd', probs, V)
        att = att.transpose(0, 2, 1, 3).reshape(b, s, d)
        return jnp.einsum('bsd,ed->bse', att, Wo) + bo

    def _L0_ffn_ref(x, wq_gate, s_gate, wq_up, s_up, wq_down, s_down):
        import jax, jax.numpy as jnp
        import numpy as np
        DIM = 256
        HID = 704
        ZERO_POINT = 128.0

        def _qlinear(x, wq, scale):
            W = (wq.astype(jnp.float32) - ZERO_POINT) * scale[:, None]
            return jnp.einsum('bsd,hd->bsh', x, W)
        gate = _qlinear(x, wq_gate, s_gate)
        gate = jax.nn.silu(gate)
        up = _qlinear(x, wq_up, s_up)
        return _qlinear(gate * up, wq_down, s_down)

    def _L1_attn_ref(x, Wq, Wk, Wv, Wo):
        import jax, jax.numpy as jnp
        import numpy as np
        H = 16
        KVH = 4
        G = H // KVH
        HD = 128
        D = 256
        BASE = 10000.0

        def _rope(x, cos, sin):
            half = HD // 2
            x1, x2 = (x[..., :half], x[..., half:])
            return jnp.concatenate([x1 * cos - x2 * sin, x1 * sin + x2 * cos], axis=-1)
        B, S, _ = x.shape
        scale = HD ** (-0.5)
        q = (x @ Wq).reshape(B, S, H, HD).transpose(0, 2, 1, 3)
        k = (x @ Wk).reshape(B, S, KVH, HD).transpose(0, 2, 1, 3)
        v = (x @ Wv).reshape(B, S, KVH, HD).transpose(0, 2, 1, 3)
        t = jnp.arange(S, dtype=x.dtype)
        inv_freq = 1.0 / BASE ** (jnp.arange(0, HD, 2, dtype=x.dtype) / HD)
        freqs = t[:, None] * inv_freq[None, :]
        cos, sin = (jnp.cos(freqs), jnp.sin(freqs))
        q = _rope(q, cos, sin)
        k = _rope(k, cos, sin)
        qg = q.reshape(B, KVH, G, S, HD)
        scores = jnp.einsum('bkgqd,bksd->bkgqs', qg, k) * scale
        causal = jnp.triu(jnp.full((S, S), -jnp.inf, dtype=x.dtype), k=1)
        scores = scores + causal
        attn = jax.nn.softmax(scores, axis=-1)
        out = jnp.einsum('bkgqs,bksd->bkgqd', attn, v)
        out = out.reshape(B, H, S, HD).transpose(0, 2, 1, 3).reshape(B, S, H * HD)
        return out @ Wo

    def _L1_ffn_ref(x, Wr, Wg, Wu, Wd, Wsg, Wsu, Wsd):
        import jax, jax.numpy as jnp
        import numpy as np
        D = 256
        F = 176
        E = 8
        K = 2
        FS = 352
        B, S = (2, 128)
        silu = jax.nn.silu
        sg = silu(jnp.einsum('bsd,fd->bsf', x, Wsg))
        su = jnp.einsum('bsd,fd->bsf', x, Wsu)
        shared_out = jnp.einsum('bsf,df->bsd', sg * su, Wsd)
        logits = jnp.einsum('bsd,ed->bse', x, Wr)
        scores = jax.nn.softmax(logits, axis=-1)
        topk_scores, topk_idx = jax.lax.top_k(scores, K)
        w_full = jnp.sum(jax.nn.one_hot(topk_idx, E, dtype=x.dtype) * topk_scores[..., None], axis=-2)
        g = silu(jnp.einsum('bsd,efd->bsef', x, Wg))
        u = jnp.einsum('bsd,efd->bsef', x, Wu)
        out_e = jnp.einsum('bsef,edf->bsed', g * u, Wd)
        routed_out = jnp.einsum('bsed,bse->bsd', out_e, w_full)
        return routed_out + shared_out
    x = L0_attn_x
    xn = _layernorm(x, axis=-1)
    s = _L0_attn_ref(xn, L0_attn_Wq, L0_attn_bq, L0_attn_Wk, L0_attn_bk, L0_attn_Wv, L0_attn_bv, L0_attn_Wo, L0_attn_bo)
    g = _silu(_L0_ffn_ref(xn, L0_ffn_wq_gate, L0_ffn_s_gate, L0_ffn_wq_up, L0_ffn_s_up, L0_ffn_wq_down, L0_ffn_s_down))
    x = x + s * g
    xn = _layernorm(x, axis=-1)
    s = _L1_attn_ref(xn, L1_attn_Wq, L1_attn_Wk, L1_attn_Wv, L1_attn_Wo)
    g = _silu(_L1_ffn_ref(xn, L1_ffn_Wr, L1_ffn_Wg, L1_ffn_Wu, L1_ffn_Wd, L1_ffn_Wsg, L1_ffn_Wsu, L1_ffn_Wsd))
    x = x + s * g
    return x

_drawn_inputs = setup_inputs


def setup_inputs(seed=0):
    import zlib

    import numpy as np

    out = dict(_drawn_inputs(seed))
    spreads = {}
    factors = {'L0_attn_Wq': 8.0,
     'L0_attn_bq': 8.0,
     'L0_attn_Wk': 8.0,
     'L0_attn_bk': 8.0,
     'L0_attn_Wv': 8.0,
     'L0_attn_bv': 8.0,
     'L0_attn_Wo': 8.0,
     'L0_attn_bo': 178.37,
     'L0_ffn_s_gate': 8.0,
     'L0_ffn_s_up': 8.0,
     'L0_ffn_s_down': 8.0,
     'L1_attn_Wq': 8.0,
     'L1_attn_Wk': 8.0,
     'L1_attn_Wv': 8.0,
     'L1_attn_Wo': 8.0,
     'L1_ffn_Wr': 8.0,
     'L1_ffn_Wg': 8.0,
     'L1_ffn_Wu': 8.0,
     'L1_ffn_Wd': 8.0,
     'L1_ffn_Wsg': 8.0,
     'L1_ffn_Wsu': 8.0,
     'L1_ffn_Wsd': 8.0}
    for name, (base, spread) in spreads.items():
        noise = np.random.default_rng([zlib.crc32(name.encode()), seed]).standard_normal(out[name].shape)
        drawn = base * np.exp(spread * noise) if base else spread * noise
        out[name] = jnp.asarray(drawn.astype(out[name].dtype))
    for name, factor in factors.items():
        out[name] = (out[name] * factor).astype(out[name].dtype)
    return out
```

```python
from contextlib import ExitStack

import numpy as np

import concourse.bass as bass
from concourse import mybir

F32, F32R = mybir.dt.float32, mybir.dt.float32r
F16, BF16, I32 = mybir.dt.float16, mybir.dt.bfloat16, mybir.dt.int32
ALU = mybir.AluOpType
ACT = mybir.ActivationFunctionType
AX = mybir.AxisListType

P = 128
T = 1024
D = 256
NT = T // P
NK = D // P
HALF = 512
NC = T // HALF
EPS = 1e-5
MASKED = -3.0e38

H0, DH0 = 16, 16
GROUPS0, GH0 = 4, 4
PARTS0 = 3
VW0 = PARTS0 * DH0
SCALE0 = DH0 ** -0.5
FT0, HID0 = 6, 704

KV1, GH1, DH1 = 4, 4, 128
SCALE1 = DH1 ** -0.5
E1, F1, FS1 = 8, 176, 352
FT1 = (E1 * F1 + 384) // P
TOPK = 2
ZERO_POINT = 128.0
WCOLS = 2 * NK * P + D
GWCOLS1 = NK * (GH1 * P + P + P)


def chunks_of(i):
    return (i * P + P + HALF - 1) // HALF


def chunks_before(units, tile_of):
    before = [0]
    for u in range(units):
        before.append(before[-1] + chunks_of(tile_of(u)))
    return before


class Scope:

    def __init__(self, nc, tag=""):
        self.nc, self.tag, self.stack = nc, tag, ExitStack()

    def __enter__(self):
        self.stack.__enter__()
        return self

    def __exit__(self, *a):
        return self.stack.__exit__(*a)

    def sb(self, name, shape, dt):
        return self.stack.enter_context(self.nc.sbuf_tensor(self.tag + name, shape, dt))

    def ps(self, name, shape, dt=F32):
        return self.stack.enter_context(self.nc.psum_tensor(self.tag + name, shape, dt))

    def sem(self, name):
        return self.stack.enter_context(self.nc.semaphore(self.tag + name))


class Count:

    def __init__(self, sem, per):
        self.sem, self.per = sem, per

    def prime(self, eng):
        eng.sem_inc(self.sem, self.per)

    def at(self, g, n):
        return g * self.per + (self.per + n)


def f32(ap):
    return ap.bitcast(F32)


def three_pass(pe, out, terms, start=True, stop=True, check=True):
    n, last = 0, None
    for a_hi, a_lo, b_hi, b_lo in terms:
        for a, b in ((a_hi, b_hi), (a_hi, b_lo), (a_lo, b_hi)):
            last = pe.matmul(out, a, b, start=start and n == 0,
                             stop=stop and n == 3 * len(terms) - 1, skip_group_check=not check)
            n += 1
    return last


def layer_norm(nc, tag, x_tok, xn_hi, xn_lo, ident, loads, side_jobs=None):
    with Scope(nc, tag) as s:
        xn = s.sb("xn_tok", [P, NT, D], F32)
        stats = s.sb("ln_stats", [P, NT, 6], F32)
        mv = s.sb("ln_mv", [P, NT, 2], F32)
        ve = s.sb("ln_ve", [P, NT], F32)
        sd = s.sb("ln_sd", [P, NT], F32)
        y = s.sb("ln_y", [P, 3, NT], F32)
        rstd = s.sb("ln_rstd", [P, NT], F32)
        xT = [s.ps(f"ln_xT{k}", [P, T]) for k in range(NK)]
        loaded = s.sem("ln_loaded")
        stats_done, small_done = s.sem("ln_stats_done"), s.sem("ln_small_done")
        sd_done, norm_done = s.sem("ln_sd_done"), s.sem("ln_norm_done")
        xT_ready, hi_done, lo_done = s.sem("ln_xT_ready"), s.sem("ln_hi_done"), s.sem("ln_lo_done")
        with nc.Block() as block:

            @block.sync
            def _(sp):
                for out, src in loads:
                    sp.dma_start(out, src).then_inc(loaded, 16)
                sp.wait_ge(loaded, 16 * len(loads))

            if side_jobs:
                @block.gpsimd
                def _(pool):
                    side_jobs(pool, loaded)

            @block.vector
            def _(dve):
                if loads:
                    dve.wait_ge(loaded, 16 * len(loads))
                for t in range(NT):
                    dve.bn_stats(stats[:, t, :], x_tok[:, t, :]).then_inc(stats_done, 1)
                for t in range(NT):
                    dve.wait_ge(stats_done, t + 1)
                    dve.bn_aggr(mv[:, t, :], stats[:, t, :]).then_inc(stats_done, 1)
                dve.wait_ge(stats_done, 2 * NT)
                dve.tensor_scalar(ve[:, :], mv[:, :, 1], EPS, None, ALU.add).then_inc(small_done, 1)
                dve.wait_ge(sd_done, 1)
                dve.reciprocal(y[:, 0, :], sd[:, :]).then_inc(small_done, 1)
                dve.wait_ge(small_done, 2)
                dve.tensor_tensor(y[:, 1, :], y[:, 0, :], y[:, 0, :], ALU.mult).then_inc(small_done, 1)
                dve.wait_ge(small_done, 3)
                dve.tensor_tensor(y[:, 2, :], y[:, 1, :], ve[:, :], ALU.mult).then_inc(small_done, 1)
                dve.wait_ge(small_done, 4)
                dve.tensor_scalar(y[:, 1, :], y[:, 2, :], -0.5, 1.5, ALU.mult, ALU.add)\
                   .then_inc(small_done, 1)
                dve.wait_ge(small_done, 5)
                dve.tensor_tensor(rstd[:, :], y[:, 0, :], y[:, 1, :], ALU.mult).then_inc(small_done, 1)
                dve.wait_ge(small_done, 6)
                for t in range(NT):
                    dve.tensor_scalar(xn[:, t, :], x_tok[:, t, :], mv[:, t, 0:1], rstd[:, t:t + 1],
                                      ALU.subtract, ALU.mult).then_inc(norm_done, 1)
                n = 0
                for c in range(NC):
                    for k in range(NK):
                        n += 1
                        sl = slice(c * HALF, c * HALF + HALF)
                        dve.wait_ge(hi_done, n)
                        dve.tensor_tensor(xn_lo[:, k, sl], xT[k][:, sl], f32(xn_hi[:, k, sl]),
                                          ALU.subtract).then_inc(lo_done, 1)

            @block.tensor
            def _(pe):
                if loads:
                    pe.wait_ge(loaded, 16 * len(loads))
                for t in range(NT):
                    pe.wait_ge(norm_done, t + 1)
                    for k in range(NK):
                        last = pe.transpose(xT[k][:, t * P:t * P + P], xn[:, t, k * P:k * P + P],
                                            ident[:, :])
                    last.then_inc(xT_ready, 1)

            @block.scalar
            def _(act):
                act.wait_ge(small_done, 1)
                act.activation(sd[:, :], ve[:, :], ACT.Sqrt).then_inc(sd_done, 1)
                for c in range(NC):
                    for k in range(NK):
                        sl = slice(c * HALF, c * HALF + HALF)
                        act.wait_ge(xT_ready, (c + 1) * NT // NC)
                        act.activation(xn_hi[:, k, sl], xT[k][:, sl], ACT.Copy).then_inc(hi_done, 1)


def project0(nc, xn_hi, xn_lo, w_hi, w_lo, bias, rope_c, rope_s, ident, qT, kT, v3):
    QK = 2 * H0 * DH0
    with Scope(nc) as s:
        qkv = s.sb("p0_qkv", [P, 2, 3 * D], F32)
        t1 = s.sb("p0_t1", [P, QK], F32)
        t2 = s.sb("p0_t2", [P, QK], F32)
        rot = s.sb("p0_rot", [P, 2, QK], F32)
        zq = s.sb("p0_zq", [P, 2, H0, 4, DH0], F32R)
        zk = s.sb("p0_zk", [P, 2, H0, 4, DH0], F32R)
        vr = s.sb("p0_vr", [P, 2, D], F32)
        proj = [s.ps(f"p0_proj{i}", [P, 2 * HALF]) for i in range(2)]
        tp = [s.ps(f"p0_tp{i}", [P, HALF]) for i in range(4)]
        proj_ready, qkv_done, rope_step = s.sem("p0_proj_ready"), s.sem("p0_qkv_done"), s.sem("p0_rope_step")
        z_hi_done, z_lo_done = s.sem("p0_z_hi_done"), s.sem("p0_z_lo_done")
        tp_ready, tp_taken, v_step = s.sem("p0_tp_ready"), s.sem("p0_tp_taken"), s.sem("p0_v_step")

        def pairs(z):
            return z.rearrange("p h r d -> p (h r d)").rearrange("p (a c) -> p a c", c=P)

        with nc.Block() as block:

            @block.tensor
            def _(pe):
                for t in range(NT + 1):
                    if t < NT:
                        if t >= 2:
                            pe.wait_ge(qkv_done, t - 1)
                        tok = slice(t * P, t * P + P)
                        for a, b in ((0, HALF), (HALF, 3 * D)):
                            last = three_pass(pe, proj[t % 2][:, a:b],
                                              [(xn_hi[:, k, tok], xn_lo[:, k, tok],
                                                w_hi[:, k, a:b], w_lo[:, k, a:b]) for k in range(NK)])
                        last.then_inc(proj_ready, 1)
                    if t >= 1:
                        u = t - 1
                        pe.wait_ge(z_hi_done, 2 * u + 2)
                        pe.wait_ge(z_lo_done, 2 * u + 2)
                        if u >= 1:
                            pe.wait_ge(tp_taken, 4 * u)
                        for b in range(4):
                            z = pairs((zq if b < 2 else zk)[:, u % 2])
                            for j in range(4):
                                pe_in = f32(z[:, 4 * (b % 2) + j, :])
                                last = pe.transpose(tp[b][:, j * P:j * P + P], pe_in, ident[:, :])
                            last.then_inc(tp_ready, 1)

            @block.vector
            def _(dve):
                for t in range(NT):
                    dve.wait_ge(proj_ready, t + 1)
                    if t >= 2:
                        dve.wait_ge(v_step, 4 * (t - 1))
                        dve.wait_ge(z_hi_done, 2 * (t - 1))
                    dve.tensor_tensor(qkv[:, t % 2, :], proj[t % 2][:, 0:3 * D], bias[:, :],
                                      ALU.add).then_inc(qkv_done, 1)
                    dve.wait_ge(qkv_done, t + 1)
                    if t >= 1:
                        dve.wait_ge(rope_step, 4 * t)
                    x = qkv[:, t % 2, 0:QK].rearrange("p (a h d) -> p a h d", a=2, h=H0)
                    y1 = t1[:, :].rearrange("p (a h d) -> p a h d", a=2, h=H0)
                    y2 = t2[:, :].rearrange("p (a h d) -> p a h d", a=2, h=H0)

                    def table(tab, lo):
                        v = tab[:, t, :, lo::2] if lo is not None else tab[:, t, :, :]
                        n = DH0 // 2 if lo is not None else DH0
                        return v.unsqueeze(2).broadcast_to([P, 2, H0, n])
                    dve.tensor_tensor(y1, x, table(rope_c, None), ALU.mult).then_inc(rope_step, 1)
                    dve.tensor_tensor(y2[:, :, :, 0::2], x[:, :, :, 1::2], table(rope_s, 0),
                                      ALU.mult).then_inc(rope_step, 1)
                    dve.tensor_tensor(y2[:, :, :, 1::2], x[:, :, :, 0::2], table(rope_s, 1),
                                      ALU.mult).then_inc(rope_step, 1)
                    dve.wait_ge(rope_step, 4 * t + 3)
                    dve.tensor_tensor(rot[:, t % 2, :], t1[:, :], t2[:, :], ALU.add).then_inc(rope_step, 1)
                    for a, z in enumerate((zq, zk)):
                        r = rot[:, t % 2, a * D:a * D + D].rearrange("p (h d) -> p h d", h=H0)\
                            .unsqueeze(2).broadcast_to([P, H0, 2, DH0])
                        if a == 0:
                            hi, lo = z[:, t % 2, :, 0:2, :], z[:, t % 2, :, 2:4, :]
                        else:
                            hi, lo = z[:, t % 2, :, 0::2, :], z[:, t % 2, :, 1::2, :]
                        dve.wait_ge(z_hi_done, 2 * t + 1 + a)
                        dve.tensor_tensor(lo, r, f32(hi), ALU.subtract).then_inc(z_lo_done, 1)

            @block.gpsimd
            def _(pool):
                for t in range(NT):
                    pool.wait_ge(qkv_done, t + 1)
                    v = qkv[:, t % 2, QK:3 * D].rearrange("p (h d) -> p h d", h=H0)
                    parts = [v3[:, t, :, n, :] for n in range(PARTS0)]
                    r = [vr[:, n, :].rearrange("p (h d) -> p h d", h=H0) for n in range(2)]
                    pool.tensor_copy(parts[0], v).then_inc(v_step, 1)
                    pool.wait_ge(v_step, 4 * t + 1)
                    pool.tensor_tensor(r[0], v, parts[0], ALU.subtract).then_inc(v_step, 1)
                    pool.wait_ge(v_step, 4 * t + 2)
                    pool.tensor_copy(parts[1], r[0]).then_inc(v_step, 1)
                    pool.wait_ge(v_step, 4 * t + 3)
                    pool.tensor_tensor(parts[2], r[0], parts[1], ALU.subtract).then_inc(v_step, 1)

            @block.scalar
            def _(act):
                for t in range(NT + 1):
                    if t < NT:
                        act.wait_ge(rope_step, 4 * t + 4)
                        if t >= 2:
                            act.wait_ge(tp_ready, 4 * (t - 1))
                        for a, z in enumerate((zq, zk)):
                            r = rot[:, t % 2, a * D:a * D + D].rearrange("p (h d) -> p h d", h=H0)\
                                .unsqueeze(2).broadcast_to([P, H0, 2, DH0])
                            hi = z[:, t % 2, :, 0:2, :] if a == 0 else z[:, t % 2, :, 0::2, :]
                            act.activation(hi, r, ACT.Copy).then_inc(z_hi_done, 1)
                    if t >= 1:
                        u = t - 1
                        for b in range(4):
                            act.wait_ge(tp_ready, 4 * u + b + 1)
                            dst = (qT if b < 2 else kT)[:, 4 * (b % 2):4 * (b % 2) + 4, u * P:u * P + P]
                            act.activation(dst, tp[b][:, :].rearrange("p (a c) -> p a c", a=4),
                                           ACT.Copy).then_inc(tp_taken, 1)


def attention0(nc, qT, kT, v3, ident, ident_bf, mask, att):
    PER = 2 * NT * GH0
    tile_of = lambda u: u // GH0 % NT
    before = chunks_before(PER, tile_of)
    CH = before[-1]
    RING = 3
    with Scope(nc) as s:
        qs = [s.sb(f"a0_q{b}", [P, GH0, T], F32R) for b in range(2)]
        ks = [s.sb(f"a0_k{b}", [P, GH0 // 2, T], F32R) for b in range(2)]
        vs = [s.sb(f"a0_v{b}", [P, NT, GH0 * VW0], BF16) for b in range(2)]
        prob = s.sb("a0_prob", [P, RING, T], F32)
        p_hi = s.sb("a0_p_hi", [P, RING, NT, P], F16)
        p_lo = s.sb("a0_p_lo", [P, RING, NT, P], F16)
        neg_max = s.sb("a0_neg_max", [P, 8], F32)
        sums = s.sb("a0_sums", [P, 4, GH0], F32)
        rinv = s.sb("a0_rinv", [P, 2, GH0], F32)
        osum = s.sb("a0_osum", [P, 2, GH0 * DH0], F32)
        S = [s.ps(f"a0_S{b}", [P, 2 * HALF]) for b in range(2)]
        X = [s.ps(f"a0_X{b}", [P, HALF]) for b in range(2)]
        O = [s.ps(f"a0_O{b}", [P, HALF]) for b in range(2)]
        zeroed = s.sem("a0_zeroed")
        staged = [s.sem(f"a0_staged{b}") for b in range(2)]
        scores_ready, max_done, exp_done = s.sem("a0_scores_ready"), s.sem("a0_max_done"), s.sem("a0_exp_done")
        pT_ready, hi_done, lo_done = s.sem("a0_pT_ready"), s.sem("a0_hi_done"), s.sem("a0_lo_done")
        o_ready, o_taken, rinv_done, out_done = (s.sem("a0_o_ready"), s.sem("a0_o_taken"),
                                                 s.sem("a0_rinv_done"), s.sem("a0_out_done"))
        NSTAGE = 2 * (GH0 // 2) + 1 + 1

        with nc.Block() as block:

            @block.sync
            def _(sp):
                sp.wait_ge(zeroed, 4)
                for n in range(GROUPS0):
                    b = n % 2
                    if n >= 2:
                        sp.wait_ge(scores_ready, (n - 1) * PER // 2)
                        sp.wait_ge(o_ready, (n - 1) * PER // 2)
                    for a in range(GH0 // 2):
                        pair = n * (GH0 // 2) + a
                        for e in range(2):
                            rows = slice(64 * e, 64 * e + 64)
                            sp.dma_start(f32(qs[b][rows, 2 * a + e, :]), f32(qT[rows, pair, :]))\
                              .then_inc(staged[b], 16)
                    sp.dma_start(f32(ks[b][:, :, :]), f32(kT[:, n * 2:n * 2 + 2, :])).then_inc(staged[b], 16)
                    sp.dma_start(vs[b][:, :, :],
                                 v3[:, :, n * GH0:n * GH0 + GH0].rearrange("p t h r d -> p t (h r d)"))\
                      .then_inc(staged[b], 16)
                for b in range(2):
                    sp.wait_ge(staged[b], 2 * NSTAGE * 16)

            @block.gpsimd
            def _(pool):
                for b in range(2):
                    for e in range(2):
                        rows = slice(64 - 64 * e, 128 - 64 * e)
                        pool.memset(f32(qs[b][rows, e::2, :]), 0.0).then_inc(zeroed, 1)

            @block.tensor
            def _(pe):
                with pe.Fori(0, 2, 1) as g:
                    for step in range(PER + 5):
                        if step < PER:
                            u = step
                            i, h, b = tile_of(u), u % GH0, u // (PER // 2)
                            n = (i + 1) * P
                            if u % (PER // 2) == 0:
                                pe.wait_ge(staged[b], g * (NSTAGE * 16) + NSTAGE * 16)
                            if u >= 2:
                                pe.wait_ge(exp_done, g * PER + (u - 1))
                            for a in range(0, n, HALF):
                                e = min(a + HALF, n)
                                diag = e == n
                                pe.matmul(S[u % 2][:, a:e], qs[b][:, h, i * P:i * P + P],
                                          ks[b][:, h // 2, a:e], start=True, stop=not diag)
                            pe.matmul(S[u % 2][:, n - P:n], ident_bf[:, :], mask[:, :],
                                      start=False, stop=True).then_inc(scores_ready, 1)
                        if 3 <= step < PER + 3:
                            u = step - 3
                            i = tile_of(u)
                            pe.wait_ge(exp_done, g * PER + (u + 1))
                            for c in range(chunks_of(i)):
                                m = before[u] + c
                                if m >= 2:
                                    pe.wait_ge(lo_done, g * CH + (m - 1))
                                js = range(4 * c, min(4 * c + 4, i + 1))
                                for j in js:
                                    last = pe.transpose(X[m % 2][:, (j % 4) * P:(j % 4) * P + P],
                                                        prob[:, u % RING, j * P:j * P + P], ident[:, :])
                                last.then_inc(pT_ready, 1)
                        if step >= 5:
                            u = step - 5
                            i, h, b = tile_of(u), u % GH0, u // (PER // 2)
                            r = u // GH0
                            pe.wait_ge(lo_done, g * CH + before[u + 1])
                            if h == 0 and r >= 2:
                                pe.wait_ge(o_taken, g * (PER // GH0) + (r - 1))
                            n, count = 0, 2 * (i + 1)
                            for j in range(i + 1):
                                for half in (p_hi, p_lo):
                                    last = pe.matmul(O[r % 2][:, h * VW0:h * VW0 + VW0],
                                                     half[:, u % RING, j, :],
                                                     vs[b][:, j, h * VW0:h * VW0 + VW0],
                                                     start=n == 0, stop=n == count - 1)
                                    n += 1
                            last.then_inc(o_ready, 1)

            @block.scalar
            def _(act):
                with act.Fori(0, 2, 1) as g:
                    for step in range(PER + 3):
                        if 1 <= step < PER + 1:
                            u = step - 1
                            i = tile_of(u)
                            n = (i + 1) * P
                            act.wait_ge(max_done, g * PER + (u + 1))
                            if u >= RING:
                                act.wait_ge(pT_ready, g * CH + before[u - RING + 1])
                            act.activation(prob[:, u % RING, 0:n], S[u % 2][:, 0:n], ACT.Exp,
                                           bias=neg_max[:, u % 8:u % 8 + 1],
                                           accum_out=sums[:, u // GH0 % 4, u % GH0:u % GH0 + 1])\
                               .then_inc(exp_done, 1)
                        if step >= 3:
                            u = step - 3
                            i = tile_of(u)
                            if u >= RING:
                                act.wait_ge(o_ready, g * PER + (u - RING + 1))
                            for c in range(chunks_of(i)):
                                m = before[u] + c
                                js = slice(4 * c, min(4 * c + 4, i + 1))
                                n = (js.stop - js.start) * P
                                act.wait_ge(pT_ready, g * CH + (m + 1))
                                act.activation(p_hi[:, u % RING, js, :].rearrange("p a c -> p (a c)"),
                                               X[m % 2][:, 0:n], ACT.Copy).then_inc(hi_done, 1)

            @block.vector
            def _(dve):
                with dve.Fori(0, 2, 1) as g:
                    for step in range(PER + 9):
                        if step < PER:
                            u = step
                            n = (tile_of(u) + 1) * P
                            dve.wait_ge(scores_ready, g * PER + (u + 1))
                            dve.tensor_reduce(neg_max[:, u % 8:u % 8 + 1], S[u % 2][:, 0:n], AX.X,
                                              ALU.max, negate=True).then_inc(max_done, 1)
                        if 3 <= step < PER + 3:
                            u = step - 3
                            i = tile_of(u)
                            for c in range(chunks_of(i)):
                                m = before[u] + c
                                js = slice(4 * c, min(4 * c + 4, i + 1))
                                n = (js.stop - js.start) * P
                                dve.wait_ge(hi_done, g * CH + (m + 1))
                                dve.tensor_tensor(p_lo[:, u % RING, js, :].rearrange("p a c -> p (a c)"),
                                                  X[m % 2][:, 0:n],
                                                  p_hi[:, u % RING, js, :].rearrange("p a c -> p (a c)"),
                                                  ALU.subtract).then_inc(lo_done, 1)
                        if step >= 9 and step % GH0 == 1:
                            r = step // GH0 - 2
                            i, b = r % NT, r // NT
                            done = PER // GH0
                            dve.wait_ge(o_ready, g * PER + (r + 1) * GH0)
                            dve.reciprocal(rinv[:, r % 2, :], sums[:, r % 4, :]).then_inc(rinv_done, 1)
                            dve.tensor_reduce(
                                osum[:, r % 2, :].rearrange("p (h d) -> p h d", h=GH0),
                                O[r % 2][:, 0:GH0 * VW0].rearrange("p (h r d) -> p h d r", h=GH0, r=PARTS0),
                                AX.X, ALU.add).then_inc(o_taken, 1)
                            dve.wait_ge(rinv_done, g * done + (r + 1))
                            dve.wait_ge(o_taken, g * done + (r + 1))
                            dve.tensor_tensor(
                                att[:, i, bass.ds(g * (2 * GH0 * DH0) + b * GH0 * DH0, GH0 * DH0)]
                                .rearrange("p (h d) -> p h d", h=GH0),
                                osum[:, r % 2, :].rearrange("p (h d) -> p h d", h=GH0),
                                rinv[:, r % 2, :].unsqueeze(2).broadcast_to([P, GH0, DH0]),
                                ALU.mult).then_inc(out_done, 1)


def project_out0(nc, att, wo_hi, wo_lo, bo, ident, sT):
    with Scope(nc) as s:
        a_hi = s.sb("o0_a_hi", [P, NK, T], F32R)
        a_lo = s.sb("o0_a_lo", [P, NK, T], F32R)
        aT = [s.ps(f"o0_aT{k}", [P, T]) for k in range(NK)]
        acc = [s.ps(f"o0_acc{c}", [P, 2 * HALF]) for c in range(NC)]
        aT_ready, hi_done, lo_done, y_ready, y_done = (
            s.sem("o0_aT_ready"), s.sem("o0_hi_done"), s.sem("o0_lo_done"), s.sem("o0_y_ready"), s.sem("o0_y_done"))
        with nc.Block() as block:

            @block.tensor
            def _(pe):
                for c in range(NC):
                    for k in range(NK):
                        for t in range(4 * c, 4 * c + 4):
                            last = pe.transpose(aT[k][:, t * P:t * P + P], att[:, t, k * P:k * P + P],
                                                ident[:, :])
                        last.then_inc(aT_ready, 1)
                for c in range(NC):
                    pe.wait_ge(lo_done, NK * (c + 1))
                    sl = slice(c * HALF, c * HALF + HALF)
                    for m in range(NK):
                        three_pass(pe, acc[c][:, m * HALF:m * HALF + HALF],
                                   [(wo_hi[:, k, m * P:m * P + P], wo_lo[:, k, m * P:m * P + P],
                                     a_hi[:, k, sl], a_lo[:, k, sl]) for k in range(NK)])\
                            .then_inc(y_ready, 1)

            @block.scalar
            def _(act):
                n = 0
                for c in range(NC):
                    for k in range(NK):
                        n += 1
                        sl = slice(c * HALF, c * HALF + HALF)
                        act.wait_ge(aT_ready, n)
                        act.activation(a_hi[:, k, sl], aT[k][:, sl], ACT.Copy).then_inc(hi_done, 1)

            @block.vector
            def _(dve):
                n = 0
                for c in range(NC):
                    for k in range(NK):
                        n += 1
                        sl = slice(c * HALF, c * HALF + HALF)
                        dve.wait_ge(hi_done, n)
                        dve.tensor_tensor(a_lo[:, k, sl], aT[k][:, sl], f32(a_hi[:, k, sl]),
                                          ALU.subtract).then_inc(lo_done, 1)
                n = 0
                for c in range(NC):
                    for m in range(NK):
                        n += 1
                        dve.wait_ge(y_ready, n)
                        dve.tensor_scalar(sT[:, m, c * HALF:c * HALF + HALF],
                                          acc[c][:, m * HALF:m * HALF + HALF],
                                          bo[:, m:m + 1], None, ALU.add).then_inc(y_done, 1)


def gated_ffn(nc, tag, tiles, weights, cols, offset, scales, down_scale, xn_hi, xn_lo, gate_hi, gT):
    routed = gate_hi is not None
    with Scope(nc) as s:
        raw = [s.sb(f"{tag}_raw{b}", [P, cols], weights.dtype) for b in range(2)]
        w_hi = [s.sb(f"{tag}_w_hi{b}", [P, cols], F32R) for b in range(2)]
        w_lo = [s.sb(f"{tag}_w_lo{b}", [P, WCOLS], F32R) for b in range(2)]
        sc = [s.sb(f"{tag}_sc{b}", [P, 2], F32) for b in range(2)]
        sg = s.sb(f"{tag}_sg", [P, NC, HALF], F32)
        h1 = s.sb(f"{tag}_h1", [P, NC, HALF], F32)
        hh = s.sb(f"{tag}_hh", [P, NC, HALF], F32)
        h_hi = [s.sb(f"{tag}_h_hi{b}", [P, T], F32R) for b in range(2)]
        h_lo = [s.sb(f"{tag}_h_lo{b}", [P, T], F32R) for b in range(2)]
        G = [s.ps(f"{tag}_G{c}", [P, HALF]) for c in range(NC)]
        U = [s.ps(f"{tag}_U{c}", [P, HALF]) for c in range(NC)]
        acc = [s.ps(f"{tag}_acc{c}", [P, HALF]) for c in range(NK * NC)]
        two = lambda name: [s.sem(f"{tag}_{name}{b}") for b in range(2)]
        counts = lambda name, per: [Count(x, per) for x in two(name)]
        loaded, w_hi_done, w_lo_done = two("loaded"), two("w_hi_done"), counts("w_lo_done", 1)
        gate_ready, up_ready, silu_done = two("gate_ready"), two("up_ready"), two("silu_done")
        mix_ready, h1_done, h_done = two("mix_ready"), two("h1_done"), counts("h_done", NC)
        h_hi_done, h_lo_done = counts("h_hi_done", NC), counts("h_lo_done", NC)
        down_done = counts("down_done", 1)
        zeroed, opened, all_down, g_done = (s.sem(f"{tag}_zeroed"), s.sem(f"{tag}_opened"),
                                            s.sem(f"{tag}_all_down"), s.sem(f"{tag}_g_done"))
        NL = 2 if scales is not None else 1
        passes = tiles // 2

        def w(half, part, k):
            at = (part * NK + k) * P
            return half[:, at:at + P]

        def down(pe, b, stop):
            for c in range(NC):
                for m in range(NK):
                    sl = slice(c * HALF, c * HALF + HALF)
                    last = three_pass(pe, acc[m * NC + c][:, :],
                                      [(w(wd_hi[b], 0, m), w(wd_lo[b], 0, m), h_hi[b][:, sl], h_lo[b][:, sl])],
                                      start=False, stop=stop, check=False)
            return last

        wd_hi = [t[:, 2 * NK * P:WCOLS] for t in w_hi]
        wd_lo = [t[:, 2 * NK * P:WCOLS] for t in w_lo]

        with nc.Block() as block:

            @block.sync
            def _(sp):
                with sp.Fori(0, passes, 1) as g:
                    for b in range(2):
                        sp.wait_ge(w_lo_done[b].sem, w_lo_done[b].at(g, 0))
                        sp.dma_start(raw[b][:, :], weights[g * 2 + b, :, :]).then_inc(loaded[b], 16)
                        if scales is not None:
                            sp.wait_ge(h_done[b].sem, h_done[b].at(g, 0))
                            sp.dma_start(sc[b][:, :], scales[g * 2 + b, :, :]).then_inc(loaded[b], 16)

            @block.gpsimd
            def _(pool):
                pool.memset(f32(h_hi[1][:, :]), 0.0).then_inc(zeroed, 1)
                pool.memset(f32(h_lo[1][:, :]), 0.0).then_inc(zeroed, 1)
                pool.memset(f32(w_hi[1][:, :]), 0.0).then_inc(zeroed, 1)
                pool.memset(f32(w_lo[1][:, :]), 0.0).then_inc(zeroed, 1)

            @block.tensor
            def _(pe):
                pe.wait_ge(zeroed, 4)
                for b in range(2):
                    down_done[b].prime(pe)
                for a in acc:
                    last = pe.matmul(a[:, :], wd_hi[1][:, 0:P], h_hi[1][:, 0:HALF], start=True,
                                     stop=False, skip_group_check=True)
                last.then_inc(opened, 1)
                with pe.Fori(0, passes, 1) as g:
                    for b in range(2):
                        pe.wait_ge(w_hi_done[b], g + 1)
                        pe.wait_ge(w_lo_done[b].sem, w_lo_done[b].at(g, 1))
                        for c in range(NC):
                            sl = slice(c * HALF, c * HALF + HALF)
                            pe.wait_ge(h_done[1 - b].sem, h_done[1 - b].at(g, c + 1 if b else 0))
                            x = [(xn_hi[:, k, sl], xn_lo[:, k, sl]) for k in range(NK)]
                            three_pass(pe, G[c][:, :], [(w(w_hi[b], 0, k), w(w_lo[b], 0, k), *x[k])
                                                        for k in range(NK)]).then_inc(gate_ready[b], 1)
                            three_pass(pe, U[c][:, :], [(w(w_hi[b], 1, k), w(w_lo[b], 1, k), *x[k])
                                                        for k in range(NK)]).then_inc(up_ready[b], 1)
                        if routed:
                            for c in range(NC):
                                pe.wait_ge(silu_done[b], g * NC + (c + 1))
                                pe.matmul(G[c][:, :], w_hi[b][:, WCOLS:WCOLS + P],
                                          gate_hi[:, c * HALF:c * HALF + HALF],
                                          start=True, stop=True).then_inc(mix_ready[b], 1)
                        pe.wait_ge(h_lo_done[1 - b].sem, h_lo_done[1 - b].at(g, NC if b else 0))
                        down(pe, 1 - b, False).then_inc(down_done[1 - b].sem, 1)
                pe.wait_ge(h_lo_done[1].sem, h_lo_done[1].at(passes - 1, NC))
                down(pe, 1, True).then_inc(all_down, 1)

            @block.scalar
            def _(act):
                act.wait_ge(opened, 1)
                for b in range(2):
                    h_hi_done[b].prime(act)
                with act.Fori(0, passes, 1) as g:
                    for b in range(2):
                        act.wait_ge(loaded[b], g * (16 * NL) + 16 * NL)
                        act.wait_ge(down_done[b].sem, down_done[b].at(g, b))
                        act.activation(w_hi[b][:, :], raw[b][:, :], ACT.Copy, bias=offset)\
                           .then_inc(w_hi_done[b], 1)
                        for c in range(NC):
                            act.wait_ge(gate_ready[b], g * NC + (c + 1))
                            act.wait_ge(h_done[1 - b].sem, h_done[1 - b].at(g, c + 1 if b else 0))
                            act.activation(sg[:, c, :], G[c][:, :], ACT.Silu,
                                           **({"scale": sc[b][:, 0:1]} if scales is not None else {}))\
                               .then_inc(silu_done[b], 1)
                        for c in range(NC):
                            act.wait_ge(h_done[b].sem, h_done[b].at(g, c + 1))
                            act.activation(h_hi[b][:, c * HALF:c * HALF + HALF], hh[:, c, :], ACT.Copy)\
                               .then_inc(h_hi_done[b].sem, 1)
                act.wait_ge(all_down, 1)
                for m in range(NK):
                    for c in range(NC):
                        act.activation(gT[:, m, c * HALF:c * HALF + HALF], acc[m * NC + c][:, :], ACT.Silu,
                                       **({"scale": down_scale[:, m:m + 1]} if down_scale is not None else {}))\
                           .then_inc(g_done, 1)

            @block.vector
            def _(dve):
                for b in range(2):
                    for count in (w_lo_done[b], h_done[b], h_lo_done[b]):
                        count.prime(dve)
                with dve.Fori(0, passes, 1) as g:
                    for b in range(2):
                        dve.wait_ge(w_hi_done[b], g + 1)
                        dve.scalar_tensor_tensor(w_lo[b][:, :], raw[b][:, 0:WCOLS], offset,
                                                 f32(w_hi[b][:, 0:WCOLS]), ALU.add, ALU.subtract)\
                           .then_inc(w_lo_done[b].sem, 1)
                        for c in range(NC):
                            dve.wait_ge(silu_done[b], g * NC + (c + 1))
                            dve.wait_ge(up_ready[b], g * NC + (c + 1))
                            dve.wait_ge(h_hi_done[1 - b].sem, h_hi_done[1 - b].at(g, c + 1 if b else 0))
                            dve.wait_ge(h_lo_done[1 - b].sem, h_lo_done[1 - b].at(g, c + 1 if b else 0))
                            if routed:
                                dve.tensor_tensor(h1[:, c, :], U[c][:, :], sg[:, c, :], ALU.mult)\
                                   .then_inc(h1_done[b], 1)
                                dve.wait_ge(h1_done[b], g * NC + (c + 1))
                                dve.wait_ge(mix_ready[b], g * NC + (c + 1))
                                dve.tensor_tensor(hh[:, c, :], G[c][:, :], h1[:, c, :], ALU.mult)\
                                   .then_inc(h_done[b].sem, 1)
                            else:
                                dve.scalar_tensor_tensor(hh[:, c, :], U[c][:, :], sc[b][:, 1:2], sg[:, c, :],
                                                         ALU.mult, ALU.mult).then_inc(h_done[b].sem, 1)
                        for c in range(NC):
                            sl = slice(c * HALF, c * HALF + HALF)
                            dve.wait_ge(h_hi_done[b].sem, h_hi_done[b].at(g, c + 1))
                            dve.tensor_tensor(h_lo[b][:, sl], hh[:, c, :], f32(h_hi[b][:, sl]),
                                              ALU.subtract).then_inc(h_lo_done[b].sem, 1)


def combine0(nc, xT, sT, gT, ident, x_tok):
    with Scope(nc) as s:
        prod = s.sb("c0_prod", [P, NK, T], F32)
        tp = [s.ps(f"c0_tp{b}", [P, HALF]) for b in range(4)]
        prod_done, x_done, tp_ready, taken = (s.sem("c0_prod_done"), s.sem("c0_x_done"),
                                              s.sem("c0_tp_ready"), s.sem("c0_taken"))
        with nc.Block() as block:

            @block.vector
            def _(dve):
                for c in range(NC):
                    sl = slice(c * HALF, c * HALF + HALF)
                    dve.tensor_tensor(prod[:, :, sl], sT[:, :, sl], gT[:, :, sl], ALU.mult)\
                       .then_inc(prod_done, 1)
                    dve.wait_ge(prod_done, c + 1)
                    dve.tensor_tensor(xT[:, :, sl], xT[:, :, sl], prod[:, :, sl], ALU.add)\
                       .then_inc(x_done, 1)

            @block.tensor
            def _(pe):
                for n in range(NT // 2):
                    pe.wait_ge(x_done, n // 2 + 1)
                    for j in range(2):
                        for k in range(NK):
                            t = 2 * n + j
                            last = pe.transpose(tp[n][:, (j * NK + k) * P:(j * NK + k) * P + P],
                                                xT[:, k, t * P:t * P + P], ident[:, :])
                    last.then_inc(tp_ready, 1)

            @block.scalar
            def _(act):
                for n in range(NT // 2):
                    act.wait_ge(tp_ready, n + 1)
                    act.activation(x_tok[:, 2 * n:2 * n + 2, :],
                                   tp[n][:, :].rearrange("p (t d) -> p t d", t=2),
                                   ACT.Copy).then_inc(taken, 1)


def route1(nc, xn_hi, xn_lo, wr, earlier, ident, gate_hi):
    E = 16
    with Scope(nc) as s:
        wr_hi = s.sb("r1_wr_hi", [P, NK, E1], F32R)
        wr_lo = s.sb("r1_wr_lo", [P, NK, E1], F32R)
        lg = s.sb("r1_lg", [E1, T], F32)
        sm = s.sb("r1_sm", [P, NT], F32)
        e = s.sb("r1_e", [P, 3, NT, E1], F32)
        cmp = s.sb("r1_cmp", [P, 3, NT, E1 * E1], F32)
        rank = s.sb("r1_rank", [P, 2, NT * E1], F32)
        wt = s.sb("r1_wt", [P, NT, E], F32)
        L = [s.ps(f"r1_L{c}", [P, HALF]) for c in range(NC)]
        LT = s.ps("r1_LT", [P, HALF])
        WT = [s.ps(f"r1_WT{c}", [P, HALF]) for c in range(NC)]
        wr_hi_done, step, act_step = s.sem("r1_wr_hi_done"), s.sem("r1_step"), s.sem("r1_act_step")
        logits_ready, lt_ready, wt_ready = s.sem("r1_logits_ready"), s.sem("r1_lt_ready"), s.sem("r1_wt_ready")
        zeroed, g_hi_done = s.sem("r1_zeroed"), s.sem("r1_g_hi_done")
        with nc.Block() as block:

            @block.gpsimd
            def _(pool):
                pool.memset(f32(gate_hi[:, :]), 0.0).then_inc(zeroed, 1)
                pool.memset(wt[:, :, E1:E1 + 1], 1.0).then_inc(zeroed, 1)
                pool.memset(wt[:, :, E1 + 1:E], 0.0).then_inc(zeroed, 1)

            @block.scalar
            def _(act):
                act.activation(wr_hi[:, :, :], wr[:, :, :], ACT.Copy).then_inc(wr_hi_done, 1)
                for c in range(NC):
                    act.wait_ge(logits_ready, c + 1)
                    act.activation(lg[:, c * HALF:c * HALF + HALF], L[c][0:E1, :], ACT.Copy)\
                       .then_inc(act_step, 1)
                act.wait_ge(step, 3)
                act.activation(e[:, 1, :, :], e[:, 0, :, :], ACT.Exp).then_inc(act_step, 1)
                act.wait_ge(zeroed, 3)
                for c in range(NC):
                    act.wait_ge(wt_ready, c + 1)
                    act.activation(gate_hi[0:E, c * HALF:c * HALF + HALF], WT[c][0:E, :], ACT.Copy)\
                       .then_inc(g_hi_done, 1)

            @block.tensor
            def _(pe):
                pe.wait_ge(step, 1)
                for c in range(NC):
                    sl = slice(c * HALF, c * HALF + HALF)
                    three_pass(pe, L[c][0:E1, :], [(wr_hi[:, k, :], wr_lo[:, k, :], xn_hi[:, k, sl],
                                                    xn_lo[:, k, sl]) for k in range(NK)])\
                        .then_inc(logits_ready, 1)
                for t in range(NT):
                    pe.wait_ge(act_step, t // 4 + 1)
                    last = pe.transpose(LT[:, t * E1:t * E1 + E1], lg[0:E1, t * P:t * P + P],
                                        ident[0:E1, 0:E1])
                last.then_inc(lt_ready, 1)
                pe.wait_ge(step, 13)
                pe.wait_ge(zeroed, 3)
                for c in range(NC):
                    for j in range(4):
                        last = pe.transpose(WT[c][0:E, j * P:j * P + P], wt[:, 4 * c + j, :], ident[:, :])
                    last.then_inc(wt_ready, 1)

            @block.vector
            def _(dve):
                def done(n):
                    dve.wait_ge(step, n)

                dve.wait_ge(wr_hi_done, 1)
                dve.tensor_tensor(wr_lo[:, :, :], wr[:, :, :], f32(wr_hi[:, :, :]), ALU.subtract)\
                   .then_inc(step, 1)
                dve.wait_ge(lt_ready, 1)
                lt = LT[:, 0:NT * E1].rearrange("p (t e) -> p t e", t=NT)
                wide = lambda v: v.unsqueeze(2).broadcast_to([P, NT, E1])
                dve.tensor_reduce(sm[:, :], lt, AX.X, ALU.max).then_inc(step, 1)
                done(2)
                dve.tensor_tensor(e[:, 0, :, :], lt, wide(sm[:, :]), ALU.subtract).then_inc(step, 1)
                dve.wait_ge(act_step, NC + 1)
                done(3)
                dve.tensor_reduce(sm[:, :], e[:, 1, :, :], AX.X, ALU.add).then_inc(step, 1)
                done(4)
                dve.reciprocal(rank[:, 0, 0:NT], sm[:, :]).then_inc(step, 1)
                done(5)
                dve.tensor_tensor(e[:, 2, :, :], e[:, 1, :, :], wide(rank[:, 0, 0:NT]), ALU.mult)\
                   .then_inc(step, 1)
                done(6)
                this = e[:, 2, :, :].unsqueeze(3).broadcast_to([P, NT, E1, E1])
                other = e[:, 2, :, :].unsqueeze(2).broadcast_to([P, NT, E1, E1])
                c4 = lambda n: cmp[:, n, :, :].rearrange("p t (a b) -> p t a b", a=E1)
                dve.tensor_tensor(c4(0), other, this, ALU.is_gt).then_inc(step, 1)
                dve.tensor_tensor(c4(1), other, this, ALU.is_equal).then_inc(step, 1)
                done(8)
                dve.tensor_tensor(cmp[:, 2, :, :], cmp[:, 1, :, :],
                                  earlier[:, :].unsqueeze(1).broadcast_to([P, NT, E1 * E1]), ALU.mult)\
                   .then_inc(step, 1)
                done(9)
                dve.tensor_tensor(cmp[:, 1, :, :], cmp[:, 0, :, :], cmp[:, 2, :, :], ALU.add)\
                   .then_inc(step, 1)
                done(10)
                dve.tensor_reduce(rank[:, 0, :].rearrange("p (t e) -> p t e", t=NT), c4(1), AX.X, ALU.add)\
                   .then_inc(step, 1)
                done(11)
                dve.tensor_scalar(rank[:, 1, :], rank[:, 0, :], float(TOPK) - 0.5, None, ALU.is_lt)\
                   .then_inc(step, 1)
                done(12)
                dve.tensor_tensor(wt[:, :, 0:E1], e[:, 2, :, :],
                                  rank[:, 1, :].rearrange("p (t e) -> p t e", t=NT), ALU.mult)\
                   .then_inc(step, 1)
                for c in range(NC):
                    sl = slice(c * HALF, c * HALF + HALF)
                    dve.wait_ge(g_hi_done, c + 1)
                    dve.tensor_tensor(gate_hi[32:32 + E, sl], WT[c][0:E, :], f32(gate_hi[0:E, sl]),
                                      ALU.subtract).then_inc(step, 1)


def attention1(nc, xn_hi, xn_lo, w_qkv, w_out, rope_c, rope_s, ident, ident_bf, mask, acc):
    PER = NT * GH1
    PAIRS = PER // 2
    tile_of = lambda u: u // GH1
    before = chunks_before(PER, tile_of)
    CH = before[-1]
    NP = (GH1 + 2) * NC
    QC = (GH1 + 1) * NC
    RP, RX = 3, 2
    with Scope(nc) as s:
        raw = s.sb("a1_raw", [P, GWCOLS1], F32)
        zero = s.sb("a1_zero", [P, 1], F32)
        w_hi = s.sb("a1_w_hi", [P, NK, (GH1 + 2) * P], F32R)
        w_lo = s.sb("a1_w_lo", [P, NK, (GH1 + 2) * P], F32R)
        wo_hi = s.sb("a1_wo_hi", [P, GH1, D], F32R)
        wo_lo = s.sb("a1_wo_lo", [P, GH1, D], F32R)
        q_hi = s.sb("a1_q_hi", [P, GH1 + 1, T], F32R)
        q_lo = s.sb("a1_q_lo", [P, GH1 + 1, T], F32R)
        vT = s.sb("a1_vT", [P, T], F32)
        v_hi = s.sb("a1_v_hi", [P, T], F32R)
        v_lo = s.sb("a1_v_lo", [P, T], F32R)
        swapped = s.sb("a1_swapped", [P, 2, HALF], F32)
        t1 = s.sb("a1_t1", [P, 2, HALF], F32)
        t2 = s.sb("a1_t2", [P, 2, HALF], F32)
        rot = s.sb("a1_rot", [P, 2, HALF], F32)
        prob = s.sb("a1_prob", [P, RP, T], F32)
        p_hi = s.sb("a1_p_hi", [P, RX, NT, 2, P], F32R)
        p_lo = s.sb("a1_p_lo", [P, RX, NT, 2, P], F32R)
        o_hi = s.sb("a1_o_hi", [P, GH1, HALF], F32R)
        o_lo = s.sb("a1_o_lo", [P, GH1, HALF], F32R)
        neg_max = s.sb("a1_neg_max", [P, 8], F32)
        sums = s.sb("a1_sums", [P, 8], F32)
        rinv = s.sb("a1_rinv", [P, 8], F32)
        S = [s.ps(f"a1_S{b}", [P, 2 * HALF]) for b in range(2)]
        X = [s.ps(f"a1_X{b}", [P, HALF]) for b in range(2)]
        O = [s.ps(f"a1_O{b}", [P, HALF]) for b in range(2)]
        proj = [S[n // 2][:, (n % 2) * HALF:(n % 2) * HALF + HALF] for n in range(4)]

        loaded, w_step = s.sem("a1_loaded"), Count(s.sem("a1_w_step"), 4)
        proj_ready, swap_done, rope_step = (Count(s.sem("a1_proj_ready"), NP), s.sem("a1_swap_done"),
                                            s.sem("a1_rope_step"))
        q_hi_done, q_lo_done = s.sem("a1_q_hi_done"), s.sem("a1_q_lo_done")
        vT_done, v_ready, v_hi_done, v_lo_done = (s.sem("a1_vT_done"), s.sem("a1_v_ready"),
                                                  s.sem("a1_v_hi_done"), s.sem("a1_v_lo_done"))
        scores_ready, max_done, exp_done = s.sem("a1_scores_ready"), s.sem("a1_max_done"), s.sem("a1_exp_done")
        rinv_done, norm_done = s.sem("a1_rinv_done"), s.sem("a1_norm_done")
        pT_ready, hi_done, lo_done = s.sem("a1_pT_ready"), s.sem("a1_hi_done"), s.sem("a1_lo_done")
        o_ready, o_hi_done, o_lo_done = s.sem("a1_o_ready"), s.sem("a1_o_hi_done"), s.sem("a1_o_lo_done")
        y_ready, y_done = Count(s.sem("a1_y_ready"), NC * NK), Count(s.sem("a1_y_done"), NC * NK)
        zeroed = s.sem("a1_zeroed")

        with nc.Block() as block:

            @block.sync
            def _(sp):
                with sp.Fori(0, KV1, 1) as g:
                    sp.wait_ge(w_step.sem, w_step.at(g, 0))
                    sp.dma_start(raw[:, :], w_qkv[g, :, :]).then_inc(loaded, 16)
                    sp.wait_ge(w_step.sem, w_step.at(g, 2))
                    sp.dma_start(raw[:, 0:GH1 * D], w_out[g, :, :]).then_inc(loaded, 16)

            @block.gpsimd
            def _(pool):
                pool.memset(acc[:, :, :], 0.0).then_inc(zeroed, 1)
                pool.memset(zero[:, :], 0.0).then_inc(zeroed, 1)
                pool.wait_ge(zeroed, 2)
                w_step.prime(pool)
                flat = lambda v: v.rearrange("p a b -> p (a b)")
                with pool.Fori(0, KV1, 1) as g:
                    pool.wait_ge(loaded, g * 32 + 16)
                    pool.wait_ge(proj_ready.sem, proj_ready.at(g, 0))
                    pool.tensor_tensor(flat(w_hi[:, :, :]), raw[:, :], zero[:, :].broadcast_to([P, GWCOLS1]), ALU.add).then_inc(w_step.sem, 1)
                    pool.wait_ge(w_step.sem, w_step.at(g, 1))
                    pool.tensor_tensor(flat(w_lo[:, :, :]), raw[:, :], f32(flat(w_hi[:, :, :])),
                                       ALU.subtract).then_inc(w_step.sem, 1)
                    pool.wait_ge(loaded, g * 32 + 32)
                    pool.wait_ge(y_ready.sem, y_ready.at(g, 0))
                    pool.tensor_tensor(flat(wo_hi[:, :, :]), raw[:, 0:GH1 * D], zero[:, :].broadcast_to([P, GH1 * D]), ALU.add).then_inc(w_step.sem, 1)
                    pool.wait_ge(w_step.sem, w_step.at(g, 3))
                    pool.tensor_tensor(flat(wo_lo[:, :, :]), raw[:, 0:GH1 * D], f32(flat(wo_hi[:, :, :])),
                                       ALU.subtract).then_inc(w_step.sem, 1)

            @block.tensor
            def _(pe):
                proj_ready.prime(pe)
                y_ready.prime(pe)
                with pe.Fori(0, KV1, 1) as g:
                    pe.wait_ge(w_step.sem, w_step.at(g, 2))
                    for n in range(NP):
                        m, c = n // NC, n % NC
                        sl = slice(c * HALF, c * HALF + HALF)
                        if n >= 4:
                            pe.wait_ge(rope_step, g * 3 * QC + 3 * (n - 4) + 1)
                        last = three_pass(pe, proj[n % 4],
                                          [(w_hi[:, k, m * P:m * P + P], w_lo[:, k, m * P:m * P + P],
                                            xn_hi[:, k, sl], xn_lo[:, k, sl]) for k in range(NK)])
                        last.then_inc(proj_ready.sem, 1)
                    for c in range(NC):
                        pe.wait_ge(vT_done, g * NC + (c + 1))
                        for j in range(4):
                            t = 4 * c + j
                            last = pe.transpose(X[c][:, j * P:j * P + P], vT[:, t * P:t * P + P],
                                                ident[:, :])
                        last.then_inc(v_ready, 1)
                    pe.wait_ge(q_lo_done, g * QC + QC)
                    pe.wait_ge(v_lo_done, g * NC + NC)
                    for step in range(PER + 6):
                        if step < PER:
                            u = step
                            i, h = tile_of(u), u % GH1
                            n, rows = (i + 1) * P, slice(i * P, i * P + P)
                            if u >= 2:
                                pe.wait_ge(exp_done, g * PER + (u - 1))
                            for a in range(0, n, HALF):
                                e = min(a + HALF, n)
                                three_pass(pe, S[u % 2][:, a:e],
                                           [(q_hi[:, h, rows], q_lo[:, h, rows],
                                             q_hi[:, GH1, a:e], q_lo[:, GH1, a:e])], stop=e != n)
                            pe.matmul(S[u % 2][:, n - P:n], ident_bf[:, :], mask[:, :], start=False,
                                      stop=True).then_inc(scores_ready, 1)
                        if 3 <= step < PER + 3:
                            u = step - 3
                            i = tile_of(u)
                            pe.wait_ge(norm_done, g * PER + (u + 1))
                            for c in range(chunks_of(i)):
                                m = before[u] + c
                                if m >= 2:
                                    pe.wait_ge(lo_done, g * CH + (m - 1))
                                for j in range(4 * c, min(4 * c + 4, i + 1)):
                                    last = pe.transpose(X[m % 2][:, (j % 4) * P:(j % 4) * P + P],
                                                        prob[:, u % RP, j * P:j * P + P], ident[:, :])
                                last.then_inc(pT_ready, 1)
                        if step in (21, 37):
                            c = step // 16 - 1
                            pe.wait_ge(o_lo_done, g * PAIRS + 8 * (c + 1))
                            pe.wait_ge(w_step.sem, w_step.at(g, 4))
                            for m in range(NK):
                                three_pass(pe, O[m][:, :],
                                           [(wo_hi[:, h, m * P:m * P + P], wo_lo[:, h, m * P:m * P + P],
                                             o_hi[:, h, :], o_lo[:, h, :]) for h in range(GH1)])\
                                    .then_inc(y_ready.sem, 1)
                        if 5 <= step < PER + 5 and step % 2 == 1:
                            p = (step - 5) // 2
                            i = tile_of(2 * p)
                            pe.wait_ge(lo_done, g * CH + before[2 * p + 2])
                            if p % 8 >= 2:
                                pe.wait_ge(o_lo_done, g * PAIRS + (p - 1))
                            else:
                                pe.wait_ge(y_done.sem, y_done.at(g, (p % 8 + 1 if p >= 8 else 0)))
                            three_pass(pe, O[p % 2][:, 0:2 * P],
                                       [(v_hi[:, j * P:j * P + P], v_lo[:, j * P:j * P + P],
                                         p_hi[:, p % RX, j].rearrange("p h c -> p (h c)"),
                                         p_lo[:, p % RX, j].rearrange("p h c -> p (h c)"))
                                        for j in range(i + 1)]).then_inc(o_ready, 1)

            @block.scalar
            def _(act):
                with act.Fori(0, KV1, 1) as g:
                    for n in range(NP + 1):
                        if n < NP:
                            act.wait_ge(proj_ready.sem, proj_ready.at(g, n + 1))
                            if n < QC:
                                if n >= 2:
                                    act.wait_ge(rope_step, g * 3 * QC + 3 * (n - 2) + 2)
                                for e in range(2):
                                    act.activation(swapped[64 * e:64 * e + 64, n % 2, :],
                                                   proj[n % 4][64 - 64 * e:128 - 64 * e, :], ACT.Copy)\
                                       .then_inc(swap_done, 1)
                            else:
                                c = n - QC
                                act.activation(vT[:, c * HALF:c * HALF + HALF], proj[n % 4], ACT.Copy)\
                                   .then_inc(vT_done, 1)
                        if 1 <= n <= QC:
                            m, c = (n - 1) // NC, (n - 1) % NC
                            act.wait_ge(rope_step, g * 3 * QC + 3 * n)
                            act.activation(q_hi[:, m, c * HALF:c * HALF + HALF], rot[:, (n - 1) % 2, :],
                                           ACT.Copy, scale=SCALE1 if m < GH1 else 1.0).then_inc(q_hi_done, 1)
                    for c in range(NC):
                        act.wait_ge(v_ready, g * NC + (c + 1))
                        act.activation(v_hi[:, c * HALF:c * HALF + HALF], X[c][:, :], ACT.Copy)\
                           .then_inc(v_hi_done, 1)
                    for step in range(PER + 5):
                        if 1 <= step < PER + 1:
                            u = step - 1
                            n = (tile_of(u) + 1) * P
                            act.wait_ge(max_done, g * PER + (u + 1))
                            if u >= RP:
                                act.wait_ge(pT_ready, g * CH + before[u - RP + 1])
                            act.activation(prob[:, u % RP, 0:n], S[u % 2][:, 0:n], ACT.Exp,
                                           bias=neg_max[:, u % 8:u % 8 + 1],
                                           accum_out=sums[:, u % 8:u % 8 + 1]).then_inc(exp_done, 1)
                        if 3 <= step < PER + 3:
                            u = step - 3
                            i, p = tile_of(u), u // 2
                            if p >= RX:
                                act.wait_ge(o_ready, g * PAIRS + (p - RX + 1))
                            for c in range(chunks_of(i)):
                                m = before[u] + c
                                js = slice(4 * c, min(4 * c + 4, i + 1))
                                act.wait_ge(pT_ready, g * CH + (m + 1))
                                act.activation(p_hi[:, p % RX, js, u % 2, :],
                                               X[m % 2][:, 0:(js.stop - js.start) * P]
                                               .rearrange("p (a c) -> p a c", c=P),
                                               ACT.Copy).then_inc(hi_done, 1)
                        if 2 <= step < PER + 2:
                            u = step - 2
                            n = (tile_of(u) + 1) * P
                            act.wait_ge(rinv_done, g * PER + (u + 1))
                            act.activation(prob[:, u % RP, 0:n], prob[:, u % RP, 0:n], ACT.Copy,
                                           scale=rinv[:, u % 8:u % 8 + 1]).then_inc(norm_done, 1)
                        if step >= 6 and step % 2 == 0:
                            p = (step - 6) // 2
                            i, h = tile_of(2 * p), 2 * p % GH1
                            act.wait_ge(o_ready, g * PAIRS + (p + 1))
                            if p % 8 == 0:
                                act.wait_ge(y_ready.sem, y_ready.at(g, (NK if p else 0)))
                            act.activation(o_hi[:, h:h + 2, (i % 4) * P:(i % 4) * P + P],
                                           O[p % 2][:, 0:2 * P].rearrange("p (h c) -> p h c", h=2),
                                           ACT.Copy).then_inc(o_hi_done, 1)

            @block.vector
            def _(dve):
                dve.wait_ge(zeroed, 2)
                y_done.prime(dve)
                with dve.Fori(0, KV1, 1) as g:
                    for n in range(QC):
                        m, c = n // NC, n % NC
                        sl, b = slice(c * HALF, c * HALF + HALF), n % 2
                        dve.wait_ge(swap_done, g * 2 * QC + 2 * n + 2)
                        dve.tensor_tensor(t1[:, b, :], proj[n % 4], rope_c[:, sl], ALU.mult)\
                           .then_inc(rope_step, 1)
                        dve.tensor_tensor(t2[:, b, :], swapped[:, b, :], rope_s[:, sl], ALU.mult)\
                           .then_inc(rope_step, 1)
                        dve.wait_ge(rope_step, g * 3 * QC + 3 * n + 2)
                        if n >= 2:
                            dve.wait_ge(q_hi_done, g * QC + (n - 1))
                        dve.tensor_tensor(rot[:, b, :], t1[:, b, :], t2[:, b, :], ALU.add)\
                           .then_inc(rope_step, 1)
                        dve.wait_ge(q_hi_done, g * QC + (n + 1))
                        dve.scalar_tensor_tensor(q_lo[:, m, sl], rot[:, b, :],
                                                 SCALE1 if m < GH1 else 1.0, f32(q_hi[:, m, sl]),
                                                 ALU.mult, ALU.subtract).then_inc(q_lo_done, 1)
                    for c in range(NC):
                        sl = slice(c * HALF, c * HALF + HALF)
                        dve.wait_ge(v_hi_done, g * NC + (c + 1))
                        dve.tensor_tensor(v_lo[:, sl], X[c][:, :], f32(v_hi[:, sl]), ALU.subtract)\
                           .then_inc(v_lo_done, 1)
                    for step in range(PER + 6):
                        if 2 <= step < PER + 2:
                            u = step - 2
                            dve.wait_ge(exp_done, g * PER + (u + 1))
                            dve.reciprocal(rinv[:, u % 8:u % 8 + 1], sums[:, u % 8:u % 8 + 1])\
                               .then_inc(rinv_done, 1)
                        if step < PER:
                            u = step
                            n = (tile_of(u) + 1) * P
                            dve.wait_ge(scores_ready, g * PER + (u + 1))
                            dve.tensor_reduce(neg_max[:, u % 8:u % 8 + 1], S[u % 2][:, 0:n], AX.X,
                                              ALU.max, negate=True).then_inc(max_done, 1)
                        if 3 <= step < PER + 3:
                            u = step - 3
                            i, p = tile_of(u), u // 2
                            for c in range(chunks_of(i)):
                                m = before[u] + c
                                js = slice(4 * c, min(4 * c + 4, i + 1))
                                dve.wait_ge(hi_done, g * CH + (m + 1))
                                dve.tensor_tensor(p_lo[:, p % RX, js, u % 2, :],
                                                  X[m % 2][:, 0:(js.stop - js.start) * P]
                                                  .rearrange("p (a c) -> p a c", c=P),
                                                  f32(p_hi[:, p % RX, js, u % 2, :]),
                                                  ALU.subtract).then_inc(lo_done, 1)
                        if 6 <= step < PER + 5 and step % 2 == 0:
                            p = (step - 6) // 2
                            i, h = tile_of(2 * p), 2 * p % GH1
                            sl = slice((i % 4) * P, (i % 4) * P + P)
                            dve.wait_ge(o_hi_done, g * PAIRS + (p + 1))
                            dve.tensor_tensor(o_lo[:, h:h + 2, sl],
                                              O[p % 2][:, 0:2 * P].rearrange("p (h c) -> p h c", h=2),
                                              f32(o_hi[:, h:h + 2, sl]), ALU.subtract).then_inc(o_lo_done, 1)
                        if step in (21, 37):
                            c = step // 16 - 1
                            for m in range(NK):
                                at = acc[:, m, c * HALF:c * HALF + HALF]
                                dve.wait_ge(y_ready.sem, y_ready.at(g, c * NK + m + 1))
                                dve.wait_ge(y_done.sem, y_done.at(g, c * NK + m))
                                dve.tensor_tensor(at, O[m][:, :], at, ALU.add).then_inc(y_done.sem, 1)


def combine1(nc, xT, sT, gT, out):
    with Scope(nc) as s:
        prod = s.sb("c1_prod", [P, NK, T], F32)
        res = s.sb("c1_res", [P, NK, T], F32)
        prod_done, res_done, stored = s.sem("c1_prod_done"), s.sem("c1_res_done"), s.sem("c1_stored")
        with nc.Block() as block:

            @block.vector
            def _(dve):
                for k in range(NK):
                    dve.tensor_tensor(prod[:, k, :], sT[:, k, :], gT[:, k, :], ALU.mult)\
                       .then_inc(prod_done, 1)
                    dve.wait_ge(prod_done, k + 1)
                    dve.tensor_tensor(res[:, k, :], xT[:, k, :], prod[:, k, :], ALU.add)\
                       .then_inc(res_done, 1)

            @block.sync
            def _(sp):
                for k in range(NK):
                    sp.wait_ge(res_done, k + 1)
                    sp.dma_start(out[k, :, :], res[:, k, :]).then_inc(stored, 16)
                sp.wait_ge(stored, 16 * NK)


def build(nc, a):
    with Scope(nc) as s:
        ident = s.sb("ident", [P, P], F32)
        ident_bf = s.sb("ident_bf", [P, P], BF16)
        mask = s.sb("mask", [P, P], BF16)
        xT = s.sb("xT", [P, NK, T], F32)
        xn_hi = s.sb("xn_hi", [P, NK, T], F32R)
        xn_lo = s.sb("xn_lo", [P, NK, T], F32R)
        sT = s.sb("sT", [P, NK, T], F32)
        bo = s.sb("bo", [P, NK], F32)
        s_down = s.sb("s_down", [P, NK], F32)
        wr = s.sb("wr", [P, NK, E1], F32)
        earlier = s.sb("earlier", [P, E1 * E1], F32)
        wo_hi = s.sb("wo_hi", [P, NK, D], F32R)
        wo_lo = s.sb("wo_lo", [P, NK, D], F32R)
        split = s.sem("w0_split")

        with Scope(nc) as s0:
            qT = s0.sb("qT", [P, H0 // 2, T], F32R)
            kT = s0.sb("kT", [P, H0 // 2, T], F32R)
            v3 = s0.sb("v3", [P, NT, H0, PARTS0, DH0], BF16)
            with Scope(nc) as s1:
                x_tok = s1.sb("x_tok", [P, NT, D], F32)
                w0 = s1.sb("w0", [P, NK, 3 * D], F32)
                w0_hi = s1.sb("w0_hi", [P, NK, 3 * D], F32R)
                w0_lo = s1.sb("w0_lo", [P, NK, 3 * D], F32R)
                wo = s1.sb("wo", [P, NK, D], F32)
                bias = s1.sb("bias", [P, 3 * D], F32)
                mask_f32 = s1.sb("mask_f32", [P, P], F32)
                rope_c = s1.sb("rope0_c", [P, NT, 2, DH0], F32)
                rope_s = s1.sb("rope0_s", [P, NT, 2, DH0], F32)
                loads = [(x_tok[:, :, :], a["x_tok"]), (ident[:, :], a["ident"]), (w0[:, :, :], a["w0"]),
                         (xT[:, :, :], a["xT"]), (wo[:, :, :], a["wo0"]),
                         (bias[:, :], a["bias0"].partition_broadcast(P)),
                         (rope_c[:, :, :, :], a["rope0_c"]), (rope_s[:, :, :, :], a["rope0_s"]),
                         (bo[:, :], a["bo"]), (s_down[:, :], a["s_down"]), (wr[:, :, :], a["wr"]),
                         (earlier[:, :], a["earlier"])]
                loads += [(mask_f32[:, :], a["mask"])]

                def split_weights(pool, loaded):
                    pool.wait_ge(loaded, 16 * len(loads))
                    pool.tensor_copy(mask[:, :], mask_f32[:, :]).then_inc(split, 1)
                    pool.tensor_copy(ident_bf[:, :], ident[:, :]).then_inc(split, 1)
                    n = 2
                    for src, hi, lo in ((w0, w0_hi, w0_lo), (wo, wo_hi, wo_lo)):
                        pool.tensor_copy(hi[:, :, :], src[:, :, :]).then_inc(split, 1)
                        n += 1
                        pool.wait_ge(split, n)
                        pool.tensor_tensor(lo[:, :, :], src[:, :, :], f32(hi[:, :, :]),
                                           ALU.subtract).then_inc(split, 1)
                        n += 1
                layer_norm(nc, "l0_", x_tok, xn_hi, xn_lo, ident, loads, split_weights)
                project0(nc, xn_hi, xn_lo, w0_hi, w0_lo, bias, rope_c, rope_s, ident, qT, kT, v3)
            att = s0.sb("att", [P, NT, D], F32)
            attention0(nc, qT, kT, v3, ident, ident_bf, mask, att)
            project_out0(nc, att, wo_hi, wo_lo, bo, ident, sT)
        gT = s.sb("gT", [P, NK, T], F32)
        gated_ffn(nc, "f0", FT0, a["wf0"], WCOLS, -ZERO_POINT, a["sf0"], s_down, xn_hi, xn_lo, None, gT)
        with Scope(nc) as s1:
            x_tok = s1.sb("x1_tok", [P, NT, D], F32)
            combine0(nc, xT, sT, gT, ident, x_tok)
            layer_norm(nc, "l1_", x_tok, xn_hi, xn_lo, ident, [])
        with Scope(nc) as s1:
            gate_hi = s1.sb("gate_hi", [P, T], F32R)
            route1(nc, xn_hi, xn_lo, wr, earlier, ident, gate_hi)
            gated_ffn(nc, "f1", FT1, a["wf1"], WCOLS + P, 0.0, None, None, xn_hi, xn_lo, gate_hi, gT)
        with Scope(nc) as s1:
            rope_c = s1.sb("rope1_c", [P, T], F32)
            rope_s = s1.sb("rope1_s", [P, T], F32)
            tables = s1.sem("rope1_loaded")
            with nc.Block() as block:
                @block.sync
                def _(sp):
                    sp.dma_start(rope_c[:, :], a["rope1_c"]).then_inc(tables, 16)
                    sp.dma_start(rope_s[:, :], a["rope1_s"]).then_inc(tables, 16)
                    sp.wait_ge(tables, 32)
            attention1(nc, xn_hi, xn_lo, a["wqkv1"], a["wo1"], rope_c, rope_s, ident, ident_bf, mask, sT)
        combine1(nc, xT, sT, gT, a["out"])


def _constants():
    f = np.float32
    c = {"ident": np.eye(P, dtype=f), "mask": np.triu(np.full((P, P), MASKED, f), 1)}
    pos = np.arange(T, dtype=f)

    def tables(base, half):
        inv = f(1.0) / f(base) ** (np.arange(half, dtype=f) / f(half))
        ang = (pos[:, None] * inv[None, :]).astype(f)
        return np.cos(ang.astype(np.float64)).astype(f), np.sin(ang.astype(np.float64)).astype(f)
    cos, sin = tables(10000.0, DH0 // 2)
    c0 = np.repeat(cos, 2, 1)
    s0 = np.stack([-sin, sin], -1).reshape(T, DH0)
    for name, tab in (("rope0_c", c0), ("rope0_s", s0)):
        both = np.stack([tab * f(SCALE0), tab], 1)
        c[name] = np.ascontiguousarray(both.reshape(NT, P, 2, DH0).transpose(1, 0, 2, 3)).astype(f)
    cos, sin = tables(10000.0, DH1 // 2)
    c["rope1_c"] = np.ascontiguousarray(np.concatenate([cos, cos], 1).T)
    c["rope1_s"] = np.ascontiguousarray(np.concatenate([-sin, sin], 1).T)
    b, e = np.meshgrid(np.arange(E1), np.arange(E1))
    c["earlier"] = np.broadcast_to((b < e).astype(f).reshape(1, -1), (P, E1 * E1)).copy()
    sel = np.zeros((FT1, P, P), f)
    for tile in range(FT1):
        for j in range(P):
            row = tile * P + j
            x = row // F1 if row < E1 * F1 else E1
            sel[tile, x, j] = sel[tile, 32 + x, j] = 1.0
    return c, sel


def _rows(w):
    return np.ascontiguousarray(w.reshape(w.shape[0] // P, P, w.shape[1]).transpose(1, 0, 2))


def _ffn_tiles(wg, wu, wd, tiles):
    def pad(w):
        out = np.zeros((tiles * P, D), w.dtype)
        out[:w.shape[0]] = w
        return out.reshape(tiles, P, D)
    def up(w):
        return pad(w).reshape(tiles, P, NK, P).transpose(0, 3, 2, 1).reshape(tiles, P, NK * P)
    return np.ascontiguousarray(np.concatenate([up(wg), up(wu), pad(wd.T)], 2))


def kernel(**inputs):
    import concourse.bacc as _bacc
    from concourse.bass_utils import run_bass_kernel_spmd as _run
    x = {k: np.asarray(v) for k, v in inputs.items()}
    arrays, sel = _constants()
    x0 = x["L0_attn_x"].reshape(T, D)
    arrays["x_tok"] = np.ascontiguousarray(x0.reshape(NT, P, D).transpose(1, 0, 2))
    arrays["xT"] = _rows(x0.T)
    arrays["w0"] = _rows(np.concatenate([x["L0_attn_Wq"].T, x["L0_attn_Wk"].T, x["L0_attn_Wv"].T], 1))
    arrays["wo0"] = _rows(x["L0_attn_Wo"].T)
    arrays["bias0"] = np.concatenate([x["L0_attn_bq"], x["L0_attn_bk"], x["L0_attn_bv"]])
    arrays["bo"] = np.ascontiguousarray(x["L0_attn_bo"].reshape(NK, P).T)
    arrays["s_down"] = np.ascontiguousarray(x["L0_ffn_s_down"].reshape(NK, P).T)
    arrays["wf0"] = _ffn_tiles(x["L0_ffn_wq_gate"], x["L0_ffn_wq_up"], x["L0_ffn_wq_down"], FT0)
    sf = np.zeros((2, FT0 * P), np.float32)
    sf[0, :HID0], sf[1, :HID0] = x["L0_ffn_s_gate"], x["L0_ffn_s_up"]
    arrays["sf0"] = np.ascontiguousarray(sf.reshape(2, FT0, P).transpose(1, 2, 0))
    arrays["wr"] = _rows(x["L1_ffn_Wr"].T)
    wg = np.concatenate([x["L1_ffn_Wg"].reshape(E1 * F1, D), x["L1_ffn_Wsg"]])
    wu = np.concatenate([x["L1_ffn_Wu"].reshape(E1 * F1, D), x["L1_ffn_Wsu"]])
    wd = np.concatenate([x["L1_ffn_Wd"].transpose(1, 0, 2).reshape(D, E1 * F1), x["L1_ffn_Wsd"]], 1)
    arrays["wf1"] = np.concatenate([_ffn_tiles(wg, wu, wd, FT1), sel], 2)
    q = x["L1_attn_Wq"].reshape(NK, P, KV1, GH1 * DH1)
    k = x["L1_attn_Wk"].reshape(NK, P, KV1, DH1)
    v = x["L1_attn_Wv"].reshape(NK, P, KV1, DH1)
    arrays["wqkv1"] = np.ascontiguousarray(
        np.concatenate([q, k, v], 3).transpose(2, 1, 0, 3).reshape(KV1, P, GWCOLS1))
    arrays["wo1"] = np.ascontiguousarray(
        x["L1_attn_Wo"].reshape(KV1, GH1, P, D).transpose(0, 2, 1, 3).reshape(KV1, P, GH1 * D))

    nc = _bacc.Bacc("TRN2", target_bir_lowering=False, num_devices=1)
    a = {n: nc.dram_tensor(f"in_{n}", v.shape, mybir.dt.from_np(v.dtype), kind="ExternalInput").ap()
         for n, v in arrays.items()}
    a["out"] = nc.dram_tensor("out_x", (NK, P, T), F32, kind="ExternalOutput").ap()
    build(nc, a)
    r = _run(nc, [{f"in_{n}": v for n, v in arrays.items()}], core_ids=[0])
    out = np.asarray(r.results[0]["out_x"])
    return np.ascontiguousarray(out.reshape(D, T).T).reshape(1, T, D)
```

```python
from contextlib import ExitStack

import numpy as np

import concourse.bass as bass
from concourse import mybir

F32, F32R = mybir.dt.float32, mybir.dt.float32r
F16, BF16, I32 = mybir.dt.float16, mybir.dt.bfloat16, mybir.dt.int32
ALU = mybir.AluOpType
ACT = mybir.ActivationFunctionType
AX = mybir.AxisListType

P = 128
T = 1024
D = 256
NT = T // P
NK = D // P
HALF = 512
NC = T // HALF
EPS = 1e-5
MASKED = -3.0e38

H0, DH0 = 16, 16
GROUPS0, GH0 = 4, 4
PARTS0 = 3
VW0 = PARTS0 * DH0
SCALE0 = DH0 ** -0.5
FT0, HID0 = 6, 704

KV1, GH1, DH1 = 4, 4, 128
SCALE1 = DH1 ** -0.5
E1, F1, FS1 = 8, 176, 352
FT1 = (E1 * F1 + 384) // P
TOPK = 2
ZERO_POINT = 128.0
WCOLS = 2 * NK * P + D
GWCOLS1 = NK * (GH1 * P + P + P)


def chunks_of(i):
    return (i * P + P + HALF - 1) // HALF


def chunks_before(units, tile_of):
    before = [0]
    for u in range(units):
        before.append(before[-1] + chunks_of(tile_of(u)))
    return before


class Scope:

    def __init__(self, nc, tag=""):
        self.nc, self.tag, self.stack = nc, tag, ExitStack()

    def __enter__(self):
        self.stack.__enter__()
        return self

    def __exit__(self, *a):
        return self.stack.__exit__(*a)

    def sb(self, name, shape, dt):
        return self.stack.enter_context(self.nc.sbuf_tensor(self.tag + name, shape, dt))

    def ps(self, name, shape, dt=F32):
        return self.stack.enter_context(self.nc.psum_tensor(self.tag + name, shape, dt))

    def sem(self, name):
        return self.stack.enter_context(self.nc.semaphore(self.tag + name))


class Count:

    def __init__(self, sem, per):
        self.sem, self.per = sem, per

    def prime(self, eng):
        eng.sem_inc(self.sem, self.per)

    def at(self, g, n):
        return g * self.per + (self.per + n)


def f32(ap):
    return ap.bitcast(F32)


def three_pass(pe, out, terms, start=True, stop=True, check=True):
    n, last = 0, None
    for a_hi, a_lo, b_hi, b_lo in terms:
        for a, b in ((a_hi, b_hi), (a_hi, b_lo), (a_lo, b_hi)):
            last = pe.matmul(out, a, b, start=start and n == 0,
                             stop=stop and n == 3 * len(terms) - 1, skip_group_check=not check)
            n += 1
    return last


def layer_norm(nc, tag, x_tok, xn_hi, xn_lo, ident, loads, side_jobs=None):
    with Scope(nc, tag) as s:
        xn = s.sb("xn_tok", [P, NT, D], F32)
        stats = s.sb("ln_stats", [P, NT, 6], F32)
        mv = s.sb("ln_mv", [P, NT, 2], F32)
        ve = s.sb("ln_ve", [P, NT], F32)
        sd = s.sb("ln_sd", [P, NT], F32)
        y = s.sb("ln_y", [P, 3, NT], F32)
        rstd = s.sb("ln_rstd", [P, NT], F32)
        xT = [s.ps(f"ln_xT{k}", [P, T]) for k in range(NK)]
        loaded = s.sem("ln_loaded")
        stats_done, small_done = s.sem("ln_stats_done"), s.sem("ln_small_done")
        sd_done, norm_done = s.sem("ln_sd_done"), s.sem("ln_norm_done")
        xT_ready, hi_done, lo_done = s.sem("ln_xT_ready"), s.sem("ln_hi_done"), s.sem("ln_lo_done")
        with nc.Block() as block:

            @block.sync
            def _(sp):
                for out, src in loads:
                    sp.dma_start(out, src).then_inc(loaded, 16)
                sp.wait_ge(loaded, 16 * len(loads))

            if side_jobs:
                @block.gpsimd
                def _(pool):
                    side_jobs(pool, loaded)

            @block.vector
            def _(dve):
                if loads:
                    dve.wait_ge(loaded, 16 * len(loads))
                for t in range(NT):
                    dve.bn_stats(stats[:, t, :], x_tok[:, t, :]).then_inc(stats_done, 1)
                for t in range(NT):
                    dve.wait_ge(stats_done, t + 1)
                    dve.bn_aggr(mv[:, t, :], stats[:, t, :]).then_inc(stats_done, 1)
                dve.wait_ge(stats_done, 2 * NT)
                dve.tensor_scalar(ve[:, :], mv[:, :, 1], EPS, None, ALU.add).then_inc(small_done, 1)
                dve.wait_ge(sd_done, 1)
                dve.reciprocal(y[:, 0, :], sd[:, :]).then_inc(small_done, 1)
                dve.wait_ge(small_done, 2)
                dve.tensor_tensor(y[:, 1, :], y[:, 0, :], y[:, 0, :], ALU.mult).then_inc(small_done, 1)
                dve.wait_ge(small_done, 3)
                dve.tensor_tensor(y[:, 2, :], y[:, 1, :], ve[:, :], ALU.mult).then_inc(small_done, 1)
                dve.wait_ge(small_done, 4)
                dve.tensor_scalar(y[:, 1, :], y[:, 2, :], -0.5, 1.5, ALU.mult, ALU.add)\
                   .then_inc(small_done, 1)
                dve.wait_ge(small_done, 5)
                dve.tensor_tensor(rstd[:, :], y[:, 0, :], y[:, 1, :], ALU.mult).then_inc(small_done, 1)
                dve.wait_ge(small_done, 6)
                for t in range(NT):
                    dve.tensor_scalar(xn[:, t, :], x_tok[:, t, :], mv[:, t, 0:1], rstd[:, t:t + 1],
                                      ALU.subtract, ALU.mult).then_inc(norm_done, 1)
                n = 0
                for c in range(NC):
                    for k in range(NK):
                        n += 1
                        sl = slice(c * HALF, c * HALF + HALF)
                        dve.wait_ge(hi_done, n)
                        dve.tensor_tensor(xn_lo[:, k, sl], xT[k][:, sl], f32(xn_hi[:, k, sl]),
                                          ALU.subtract).then_inc(lo_done, 1)

            @block.tensor
            def _(pe):
                if loads:
                    pe.wait_ge(loaded, 16 * len(loads))
                for t in range(NT):
                    pe.wait_ge(norm_done, t + 1)
                    for k in range(NK):
                        last = pe.transpose(xT[k][:, t * P:t * P + P], xn[:, t, k * P:k * P + P],
                                            ident[:, :])
                    last.then_inc(xT_ready, 1)

            @block.scalar
            def _(act):
                act.wait_ge(small_done, 1)
                act.activation(sd[:, :], ve[:, :], ACT.Sqrt).then_inc(sd_done, 1)
                for c in range(NC):
                    for k in range(NK):
                        sl = slice(c * HALF, c * HALF + HALF)
                        act.wait_ge(xT_ready, (c + 1) * NT // NC)
                        act.activation(xn_hi[:, k, sl], xT[k][:, sl], ACT.Copy).then_inc(hi_done, 1)


def project0(nc, xn_hi, xn_lo, w_hi, w_lo, bias, rope_c, rope_s, ident, qT, kT, v3):
    QK = 2 * H0 * DH0
    with Scope(nc) as s:
        qkv = s.sb("p0_qkv", [P, 2, 3 * D], F32)
        t1 = s.sb("p0_t1", [P, QK], F32)
        t2 = s.sb("p0_t2", [P, QK], F32)
        rot = s.sb("p0_rot", [P, 2, QK], F32)
        zq = s.sb("p0_zq", [P, 2, H0, 4, DH0], F32R)
        zk = s.sb("p0_zk", [P, 2, H0, 4, DH0], F32R)
        vr = s.sb("p0_vr", [P, 2, D], F32)
        proj = [s.ps(f"p0_proj{i}", [P, 2 * HALF]) for i in range(2)]
        tp = [s.ps(f"p0_tp{i}", [P, HALF]) for i in range(4)]
        proj_ready, qkv_done, rope_step = s.sem("p0_proj_ready"), s.sem("p0_qkv_done"), s.sem("p0_rope_step")
        z_hi_done, z_lo_done = s.sem("p0_z_hi_done"), s.sem("p0_z_lo_done")
        tp_ready, tp_taken, v_step = s.sem("p0_tp_ready"), s.sem("p0_tp_taken"), s.sem("p0_v_step")

        def pairs(z):
            return z.rearrange("p h r d -> p (h r d)").rearrange("p (a c) -> p a c", c=P)

        with nc.Block() as block:

            @block.tensor
            def _(pe):
                for t in range(NT + 1):
                    if t < NT:
                        if t >= 2:
                            pe.wait_ge(qkv_done, t - 1)
                        tok = slice(t * P, t * P + P)
                        for a, b in ((0, HALF), (HALF, 3 * D)):
                            last = three_pass(pe, proj[t % 2][:, a:b],
                                              [(xn_hi[:, k, tok], xn_lo[:, k, tok],
                                                w_hi[:, k, a:b], w_lo[:, k, a:b]) for k in range(NK)])
                        last.then_inc(proj_ready, 1)
                    if t >= 1:
                        u = t - 1
                        pe.wait_ge(z_hi_done, 2 * u + 2)
                        pe.wait_ge(z_lo_done, 2 * u + 2)
                        if u >= 1:
                            pe.wait_ge(tp_taken, 4 * u)
                        for b in range(4):
                            z = pairs((zq if b < 2 else zk)[:, u % 2])
                            for j in range(4):
                                pe_in = f32(z[:, 4 * (b % 2) + j, :])
                                last = pe.transpose(tp[b][:, j * P:j * P + P], pe_in, ident[:, :])
                            last.then_inc(tp_ready, 1)

            @block.vector
            def _(dve):
                for t in range(NT):
                    dve.wait_ge(proj_ready, t + 1)
                    if t >= 2:
                        dve.wait_ge(v_step, 4 * (t - 1))
                        dve.wait_ge(z_hi_done, 2 * (t - 1))
                    dve.tensor_tensor(qkv[:, t % 2, :], proj[t % 2][:, 0:3 * D], bias[:, :],
                                      ALU.add).then_inc(qkv_done, 1)
                    dve.wait_ge(qkv_done, t + 1)
                    if t >= 1:
                        dve.wait_ge(rope_step, 4 * t)
                    x = qkv[:, t % 2, 0:QK].rearrange("p (a h d) -> p a h d", a=2, h=H0)
                    y1 = t1[:, :].rearrange("p (a h d) -> p a h d", a=2, h=H0)
                    y2 = t2[:, :].rearrange("p (a h d) -> p a h d", a=2, h=H0)

                    def table(tab, lo):
                        v = tab[:, t, :, lo::2] if lo is not None else tab[:, t, :, :]
                        n = DH0 // 2 if lo is not None else DH0
                        return v.unsqueeze(2).broadcast_to([P, 2, H0, n])
                    dve.tensor_tensor(y1, x, table(rope_c, None), ALU.mult).then_inc(rope_step, 1)
                    dve.tensor_tensor(y2[:, :, :, 0::2], x[:, :, :, 1::2], table(rope_s, 0),
                                      ALU.mult).then_inc(rope_step, 1)
                    dve.tensor_tensor(y2[:, :, :, 1::2], x[:, :, :, 0::2], table(rope_s, 1),
                                      ALU.mult).then_inc(rope_step, 1)
                    dve.wait_ge(rope_step, 4 * t + 3)
                    dve.tensor_tensor(rot[:, t % 2, :], t1[:, :], t2[:, :], ALU.add).then_inc(rope_step, 1)
                    for a, z in enumerate((zq, zk)):
                        r = rot[:, t % 2, a * D:a * D + D].rearrange("p (h d) -> p h d", h=H0)\
                            .unsqueeze(2).broadcast_to([P, H0, 2, DH0])
                        if a == 0:
                            hi, lo = z[:, t % 2, :, 0:2, :], z[:, t % 2, :, 2:4, :]
                        else:
                            hi, lo = z[:, t % 2, :, 0::2, :], z[:, t % 2, :, 1::2, :]
                        dve.wait_ge(z_hi_done, 2 * t + 1 + a)
                        dve.tensor_tensor(lo, r, f32(hi), ALU.subtract).then_inc(z_lo_done, 1)

            @block.gpsimd
            def _(pool):
                for t in range(NT):
                    pool.wait_ge(qkv_done, t + 1)
                    v = qkv[:, t % 2, QK:3 * D].rearrange("p (h d) -> p h d", h=H0)
                    parts = [v3[:, t, :, n, :] for n in range(PARTS0)]
                    r = [vr[:, n, :].rearrange("p (h d) -> p h d", h=H0) for n in range(2)]
                    pool.tensor_copy(parts[0], v).then_inc(v_step, 1)
                    pool.wait_ge(v_step, 4 * t + 1)
                    pool.tensor_tensor(r[0], v, parts[0], ALU.subtract).then_inc(v_step, 1)
                    pool.wait_ge(v_step, 4 * t + 2)
                    pool.tensor_copy(parts[1], r[0]).then_inc(v_step, 1)
                    pool.wait_ge(v_step, 4 * t + 3)
                    pool.tensor_tensor(parts[2], r[0], parts[1], ALU.subtract).then_inc(v_step, 1)

            @block.scalar
            def _(act):
                for t in range(NT + 1):
                    if t < NT:
                        act.wait_ge(rope_step, 4 * t + 4)
                        if t >= 2:
                            act.wait_ge(tp_ready, 4 * (t - 1))
                        for a, z in enumerate((zq, zk)):
                            r = rot[:, t % 2, a * D:a * D + D].rearrange("p (h d) -> p h d", h=H0)\
                                .unsqueeze(2).broadcast_to([P, H0, 2, DH0])
                            hi = z[:, t % 2, :, 0:2, :] if a == 0 else z[:, t % 2, :, 0::2, :]
                            act.activation(hi, r, ACT.Copy).then_inc(z_hi_done, 1)
                    if t >= 1:
                        u = t - 1
                        for b in range(4):
                            act.wait_ge(tp_ready, 4 * u + b + 1)
                            dst = (qT if b < 2 else kT)[:, 4 * (b % 2):4 * (b % 2) + 4, u * P:u * P + P]
                            act.activation(dst, tp[b][:, :].rearrange("p (a c) -> p a c", a=4),
                                           ACT.Copy).then_inc(tp_taken, 1)


def attention0(nc, qT, kT, v3, ident, ident_bf, mask, att):
    PER = 2 * NT * GH0
    tile_of = lambda u: u // GH0 % NT
    before = chunks_before(PER, tile_of)
    CH = before[-1]
    RING = 3
    with Scope(nc) as s:
        qs = [s.sb(f"a0_q{b}", [P, GH0, T], F32R) for b in range(2)]
        ks = [s.sb(f"a0_k{b}", [P, GH0 // 2, T], F32R) for b in range(2)]
        vs = [s.sb(f"a0_v{b}", [P, NT, GH0 * VW0], BF16) for b in range(2)]
        prob = s.sb("a0_prob", [P, RING, T], F32)
        p_hi = s.sb("a0_p_hi", [P, RING, NT, P], F16)
        p_lo = s.sb("a0_p_lo", [P, RING, NT, P], F16)
        neg_max = s.sb("a0_neg_max", [P, 8], F32)
        sums = s.sb("a0_sums", [P, 4, GH0], F32)
        rinv = s.sb("a0_rinv", [P, 2, GH0], F32)
        osum = s.sb("a0_osum", [P, 2, GH0 * DH0], F32)
        S = [s.ps(f"a0_S{b}", [P, 2 * HALF]) for b in range(2)]
        X = [s.ps(f"a0_X{b}", [P, HALF]) for b in range(2)]
        O = [s.ps(f"a0_O{b}", [P, HALF]) for b in range(2)]
        zeroed = s.sem("a0_zeroed")
        staged = [s.sem(f"a0_staged{b}") for b in range(2)]
        scores_ready, max_done, exp_done = s.sem("a0_scores_ready"), s.sem("a0_max_done"), s.sem("a0_exp_done")
        pT_ready, hi_done, lo_done = s.sem("a0_pT_ready"), s.sem("a0_hi_done"), s.sem("a0_lo_done")
        o_ready, o_taken, rinv_done, out_done = (s.sem("a0_o_ready"), s.sem("a0_o_taken"),
                                                 s.sem("a0_rinv_done"), s.sem("a0_out_done"))
        NSTAGE = 2 * (GH0 // 2) + 1 + 1

        with nc.Block() as block:

            @block.sync
            def _(sp):
                sp.wait_ge(zeroed, 4)
                for n in range(GROUPS0):
                    b = n % 2
                    if n >= 2:
                        sp.wait_ge(scores_ready, (n - 1) * PER // 2)
                        sp.wait_ge(o_ready, (n - 1) * PER // 2)
                    for a in range(GH0 // 2):
                        pair = n * (GH0 // 2) + a
                        for e in range(2):
                            rows = slice(64 * e, 64 * e + 64)
                            sp.dma_start(f32(qs[b][rows, 2 * a + e, :]), f32(qT[rows, pair, :]))\
                              .then_inc(staged[b], 16)
                    sp.dma_start(f32(ks[b][:, :, :]), f32(kT[:, n * 2:n * 2 + 2, :])).then_inc(staged[b], 16)
                    sp.dma_start(vs[b][:, :, :],
                                 v3[:, :, n * GH0:n * GH0 + GH0].rearrange("p t h r d -> p t (h r d)"))\
                      .then_inc(staged[b], 16)
                for b in range(2):
                    sp.wait_ge(staged[b], 2 * NSTAGE * 16)

            @block.gpsimd
            def _(pool):
                for b in range(2):
                    for e in range(2):
                        rows = slice(64 - 64 * e, 128 - 64 * e)
                        pool.memset(f32(qs[b][rows, e::2, :]), 0.0).then_inc(zeroed, 1)

            @block.tensor
            def _(pe):
                with pe.Fori(0, 2, 1) as g:
                    for step in range(PER + 5):
                        if step < PER:
                            u = step
                            i, h, b = tile_of(u), u % GH0, u // (PER // 2)
                            n = (i + 1) * P
                            if u % (PER // 2) == 0:
                                pe.wait_ge(staged[b], g * (NSTAGE * 16) + NSTAGE * 16)
                            if u >= 2:
                                pe.wait_ge(exp_done, g * PER + (u - 1))
                            for a in range(0, n, HALF):
                                e = min(a + HALF, n)
                                diag = e == n
                                pe.matmul(S[u % 2][:, a:e], qs[b][:, h, i * P:i * P + P],
                                          ks[b][:, h // 2, a:e], start=True, stop=not diag)
                            pe.matmul(S[u % 2][:, n - P:n], ident_bf[:, :], mask[:, :],
                                      start=False, stop=True).then_inc(scores_ready, 1)
                        if 3 <= step < PER + 3:
                            u = step - 3
                            i = tile_of(u)
                            pe.wait_ge(exp_done, g * PER + (u + 1))
                            for c in range(chunks_of(i)):
                                m = before[u] + c
                                if m >= 2:
                                    pe.wait_ge(lo_done, g * CH + (m - 1))
                                js = range(4 * c, min(4 * c + 4, i + 1))
                                for j in js:
                                    last = pe.transpose(X[m % 2][:, (j % 4) * P:(j % 4) * P + P],
                                                        prob[:, u % RING, j * P:j * P + P], ident[:, :])
                                last.then_inc(pT_ready, 1)
                        if step >= 5:
                            u = step - 5
                            i, h, b = tile_of(u), u % GH0, u // (PER // 2)
                            r = u // GH0
                            pe.wait_ge(lo_done, g * CH + before[u + 1])
                            if h == 0 and r >= 2:
                                pe.wait_ge(o_taken, g * (PER // GH0) + (r - 1))
                            n, count = 0, 2 * (i + 1)
                            for j in range(i + 1):
                                for half in (p_hi, p_lo):
                                    last = pe.matmul(O[r % 2][:, h * VW0:h * VW0 + VW0],
                                                     half[:, u % RING, j, :],
                                                     vs[b][:, j, h * VW0:h * VW0 + VW0],
                                                     start=n == 0, stop=n == count - 1)
                                    n += 1
                            last.then_inc(o_ready, 1)

            @block.scalar
            def _(act):
                with act.Fori(0, 2, 1) as g:
                    for step in range(PER + 3):
                        if 1 <= step < PER + 1:
                            u = step - 1
                            i = tile_of(u)
                            n = (i + 1) * P
                            act.wait_ge(max_done, g * PER + (u + 1))
                            if u >= RING:
                                act.wait_ge(pT_ready, g * CH + before[u - RING + 1])
                            act.activation(prob[:, u % RING, 0:n], S[u % 2][:, 0:n], ACT.Exp,
                                           bias=neg_max[:, u % 8:u % 8 + 1],
                                           accum_out=sums[:, u // GH0 % 4, u % GH0:u % GH0 + 1])\
                               .then_inc(exp_done, 1)
                        if step >= 3:
                            u = step - 3
                            i = tile_of(u)
                            if u >= RING:
                                act.wait_ge(o_ready, g * PER + (u - RING + 1))
                            for c in range(chunks_of(i)):
                                m = before[u] + c
                                js = slice(4 * c, min(4 * c + 4, i + 1))
                                n = (js.stop - js.start) * P
                                act.wait_ge(pT_ready, g * CH + (m + 1))
                                act.activation(p_hi[:, u % RING, js, :].rearrange("p a c -> p (a c)"),
                                               X[m % 2][:, 0:n], ACT.Copy).then_inc(hi_done, 1)

            @block.vector
            def _(dve):
                with dve.Fori(0, 2, 1) as g:
                    for step in range(PER + 9):
                        if step < PER:
                            u = step
                            n = (tile_of(u) + 1) * P
                            dve.wait_ge(scores_ready, g * PER + (u + 1))
                            dve.tensor_reduce(neg_max[:, u % 8:u % 8 + 1], S[u % 2][:, 0:n], AX.X,
                                              ALU.max, negate=True).then_inc(max_done, 1)
                        if 3 <= step < PER + 3:
                            u = step - 3
                            i = tile_of(u)
                            for c in range(chunks_of(i)):
                                m = before[u] + c
                                js = slice(4 * c, min(4 * c + 4, i + 1))
                                n = (js.stop - js.start) * P
                                dve.wait_ge(hi_done, g * CH + (m + 1))
                                dve.tensor_tensor(p_lo[:, u % RING, js, :].rearrange("p a c -> p (a c)"),
                                                  X[m % 2][:, 0:n],
                                                  p_hi[:, u % RING, js, :].rearrange("p a c -> p (a c)"),
                                                  ALU.subtract).then_inc(lo_done, 1)
                        if step >= 9 and step % GH0 == 1:
                            r = step // GH0 - 2
                            i, b = r % NT, r // NT
                            done = PER // GH0
                            dve.wait_ge(o_ready, g * PER + (r + 1) * GH0)
                            dve.reciprocal(rinv[:, r % 2, :], sums[:, r % 4, :]).then_inc(rinv_done, 1)
                            dve.tensor_reduce(
                                osum[:, r % 2, :].rearrange("p (h d) -> p h d", h=GH0),
                                O[r % 2][:, 0:GH0 * VW0].rearrange("p (h r d) -> p h d r", h=GH0, r=PARTS0),
                                AX.X, ALU.add).then_inc(o_taken, 1)
                            dve.wait_ge(rinv_done, g * done + (r + 1))
                            dve.wait_ge(o_taken, g * done + (r + 1))
                            dve.tensor_tensor(
                                att[:, i, bass.ds(g * (2 * GH0 * DH0) + b * GH0 * DH0, GH0 * DH0)]
                                .rearrange("p (h d) -> p h d", h=GH0),
                                osum[:, r % 2, :].rearrange("p (h d) -> p h d", h=GH0),
                                rinv[:, r % 2, :].unsqueeze(2).broadcast_to([P, GH0, DH0]),
                                ALU.mult).then_inc(out_done, 1)


def project_out0(nc, att, wo_hi, wo_lo, bo, ident, sT):
    with Scope(nc) as s:
        a_hi = s.sb("o0_a_hi", [P, NK, T], F32R)
        a_lo = s.sb("o0_a_lo", [P, NK, T], F32R)
        aT = [s.ps(f"o0_aT{k}", [P, T]) for k in range(NK)]
        acc = [s.ps(f"o0_acc{c}", [P, 2 * HALF]) for c in range(NC)]
        aT_ready, hi_done, lo_done, y_ready, y_done = (
            s.sem("o0_aT_ready"), s.sem("o0_hi_done"), s.sem("o0_lo_done"), s.sem("o0_y_ready"), s.sem("o0_y_done"))
        with nc.Block() as block:

            @block.tensor
            def _(pe):
                for c in range(NC):
                    for k in range(NK):
                        for t in range(4 * c, 4 * c + 4):
                            last = pe.transpose(aT[k][:, t * P:t * P + P], att[:, t, k * P:k * P + P],
                                                ident[:, :])
                        last.then_inc(aT_ready, 1)
                for c in range(NC):
                    pe.wait_ge(lo_done, NK * (c + 1))
                    sl = slice(c * HALF, c * HALF + HALF)
                    for m in range(NK):
                        three_pass(pe, acc[c][:, m * HALF:m * HALF + HALF],
                                   [(wo_hi[:, k, m * P:m * P + P], wo_lo[:, k, m * P:m * P + P],
                                     a_hi[:, k, sl], a_lo[:, k, sl]) for k in range(NK)])\
                            .then_inc(y_ready, 1)

            @block.scalar
            def _(act):
                n = 0
                for c in range(NC):
                    for k in range(NK):
                        n += 1
                        sl = slice(c * HALF, c * HALF + HALF)
                        act.wait_ge(aT_ready, n)
                        act.activation(a_hi[:, k, sl], aT[k][:, sl], ACT.Copy).then_inc(hi_done, 1)

            @block.vector
            def _(dve):
                n = 0
                for c in range(NC):
                    for k in range(NK):
                        n += 1
                        sl = slice(c * HALF, c * HALF + HALF)
                        dve.wait_ge(hi_done, n)
                        dve.tensor_tensor(a_lo[:, k, sl], aT[k][:, sl], f32(a_hi[:, k, sl]),
                                          ALU.subtract).then_inc(lo_done, 1)
                n = 0
                for c in range(NC):
                    for m in range(NK):
                        n += 1
                        dve.wait_ge(y_ready, n)
                        dve.tensor_scalar(sT[:, m, c * HALF:c * HALF + HALF],
                                          acc[c][:, m * HALF:m * HALF + HALF],
                                          bo[:, m:m + 1], None, ALU.add).then_inc(y_done, 1)


def gated_ffn(nc, tag, tiles, weights, cols, offset, scales, down_scale, xn_hi, xn_lo, gate_hi, gT,
              side_loads=None, side_jobs=None):
    routed = gate_hi is not None
    with Scope(nc) as s:
        raw = [s.sb(f"{tag}_raw{b}", [P, cols], weights.dtype) for b in range(2)]
        wx_hi = [s.sb(f"{tag}_wx_hi{b}", [P, cols - D], F32R) for b in range(2)]
        wx_lo = [s.sb(f"{tag}_wx_lo{b}", [P, 2 * NK * P], F32R) for b in range(2)]
        wd_hi = [s.sb(f"{tag}_wd_hi{b}", [P, D], F32R) for b in range(2)]
        wd_lo = [s.sb(f"{tag}_wd_lo{b}", [P, D], F32R) for b in range(2)]
        sc = [s.sb(f"{tag}_sc{b}", [P, 2], F32) for b in range(2)]
        sg = s.sb(f"{tag}_sg", [P, NC, HALF], F32)
        h1 = s.sb(f"{tag}_h1", [P, NC, HALF], F32)
        hh = s.sb(f"{tag}_hh", [P, NC, HALF], F32)
        h_hi = [s.sb(f"{tag}_h_hi{b}", [P, T], F32R) for b in range(2)]
        h_lo = [s.sb(f"{tag}_h_lo{b}", [P, T], F32R) for b in range(2)]
        G = [s.ps(f"{tag}_G{c}", [P, HALF]) for c in range(NC)]
        U = [s.ps(f"{tag}_U{c}", [P, HALF]) for c in range(NC)]
        acc = [s.ps(f"{tag}_acc{c}", [P, HALF]) for c in range(NK * NC)]
        two = lambda name: [s.sem(f"{tag}_{name}{b}") for b in range(2)]
        counts = lambda name, per: [Count(x, per) for x in two(name)]
        loaded, wx_hi_done, wx_lo_done = two("loaded"), two("wx_hi_done"), two("wx_lo_done")
        wd_hi_done, wd_lo_done = two("wd_hi_done"), counts("wd_lo_done", 1)
        gate_ready, up_ready, silu_done = two("gate_ready"), two("up_ready"), two("silu_done")
        mix_ready, h1_done, h_done = two("mix_ready"), two("h1_done"), counts("h_done", NC)
        h_hi_done, h_lo_done = counts("h_hi_done", NC), counts("h_lo_done", NC)
        down_done = counts("down_done", 1)
        zeroed, opened, all_down, g_done = (s.sem(f"{tag}_zeroed"), s.sem(f"{tag}_opened"),
                                            s.sem(f"{tag}_all_down"), s.sem(f"{tag}_g_done"))
        NL = 2 if scales is not None else 1
        passes = tiles // 2
        half = lambda c: slice(c * HALF, c * HALF + HALF)

        def w(t, part, k):
            at = (part * NK + k) * P
            return t[:, at:at + P]

        def down(pe, b, stop):
            for c in range(NC):
                for m in range(NK):
                    cut = slice(m * P, m * P + P)
                    last = three_pass(pe, acc[m * NC + c][:, :],
                                      [(wd_hi[b][:, cut], wd_lo[b][:, cut], h_hi[b][:, half(c)], h_lo[b][:, half(c)])],
                                      start=False, stop=stop, check=False)
            return last

        with nc.Block() as block:

            @block.sync
            def _(sp):
                sp.dma_start(raw[0][:, :], weights[0, :, :]).then_inc(loaded[0], 16)
                if scales is not None:
                    sp.dma_start(sc[0][:, :], scales[0, :, :]).then_inc(loaded[0], 16)
                if side_loads:
                    side_loads(sp)
                with sp.Fori(0, passes, 1) as g:
                    for b in range(2):
                        n = 1 - b
                        sp.wait_ge(wd_lo_done[n].sem, wd_lo_done[n].at(g, b))
                        sp.dma_start(raw[n][:, :], weights[g * 2 + (b + 1), :, :]).then_inc(loaded[n], 16)
                        if scales is not None:
                            sp.wait_ge(h_done[n].sem, h_done[n].at(g, NC * b))
                            sp.dma_start(sc[n][:, :], scales[g * 2 + (b + 1), :, :]).then_inc(loaded[n], 16)

            @block.gpsimd
            def _(pool):
                for t in (h_hi, h_lo, wd_hi, wd_lo):
                    pool.memset(f32(t[1][:, :]), 0.0).then_inc(zeroed, 1)
                if side_jobs:
                    side_jobs(pool)

            @block.tensor
            def _(pe):
                pe.wait_ge(zeroed, 4)
                for b in range(2):
                    down_done[b].prime(pe)
                for a in acc:
                    last = pe.matmul(a[:, :], wd_hi[1][:, 0:P], h_hi[1][:, 0:HALF], start=True,
                                     stop=False, skip_group_check=True)
                last.then_inc(opened, 1)
                with pe.Fori(0, passes, 1) as g:
                    for b in range(2):
                        def mix(c):
                            pe.wait_ge(silu_done[b], g * NC + (c + 1))
                            pe.matmul(G[c][:, :], wx_hi[b][:, 2 * NK * P:2 * NK * P + P],
                                      gate_hi[:, half(c)], start=True, stop=True).then_inc(mix_ready[b], 1)
                        pe.wait_ge(wx_hi_done[b], g + 1)
                        pe.wait_ge(wx_lo_done[b], g + 1)
                        for c in range(NC):
                            pe.wait_ge(h_done[1 - b].sem, h_done[1 - b].at(g, c + 1 if b else 0))
                            x = [(xn_hi[:, k, half(c)], xn_lo[:, k, half(c)]) for k in range(NK)]
                            three_pass(pe, G[c][:, :], [(w(wx_hi[b], 0, k), w(wx_lo[b], 0, k), *x[k])
                                                        for k in range(NK)]).then_inc(gate_ready[b], 1)
                            if routed and c:
                                mix(c - 1)
                            three_pass(pe, U[c][:, :], [(w(wx_hi[b], 1, k), w(wx_lo[b], 1, k), *x[k])
                                                        for k in range(NK)]).then_inc(up_ready[b], 1)
                        if routed:
                            mix(NC - 1)
                        pe.wait_ge(wd_lo_done[1 - b].sem, wd_lo_done[1 - b].at(g, b))
                        pe.wait_ge(h_lo_done[1 - b].sem, h_lo_done[1 - b].at(g, NC * b))
                        down(pe, 1 - b, False).then_inc(down_done[1 - b].sem, 1)
                pe.wait_ge(wd_lo_done[1].sem, wd_lo_done[1].at(passes - 1, 1))
                pe.wait_ge(h_lo_done[1].sem, h_lo_done[1].at(passes - 1, NC))
                down(pe, 1, True).then_inc(all_down, 1)

            @block.scalar
            def _(act):
                for b in range(2):
                    h_hi_done[b].prime(act)
                act.wait_ge(loaded[0], 16 * NL)
                act.activation(wx_hi[0][:, :], raw[0][:, D:cols], ACT.Copy, bias=offset)\
                   .then_inc(wx_hi_done[0], 1)
                with act.Fori(0, passes, 1) as g:
                    for b in range(2):
                        for c in range(NC):
                            act.wait_ge(gate_ready[b], g * NC + (c + 1))
                            act.wait_ge(h_done[1 - b].sem, h_done[1 - b].at(g, c + 1 if b else 0))
                            act.activation(sg[:, c, :], G[c][:, :], ACT.Silu,
                                           **({"scale": sc[b][:, 0:1]} if scales is not None else {}))\
                               .then_inc(silu_done[b], 1)
                            if c == 0:
                                act.wait_ge(down_done[b].sem, down_done[b].at(g, b))
                                act.activation(wd_hi[b][:, :], raw[b][:, 0:D], ACT.Copy, bias=offset)\
                                   .then_inc(wd_hi_done[b], 1)
                                act.wait_ge(loaded[1 - b], g * (16 * NL) + 16 * NL * (b + 1))
                                act.activation(wx_hi[1 - b][:, :], raw[1 - b][:, D:cols], ACT.Copy, bias=offset)\
                                   .then_inc(wx_hi_done[1 - b], 1)
                        for c in range(NC):
                            act.wait_ge(h_done[b].sem, h_done[b].at(g, c + 1))
                            act.activation(h_hi[b][:, half(c)], hh[:, c, :], ACT.Copy)\
                               .then_inc(h_hi_done[b].sem, 1)
                act.wait_ge(all_down, 1)
                for m in range(NK):
                    for c in range(NC):
                        act.activation(gT[:, m, half(c)], acc[m * NC + c][:, :], ACT.Silu,
                                       **({"scale": down_scale[:, m:m + 1]} if down_scale is not None else {}))\
                           .then_inc(g_done, 1)

            @block.vector
            def _(dve):
                def split_lo(lo, source, hi, count):
                    dve.scalar_tensor_tensor(lo, source, offset, f32(hi), ALU.add, ALU.subtract).then_inc(count, 1)
                for b in range(2):
                    for count in (wd_lo_done[b], h_done[b], h_lo_done[b]):
                        count.prime(dve)
                gate_up = slice(D, D + 2 * NK * P)
                dve.wait_ge(wx_hi_done[0], 1)
                split_lo(wx_lo[0][:, :], raw[0][:, gate_up], wx_hi[0][:, 0:2 * NK * P], wx_lo_done[0])
                with dve.Fori(0, passes, 1) as g:
                    for b in range(2):
                        for c in range(NC):
                            if c == NC - 1:
                                dve.wait_ge(wd_hi_done[b], g + 1)
                                split_lo(wd_lo[b][:, :], raw[b][:, 0:D], wd_hi[b][:, :], wd_lo_done[b].sem)
                                dve.wait_ge(wx_hi_done[1 - b], g + (1 + b))
                                split_lo(wx_lo[1 - b][:, :], raw[1 - b][:, gate_up],
                                         wx_hi[1 - b][:, 0:2 * NK * P], wx_lo_done[1 - b])
                            dve.wait_ge(silu_done[b], g * NC + (c + 1))
                            dve.wait_ge(up_ready[b], g * NC + (c + 1))
                            dve.wait_ge(h_hi_done[1 - b].sem, h_hi_done[1 - b].at(g, c + 1 if b else 0))
                            dve.wait_ge(h_lo_done[1 - b].sem, h_lo_done[1 - b].at(g, c + 1 if b else 0))
                            if routed:
                                dve.tensor_tensor(h1[:, c, :], U[c][:, :], sg[:, c, :], ALU.mult)\
                                   .then_inc(h1_done[b], 1)
                                dve.wait_ge(h1_done[b], g * NC + (c + 1))
                                dve.wait_ge(mix_ready[b], g * NC + (c + 1))
                                dve.tensor_tensor(hh[:, c, :], G[c][:, :], h1[:, c, :], ALU.mult)\
                                   .then_inc(h_done[b].sem, 1)
                            else:
                                dve.scalar_tensor_tensor(hh[:, c, :], U[c][:, :], sc[b][:, 1:2], sg[:, c, :],
                                                         ALU.mult, ALU.mult).then_inc(h_done[b].sem, 1)
                        for c in range(NC):
                            dve.wait_ge(h_hi_done[b].sem, h_hi_done[b].at(g, c + 1))
                            dve.tensor_tensor(h_lo[b][:, half(c)], hh[:, c, :], f32(h_hi[b][:, half(c)]),
                                              ALU.subtract).then_inc(h_lo_done[b].sem, 1)


def combine0(nc, xT, sT, gT, ident, x_tok):
    with Scope(nc) as s:
        prod = s.sb("c0_prod", [P, NK, T], F32)
        tp = [s.ps(f"c0_tp{b}", [P, HALF]) for b in range(4)]
        prod_done, x_done, tp_ready, taken = (s.sem("c0_prod_done"), s.sem("c0_x_done"),
                                              s.sem("c0_tp_ready"), s.sem("c0_taken"))
        with nc.Block() as block:

            @block.vector
            def _(dve):
                for c in range(NC):
                    sl = slice(c * HALF, c * HALF + HALF)
                    dve.tensor_tensor(prod[:, :, sl], sT[:, :, sl], gT[:, :, sl], ALU.mult)\
                       .then_inc(prod_done, 1)
                    dve.wait_ge(prod_done, c + 1)
                    dve.tensor_tensor(xT[:, :, sl], xT[:, :, sl], prod[:, :, sl], ALU.add)\
                       .then_inc(x_done, 1)

            @block.tensor
            def _(pe):
                for n in range(NT // 2):
                    pe.wait_ge(x_done, n // 2 + 1)
                    for j in range(2):
                        for k in range(NK):
                            t = 2 * n + j
                            last = pe.transpose(tp[n][:, (j * NK + k) * P:(j * NK + k) * P + P],
                                                xT[:, k, t * P:t * P + P], ident[:, :])
                    last.then_inc(tp_ready, 1)

            @block.scalar
            def _(act):
                for n in range(NT // 2):
                    act.wait_ge(tp_ready, n + 1)
                    act.activation(x_tok[:, 2 * n:2 * n + 2, :],
                                   tp[n][:, :].rearrange("p (t d) -> p t d", t=2),
                                   ACT.Copy).then_inc(taken, 1)


def route1(nc, xn_hi, xn_lo, wr, earlier, ident, gate_hi):
    E = 16
    with Scope(nc) as s:
        wr_hi = s.sb("r1_wr_hi", [P, NK, E1], F32R)
        wr_lo = s.sb("r1_wr_lo", [P, NK, E1], F32R)
        lg = s.sb("r1_lg", [E1, T], F32)
        sm = s.sb("r1_sm", [P, NT], F32)
        e = s.sb("r1_e", [P, 3, NT, E1], F32)
        cmp = s.sb("r1_cmp", [P, 3, NT, E1 * E1], F32)
        rank = s.sb("r1_rank", [P, 2, NT * E1], F32)
        wt = s.sb("r1_wt", [P, NT, E], F32)
        L = [s.ps(f"r1_L{c}", [P, HALF]) for c in range(NC)]
        LT = s.ps("r1_LT", [P, HALF])
        WT = [s.ps(f"r1_WT{c}", [P, HALF]) for c in range(NC)]
        wr_hi_done, step, act_step = s.sem("r1_wr_hi_done"), s.sem("r1_step"), s.sem("r1_act_step")
        logits_ready, lt_ready, wt_ready = s.sem("r1_logits_ready"), s.sem("r1_lt_ready"), s.sem("r1_wt_ready")
        zeroed, g_hi_done = s.sem("r1_zeroed"), s.sem("r1_g_hi_done")
        with nc.Block() as block:

            @block.gpsimd
            def _(pool):
                pool.memset(f32(gate_hi[:, :]), 0.0).then_inc(zeroed, 1)
                pool.memset(wt[:, :, E1:E1 + 1], 1.0).then_inc(zeroed, 1)
                pool.memset(wt[:, :, E1 + 1:E], 0.0).then_inc(zeroed, 1)

            @block.scalar
            def _(act):
                act.activation(wr_hi[:, :, :], wr[:, :, :], ACT.Copy).then_inc(wr_hi_done, 1)
                for c in range(NC):
                    act.wait_ge(logits_ready, c + 1)
                    act.activation(lg[:, c * HALF:c * HALF + HALF], L[c][0:E1, :], ACT.Copy)\
                       .then_inc(act_step, 1)
                act.wait_ge(step, 3)
                act.activation(e[:, 1, :, :], e[:, 0, :, :], ACT.Exp).then_inc(act_step, 1)
                act.wait_ge(zeroed, 3)
                for c in range(NC):
                    act.wait_ge(wt_ready, c + 1)
                    act.activation(gate_hi[0:E, c * HALF:c * HALF + HALF], WT[c][0:E, :], ACT.Copy)\
                       .then_inc(g_hi_done, 1)

            @block.tensor
            def _(pe):
                pe.wait_ge(step, 1)
                for c in range(NC):
                    sl = slice(c * HALF, c * HALF + HALF)
                    three_pass(pe, L[c][0:E1, :], [(wr_hi[:, k, :], wr_lo[:, k, :], xn_hi[:, k, sl],
                                                    xn_lo[:, k, sl]) for k in range(NK)])\
                        .then_inc(logits_ready, 1)
                for t in range(NT):
                    pe.wait_ge(act_step, t // 4 + 1)
                    last = pe.transpose(LT[:, t * E1:t * E1 + E1], lg[0:E1, t * P:t * P + P],
                                        ident[0:E1, 0:E1])
                last.then_inc(lt_ready, 1)
                pe.wait_ge(step, 13)
                pe.wait_ge(zeroed, 3)
                for c in range(NC):
                    for j in range(4):
                        last = pe.transpose(WT[c][0:E, j * P:j * P + P], wt[:, 4 * c + j, :], ident[:, :])
                    last.then_inc(wt_ready, 1)

            @block.vector
            def _(dve):
                def done(n):
                    dve.wait_ge(step, n)

                dve.wait_ge(wr_hi_done, 1)
                dve.tensor_tensor(wr_lo[:, :, :], wr[:, :, :], f32(wr_hi[:, :, :]), ALU.subtract)\
                   .then_inc(step, 1)
                dve.wait_ge(lt_ready, 1)
                lt = LT[:, 0:NT * E1].rearrange("p (t e) -> p t e", t=NT)
                wide = lambda v: v.unsqueeze(2).broadcast_to([P, NT, E1])
                dve.tensor_reduce(sm[:, :], lt, AX.X, ALU.max).then_inc(step, 1)
                done(2)
                dve.tensor_tensor(e[:, 0, :, :], lt, wide(sm[:, :]), ALU.subtract).then_inc(step, 1)
                dve.wait_ge(act_step, NC + 1)
                done(3)
                dve.tensor_reduce(sm[:, :], e[:, 1, :, :], AX.X, ALU.add).then_inc(step, 1)
                done(4)
                dve.reciprocal(rank[:, 0, 0:NT], sm[:, :]).then_inc(step, 1)
                done(5)
                dve.tensor_tensor(e[:, 2, :, :], e[:, 1, :, :], wide(rank[:, 0, 0:NT]), ALU.mult)\
                   .then_inc(step, 1)
                done(6)
                this = e[:, 2, :, :].unsqueeze(3).broadcast_to([P, NT, E1, E1])
                other = e[:, 2, :, :].unsqueeze(2).broadcast_to([P, NT, E1, E1])
                c4 = lambda n: cmp[:, n, :, :].rearrange("p t (a b) -> p t a b", a=E1)
                dve.tensor_tensor(c4(0), other, this, ALU.is_gt).then_inc(step, 1)
                dve.tensor_tensor(c4(1), other, this, ALU.is_equal).then_inc(step, 1)
                done(8)
                dve.tensor_tensor(cmp[:, 2, :, :], cmp[:, 1, :, :],
                                  earlier[:, :].unsqueeze(1).broadcast_to([P, NT, E1 * E1]), ALU.mult)\
                   .then_inc(step, 1)
                done(9)
                dve.tensor_tensor(cmp[:, 1, :, :], cmp[:, 0, :, :], cmp[:, 2, :, :], ALU.add)\
                   .then_inc(step, 1)
                done(10)
                dve.tensor_reduce(rank[:, 0, :].rearrange("p (t e) -> p t e", t=NT), c4(1), AX.X, ALU.add)\
                   .then_inc(step, 1)
                done(11)
                dve.tensor_scalar(rank[:, 1, :], rank[:, 0, :], float(TOPK) - 0.5, None, ALU.is_lt)\
                   .then_inc(step, 1)
                done(12)
                dve.tensor_tensor(wt[:, :, 0:E1], e[:, 2, :, :],
                                  rank[:, 1, :].rearrange("p (t e) -> p t e", t=NT), ALU.mult)\
                   .then_inc(step, 1)
                for c in range(NC):
                    sl = slice(c * HALF, c * HALF + HALF)
                    dve.wait_ge(g_hi_done, c + 1)
                    dve.tensor_tensor(gate_hi[32:32 + E, sl], WT[c][0:E, :], f32(gate_hi[0:E, sl]),
                                      ALU.subtract).then_inc(step, 1)


def attention1(nc, xn_hi, xn_lo, raw, w_hi, w_lo, w_qkv, w_out, rope_c, rope_s, ident, ident_bf, mask, acc):
    PER = NT * GH1
    PAIRS = PER // 2
    tile_of = lambda u: u // GH1
    FIRST = NT // NC * GH1
    NH = GH1 + 2
    NP = NH * NC
    RH = GH1 + 1
    QC = RH * NC
    head_of = lambda n: (GH1, *range(GH1), GH1 + 1)[n % NH]
    bank_of = lambda n: n % 4 if n < NH else 3 - 2 * (n % 2)
    chunk_at = lambda u: chunks_before(PER, tile_of)[u] + (1 if u < FIRST else NC)
    CH = chunk_at(PER)
    V_CHUNK = (0, chunk_at(FIRST) - 1)
    chunk_in_step = lambda step: NH + step // 2 if step % 2 == 0 and 0 <= step < 2 * NH else None
    RP, RX = 3, 2
    with Scope(nc) as s:
        zero = s.sb("a1_zero", [P, 1], F32)
        wo_hi = s.sb("a1_wo_hi", [P, GH1, D], F32R)
        wo_lo = s.sb("a1_wo_lo", [P, GH1, D], F32R)
        q_hi = s.sb("a1_q_hi", [P, GH1 + 1, T], F32R)
        q_lo = s.sb("a1_q_lo", [P, GH1 + 1, T], F32R)
        vT = s.sb("a1_vT", [P, T], F32)
        v_hi = s.sb("a1_v_hi", [P, T], F32R)
        v_lo = s.sb("a1_v_lo", [P, T], F32R)
        swapped = s.sb("a1_swapped", [P, 2, HALF], F32)
        t1 = s.sb("a1_t1", [P, 2, HALF], F32)
        t2 = s.sb("a1_t2", [P, 2, HALF], F32)
        rot = s.sb("a1_rot", [P, 2, HALF], F32)
        prob = s.sb("a1_prob", [P, RP, T], F32)
        p_hi = s.sb("a1_p_hi", [P, RX, NT, 2, P], F32R)
        p_lo = s.sb("a1_p_lo", [P, RX, NT, 2, P], F32R)
        o_hi = s.sb("a1_o_hi", [P, GH1, HALF], F32R)
        o_lo = s.sb("a1_o_lo", [P, GH1, HALF], F32R)
        neg_max = s.sb("a1_neg_max", [P, 8], F32)
        sums = s.sb("a1_sums", [P, 8], F32)
        rinv = s.sb("a1_rinv", [P, 8], F32)
        S = [s.ps(f"a1_S{b}", [P, 2 * HALF]) for b in range(2)]
        X = [s.ps(f"a1_X{b}", [P, HALF]) for b in range(2)]
        O = [s.ps(f"a1_O{b}", [P, HALF]) for b in range(2)]
        proj = [S[n // 2][:, (n % 2) * HALF:(n % 2) * HALF + HALF] for n in range(4)]

        loaded, w_step = s.sem("a1_loaded"), Count(s.sem("a1_w_step"), 4)
        proj_ready, swap_done, terms_done, rot_done = (Count(s.sem("a1_proj_ready"), NP), s.sem("a1_swap_done"),
                                                       s.sem("a1_terms_done"), s.sem("a1_rot_done"))
        q_hi_done, q_lo_done = s.sem("a1_q_hi_done"), s.sem("a1_q_lo_done")
        vT_done = s.sem("a1_vT_done")
        scores_ready, max_done, exp_done = s.sem("a1_scores_ready"), s.sem("a1_max_done"), s.sem("a1_exp_done")
        rinv_done, norm_done = s.sem("a1_rinv_done"), s.sem("a1_norm_done")
        x_ready, hi_done, lo_done = s.sem("a1_x_ready"), s.sem("a1_hi_done"), s.sem("a1_lo_done")
        o_ready, o_hi_done, o_lo_done = s.sem("a1_o_ready"), s.sem("a1_o_hi_done"), s.sem("a1_o_lo_done")
        y_ready, y_done = Count(s.sem("a1_y_ready"), NC * NK), Count(s.sem("a1_y_done"), NC * NK)
        zeroed = s.sem("a1_zeroed")

        with nc.Block() as block:

            @block.sync
            def _(sp):
                with sp.Fori(0, KV1, 1) as g:
                    sp.wait_ge(w_step.sem, w_step.at(g, 0))
                    sp.dma_start(raw[:, 0:GH1 * D], w_out[g, :, :]).then_inc(loaded, 16)
                    sp.wait_ge(w_step.sem, w_step.at(g, 2))
                    sp.dma_start(raw[:, :], w_qkv[g + 1, :, :]).then_inc(loaded, 16)

            @block.gpsimd
            def _(pool):
                pool.memset(acc[:, :, :], 0.0).then_inc(zeroed, 1)
                pool.memset(zero[:, :], 0.0).then_inc(zeroed, 1)
                pool.wait_ge(zeroed, 2)
                w_step.prime(pool)
                flat = lambda v: v.rearrange("p a b -> p (a b)")

                def split(hi, lo, n, done):
                    pool.tensor_tensor(hi, raw[:, 0:n], zero[:, :].broadcast_to([P, n]), ALU.add)\
                        .then_inc(w_step.sem, 1)
                    pool.wait_ge(w_step.sem, w_step.at(g, done + 1))
                    pool.tensor_tensor(lo, raw[:, 0:n], f32(hi), ALU.subtract).then_inc(w_step.sem, 1)

                with pool.Fori(0, KV1, 1) as g:
                    for r in range(QC):
                        pool.wait_ge(terms_done, g * 2 * QC + 2 * r + 2)
                        if r >= 2:
                            pool.wait_ge(q_lo_done, g * QC + (r - 1))
                        pool.tensor_tensor(rot[:, r % 2, :], t1[:, r % 2, :], t2[:, r % 2, :], ALU.add)\
                            .then_inc(rot_done, 1)
                    pool.wait_ge(loaded, g * 32 + 16)
                    pool.wait_ge(y_ready.sem, y_ready.at(g, 0))
                    split(flat(wo_hi[:, :, :]), flat(wo_lo[:, :, :]), GH1 * D, 0)
                    pool.wait_ge(loaded, g * 32 + 32)
                    pool.wait_ge(proj_ready.sem, proj_ready.at(g, NP))
                    split(flat(w_hi[:, :, :]), flat(w_lo[:, :, :]), GWCOLS1, 2)

            @block.tensor
            def _(pe):
                proj_ready.prime(pe)
                y_ready.prime(pe)

                def project(n):
                    m, sl = head_of(n), slice(n // NH * HALF, n // NH * HALF + HALF)
                    three_pass(pe, proj[bank_of(n)],
                               [(w_hi[:, k, m * P:m * P + P], w_lo[:, k, m * P:m * P + P],
                                 xn_hi[:, k, sl], xn_lo[:, k, sl]) for k in range(NK)])\
                        .then_inc(proj_ready.sem, 1)

                def transpose_v(c):
                    pe.wait_ge(vT_done, g * NC + (c + 1))
                    if c:
                        pe.wait_ge(lo_done, g * CH + (V_CHUNK[c] - 1))
                    for j in range(4):
                        t = 4 * c + j
                        last = pe.transpose(X[V_CHUNK[c] % 2][:, j * P:j * P + P], vT[:, t * P:t * P + P],
                                            ident[:, :])
                    last.then_inc(x_ready, 1)

                with pe.Fori(0, KV1, 1) as g:
                    pe.wait_ge(w_step.sem, w_step.at(g, 0))
                    for n in range(NH):
                        if n >= 4:
                            pe.wait_ge(terms_done, g * 2 * QC + 2 * (n - 4) + 1)
                        project(n)
                    pe.wait_ge(q_lo_done, g * QC + RH)
                    for step in range(PER + 6):
                        if step < PER:
                            u = step
                            i, h = tile_of(u), u % GH1
                            n, rows = (i + 1) * P, slice(i * P, i * P + P)
                            if u >= 2:
                                pe.wait_ge(exp_done, g * PER + (u - 1))
                            if u == FIRST:
                                pe.wait_ge(q_lo_done, g * QC + QC)
                                pe.wait_ge(vT_done, g * NC + NC)
                            for a in range(0, n, HALF):
                                e = min(a + HALF, n)
                                three_pass(pe, S[u % 2][:, a:e],
                                           [(q_hi[:, h, rows], q_lo[:, h, rows],
                                             q_hi[:, GH1, a:e], q_lo[:, GH1, a:e])], stop=e != n)
                            pe.matmul(S[u % 2][:, n - P:n], ident_bf[:, :], mask[:, :], start=False,
                                      stop=True).then_inc(scores_ready, 1)
                        if step == 0:
                            transpose_v(0)
                        if step == FIRST + 3:
                            transpose_v(1)
                        if 3 <= step < PER + 3:
                            u = step - 3
                            i = tile_of(u)
                            pe.wait_ge(norm_done, g * PER + (u + 1))
                            for c in range(chunks_of(i)):
                                m = chunk_at(u) + c
                                if m >= 2:
                                    pe.wait_ge(lo_done, g * CH + (m - 1))
                                for j in range(4 * c, min(4 * c + 4, i + 1)):
                                    last = pe.transpose(X[m % 2][:, (j % 4) * P:(j % 4) * P + P],
                                                        prob[:, u % RP, j * P:j * P + P], ident[:, :])
                                last.then_inc(x_ready, 1)
                        if step in (21, 37):
                            c = step // 16 - 1
                            pe.wait_ge(o_lo_done, g * PAIRS + 8 * (c + 1))
                            pe.wait_ge(w_step.sem, w_step.at(g, 2))
                            for m in range(NK):
                                three_pass(pe, O[m][:, :],
                                           [(wo_hi[:, h, m * P:m * P + P], wo_lo[:, h, m * P:m * P + P],
                                             o_hi[:, h, :], o_lo[:, h, :]) for h in range(GH1)])\
                                    .then_inc(y_ready.sem, 1)
                        if 5 <= step < PER + 5 and step % 2 == 1:
                            p = (step - 5) // 2
                            i = tile_of(2 * p)
                            pe.wait_ge(lo_done, g * CH + chunk_at(2 * p + 1) + chunks_of(i))
                            if p % 8 >= 2:
                                pe.wait_ge(o_lo_done, g * PAIRS + (p - 1))
                            else:
                                pe.wait_ge(y_done.sem, y_done.at(g, (p % 8 + 1 if p >= 8 else 0)))
                            three_pass(pe, O[p % 2][:, 0:2 * P],
                                       [(v_hi[:, j * P:j * P + P], v_lo[:, j * P:j * P + P],
                                         p_hi[:, p % RX, j].rearrange("p h c -> p (h c)"),
                                         p_lo[:, p % RX, j].rearrange("p h c -> p (h c)"))
                                        for j in range(i + 1)]).then_inc(o_ready, 1)
                        n = chunk_in_step(step)
                        if n is not None:
                            if n == NH + 1:
                                pe.wait_ge(vT_done, g * NC + 1)
                            if n >= NH + 2:
                                r = n - 2 - n // NH
                                pe.wait_ge(terms_done, g * 2 * QC + 2 * r + 1)
                            project(n)

            @block.scalar
            def _(act):
                def exchange(n):
                    act.wait_ge(proj_ready.sem, proj_ready.at(g, n + 1))
                    c, r = n // NH, n - n // NH
                    if head_of(n) > GH1:
                        act.activation(vT[:, c * HALF:c * HALF + HALF], proj[bank_of(n)], ACT.Copy)\
                           .then_inc(vT_done, 1)
                        return
                    if r >= 2:
                        act.wait_ge(terms_done, g * 2 * QC + 2 * (r - 2) + 2)
                    for e in range(2):
                        act.activation(swapped[64 * e:64 * e + 64, r % 2, :],
                                       proj[bank_of(n)][64 - 64 * e:128 - 64 * e, :], ACT.Copy)\
                           .then_inc(swap_done, 1)

                def q_high(n):
                    m, c, r = head_of(n), n // NH, n - n // NH
                    if m > GH1:
                        return
                    act.wait_ge(rot_done, g * QC + (r + 1))
                    act.activation(q_hi[:, m, c * HALF:c * HALF + HALF], rot[:, r % 2, :],
                                   ACT.Copy, scale=SCALE1 if m < GH1 else 1.0).then_inc(q_hi_done, 1)

                def v_high(c):
                    act.wait_ge(x_ready, g * CH + (V_CHUNK[c] + 1))
                    act.activation(v_hi[:, c * HALF:c * HALF + HALF], X[V_CHUNK[c] % 2][:, :], ACT.Copy)\
                       .then_inc(hi_done, 1)

                with act.Fori(0, KV1, 1) as g:
                    for n in range(NH + 1):
                        if n < NH:
                            exchange(n)
                        if n >= 1:
                            q_high(n - 1)
                    for step in range(PER + 5):
                        if step == 1:
                            v_high(0)
                        if step == FIRST + 3:
                            v_high(1)
                        if 1 <= step < PER + 1:
                            u = step - 1
                            n = (tile_of(u) + 1) * P
                            act.wait_ge(max_done, g * PER + (u + 1))
                            if u >= RP:
                                act.wait_ge(x_ready, g * CH + chunk_at(u - RP) + chunks_of(tile_of(u - RP)))
                            act.activation(prob[:, u % RP, 0:n], S[u % 2][:, 0:n], ACT.Exp,
                                           bias=neg_max[:, u % 8:u % 8 + 1],
                                           accum_out=sums[:, u % 8:u % 8 + 1]).then_inc(exp_done, 1)
                        if 3 <= step < PER + 3:
                            u = step - 3
                            i, p = tile_of(u), u // 2
                            if p >= RX:
                                act.wait_ge(o_ready, g * PAIRS + (p - RX + 1))
                            for c in range(chunks_of(i)):
                                m = chunk_at(u) + c
                                js = slice(4 * c, min(4 * c + 4, i + 1))
                                act.wait_ge(x_ready, g * CH + (m + 1))
                                act.activation(p_hi[:, p % RX, js, u % 2, :],
                                               X[m % 2][:, 0:(js.stop - js.start) * P]
                                               .rearrange("p (a c) -> p a c", c=P),
                                               ACT.Copy).then_inc(hi_done, 1)
                        if 2 <= step < PER + 2:
                            u = step - 2
                            n = (tile_of(u) + 1) * P
                            act.wait_ge(rinv_done, g * PER + (u + 1))
                            act.activation(prob[:, u % RP, 0:n], prob[:, u % RP, 0:n], ACT.Copy,
                                           scale=rinv[:, u % 8:u % 8 + 1]).then_inc(norm_done, 1)
                        if step >= 6 and step % 2 == 0:
                            p = (step - 6) // 2
                            i, h = tile_of(2 * p), 2 * p % GH1
                            act.wait_ge(o_ready, g * PAIRS + (p + 1))
                            if p % 8 == 0:
                                act.wait_ge(y_ready.sem, y_ready.at(g, (NK if p else 0)))
                            act.activation(o_hi[:, h:h + 2, (i % 4) * P:(i % 4) * P + P],
                                           O[p % 2][:, 0:2 * P].rearrange("p (h c) -> p h c", h=2),
                                           ACT.Copy).then_inc(o_hi_done, 1)
                        if chunk_in_step(step - 1) is not None:
                            exchange(chunk_in_step(step - 1))
                        if chunk_in_step(step - 2) is not None:
                            q_high(chunk_in_step(step - 2))

            @block.vector
            def _(dve):
                dve.wait_ge(zeroed, 2)
                y_done.prime(dve)
                def rope_terms(n):
                    m, c, r = head_of(n), n // NH, n - n // NH
                    if m > GH1:
                        return
                    sl, b = slice(c * HALF, c * HALF + HALF), r % 2
                    dve.wait_ge(swap_done, g * 2 * QC + 2 * r + 2)
                    if r >= 2:
                        dve.wait_ge(rot_done, g * QC + (r - 1))
                    dve.tensor_tensor(t1[:, b, :], proj[bank_of(n)], rope_c[:, sl], ALU.mult)\
                       .then_inc(terms_done, 1)
                    dve.tensor_tensor(t2[:, b, :], swapped[:, b, :], rope_s[:, sl], ALU.mult)\
                       .then_inc(terms_done, 1)

                def q_low(n):
                    m, c, r = head_of(n), n // NH, n - n // NH
                    if m > GH1:
                        return
                    sl = slice(c * HALF, c * HALF + HALF)
                    dve.wait_ge(q_hi_done, g * QC + (r + 1))
                    dve.scalar_tensor_tensor(q_lo[:, m, sl], rot[:, r % 2, :],
                                             SCALE1 if m < GH1 else 1.0, f32(q_hi[:, m, sl]),
                                             ALU.mult, ALU.subtract).then_inc(q_lo_done, 1)

                def v_low(c):
                    sl = slice(c * HALF, c * HALF + HALF)
                    dve.wait_ge(hi_done, g * CH + (V_CHUNK[c] + 1))
                    dve.tensor_tensor(v_lo[:, sl], X[V_CHUNK[c] % 2][:, :], f32(v_hi[:, sl]), ALU.subtract)\
                       .then_inc(lo_done, 1)

                with dve.Fori(0, KV1, 1) as g:
                    for n in range(NH + 1):
                        if n < NH:
                            rope_terms(n)
                        if n >= 1:
                            q_low(n - 1)
                    for step in range(PER + 6):
                        if 2 <= step < PER + 2:
                            u = step - 2
                            dve.wait_ge(exp_done, g * PER + (u + 1))
                            dve.reciprocal(rinv[:, u % 8:u % 8 + 1], sums[:, u % 8:u % 8 + 1])\
                               .then_inc(rinv_done, 1)
                        if step < PER:
                            u = step
                            n = (tile_of(u) + 1) * P
                            dve.wait_ge(scores_ready, g * PER + (u + 1))
                            dve.tensor_reduce(neg_max[:, u % 8:u % 8 + 1], S[u % 2][:, 0:n], AX.X,
                                              ALU.max, negate=True).then_inc(max_done, 1)
                        if step == 1:
                            v_low(0)
                        if step == FIRST + 3:
                            v_low(1)
                        if 3 <= step < PER + 3:
                            u = step - 3
                            i, p = tile_of(u), u // 2
                            for c in range(chunks_of(i)):
                                m = chunk_at(u) + c
                                js = slice(4 * c, min(4 * c + 4, i + 1))
                                dve.wait_ge(hi_done, g * CH + (m + 1))
                                dve.tensor_tensor(p_lo[:, p % RX, js, u % 2, :],
                                                  X[m % 2][:, 0:(js.stop - js.start) * P]
                                                  .rearrange("p (a c) -> p a c", c=P),
                                                  f32(p_hi[:, p % RX, js, u % 2, :]),
                                                  ALU.subtract).then_inc(lo_done, 1)
                        if 6 <= step < PER + 5 and step % 2 == 0:
                            p = (step - 6) // 2
                            i, h = tile_of(2 * p), 2 * p % GH1
                            sl = slice((i % 4) * P, (i % 4) * P + P)
                            dve.wait_ge(o_hi_done, g * PAIRS + (p + 1))
                            dve.tensor_tensor(o_lo[:, h:h + 2, sl],
                                              O[p % 2][:, 0:2 * P].rearrange("p (h c) -> p h c", h=2),
                                              f32(o_hi[:, h:h + 2, sl]), ALU.subtract).then_inc(o_lo_done, 1)
                        if chunk_in_step(step - 1) is not None:
                            rope_terms(chunk_in_step(step - 1))
                        if chunk_in_step(step - 2) is not None:
                            q_low(chunk_in_step(step - 2))
                        if step in (21, 37):
                            c = step // 16 - 1
                            for m in range(NK):
                                at = acc[:, m, c * HALF:c * HALF + HALF]
                                dve.wait_ge(y_ready.sem, y_ready.at(g, c * NK + m + 1))
                                dve.wait_ge(y_done.sem, y_done.at(g, c * NK + m))
                                dve.tensor_tensor(at, O[m][:, :], at, ALU.add).then_inc(y_done.sem, 1)


def combine1(nc, xT, sT, gT, out):
    with Scope(nc) as s:
        prod = s.sb("c1_prod", [P, NK, T], F32)
        res = s.sb("c1_res", [P, NK, T], F32)
        prod_done, res_done, stored = s.sem("c1_prod_done"), s.sem("c1_res_done"), s.sem("c1_stored")
        with nc.Block() as block:

            @block.vector
            def _(dve):
                for k in range(NK):
                    dve.tensor_tensor(prod[:, k, :], sT[:, k, :], gT[:, k, :], ALU.mult)\
                       .then_inc(prod_done, 1)
                    dve.wait_ge(prod_done, k + 1)
                    dve.tensor_tensor(res[:, k, :], xT[:, k, :], prod[:, k, :], ALU.add)\
                       .then_inc(res_done, 1)

            @block.sync
            def _(sp):
                for k in range(NK):
                    sp.wait_ge(res_done, k + 1)
                    sp.dma_start(out[k, :, :], res[:, k, :]).then_inc(stored, 16)
                sp.wait_ge(stored, 16 * NK)


def build(nc, a):
    with Scope(nc) as s:
        ident = s.sb("ident", [P, P], F32)
        ident_bf = s.sb("ident_bf", [P, P], BF16)
        mask = s.sb("mask", [P, P], BF16)
        xT = s.sb("xT", [P, NK, T], F32)
        xn_hi = s.sb("xn_hi", [P, NK, T], F32R)
        xn_lo = s.sb("xn_lo", [P, NK, T], F32R)
        sT = s.sb("sT", [P, NK, T], F32)
        bo = s.sb("bo", [P, NK], F32)
        s_down = s.sb("s_down", [P, NK], F32)
        wr = s.sb("wr", [P, NK, E1], F32)
        earlier = s.sb("earlier", [P, E1 * E1], F32)
        wo_hi = s.sb("wo_hi", [P, NK, D], F32R)
        wo_lo = s.sb("wo_lo", [P, NK, D], F32R)
        split = s.sem("w0_split")

        with Scope(nc) as s0:
            qT = s0.sb("qT", [P, H0 // 2, T], F32R)
            kT = s0.sb("kT", [P, H0 // 2, T], F32R)
            v3 = s0.sb("v3", [P, NT, H0, PARTS0, DH0], BF16)
            with Scope(nc) as s1:
                x_tok = s1.sb("x_tok", [P, NT, D], F32)
                w0 = s1.sb("w0", [P, NK, 3 * D], F32)
                w0_hi = s1.sb("w0_hi", [P, NK, 3 * D], F32R)
                w0_lo = s1.sb("w0_lo", [P, NK, 3 * D], F32R)
                wo = s1.sb("wo", [P, NK, D], F32)
                bias = s1.sb("bias", [P, 3 * D], F32)
                mask_f32 = s1.sb("mask_f32", [P, P], F32)
                rope_c = s1.sb("rope0_c", [P, NT, 2, DH0], F32)
                rope_s = s1.sb("rope0_s", [P, NT, 2, DH0], F32)
                loads = [(x_tok[:, :, :], a["x_tok"]), (ident[:, :], a["ident"]), (w0[:, :, :], a["w0"]),
                         (xT[:, :, :], a["xT"]), (wo[:, :, :], a["wo0"]),
                         (bias[:, :], a["bias0"].partition_broadcast(P)),
                         (rope_c[:, :, :, :], a["rope0_c"]), (rope_s[:, :, :, :], a["rope0_s"]),
                         (bo[:, :], a["bo"]), (s_down[:, :], a["s_down"]), (wr[:, :, :], a["wr"]),
                         (earlier[:, :], a["earlier"])]
                loads += [(mask_f32[:, :], a["mask"])]

                def split_weights(pool, loaded):
                    pool.wait_ge(loaded, 16 * len(loads))
                    pool.tensor_copy(mask[:, :], mask_f32[:, :]).then_inc(split, 1)
                    pool.tensor_copy(ident_bf[:, :], ident[:, :]).then_inc(split, 1)
                    n = 2
                    for src, hi, lo in ((w0, w0_hi, w0_lo), (wo, wo_hi, wo_lo)):
                        pool.tensor_copy(hi[:, :, :], src[:, :, :]).then_inc(split, 1)
                        n += 1
                        pool.wait_ge(split, n)
                        pool.tensor_tensor(lo[:, :, :], src[:, :, :], f32(hi[:, :, :]),
                                           ALU.subtract).then_inc(split, 1)
                        n += 1
                layer_norm(nc, "l0_", x_tok, xn_hi, xn_lo, ident, loads, split_weights)
                project0(nc, xn_hi, xn_lo, w0_hi, w0_lo, bias, rope_c, rope_s, ident, qT, kT, v3)
            att = s0.sb("att", [P, NT, D], F32)
            attention0(nc, qT, kT, v3, ident, ident_bf, mask, att)
            project_out0(nc, att, wo_hi, wo_lo, bo, ident, sT)
        gT = s.sb("gT", [P, NK, T], F32)
        gated_ffn(nc, "f0", FT0, a["wf0"], WCOLS, -ZERO_POINT, a["sf0"], s_down, xn_hi, xn_lo, None, gT)
        with Scope(nc) as s1:
            x_tok = s1.sb("x1_tok", [P, NT, D], F32)
            combine0(nc, xT, sT, gT, ident, x_tok)
            layer_norm(nc, "l1_", x_tok, xn_hi, xn_lo, ident, [])
        with Scope(nc) as s1:
            raw = s1.sb("wqkv_raw", [P, GWCOLS1], F32)
            w_hi = s1.sb("wqkv_hi", [P, NK, (GH1 + 2) * P], F32R)
            w_lo = s1.sb("wqkv_lo", [P, NK, (GH1 + 2) * P], F32R)
            rope_c = s1.sb("rope1_c", [P, T], F32)
            rope_s = s1.sb("rope1_s", [P, T], F32)
            wqkv_loaded, wqkv_split = s1.sem("wqkv_loaded"), s1.sem("wqkv_split")

            def load_first_head(sp):
                sp.dma_start(raw[:, :], a["wqkv1"][0, :, :]).then_inc(wqkv_loaded, 16)
                sp.dma_start(rope_c[:, :], a["rope1_c"]).then_inc(wqkv_loaded, 16)
                sp.dma_start(rope_s[:, :], a["rope1_s"]).then_inc(wqkv_loaded, 16)

            def split_first_head(pool):
                flat = lambda v: v.rearrange("p a b -> p (a b)")
                pool.wait_ge(wqkv_loaded, 48)
                pool.tensor_copy(flat(w_hi[:, :, :]), raw[:, :]).then_inc(wqkv_split, 1)
                pool.wait_ge(wqkv_split, 1)
                pool.tensor_tensor(flat(w_lo[:, :, :]), raw[:, :], f32(flat(w_hi[:, :, :])),
                                   ALU.subtract).then_inc(wqkv_split, 1)
            with Scope(nc) as s2:
                gate_hi = s2.sb("gate_hi", [P, T], F32R)
                route1(nc, xn_hi, xn_lo, wr, earlier, ident, gate_hi)
                gated_ffn(nc, "f1", FT1, a["wf1"], WCOLS + P, 0.0, None, None, xn_hi, xn_lo, gate_hi, gT,
                          load_first_head, split_first_head)
            attention1(nc, xn_hi, xn_lo, raw, w_hi, w_lo, a["wqkv1"], a["wo1"], rope_c, rope_s,
                       ident, ident_bf, mask, sT)
        combine1(nc, xT, sT, gT, a["out"])


def _constants():
    f = np.float32
    c = {"ident": np.eye(P, dtype=f), "mask": np.triu(np.full((P, P), MASKED, f), 1)}
    pos = np.arange(T, dtype=f)

    def tables(base, half):
        inv = f(1.0) / f(base) ** (np.arange(half, dtype=f) / f(half))
        ang = (pos[:, None] * inv[None, :]).astype(f)
        return np.cos(ang.astype(np.float64)).astype(f), np.sin(ang.astype(np.float64)).astype(f)
    cos, sin = tables(10000.0, DH0 // 2)
    c0 = np.repeat(cos, 2, 1)
    s0 = np.stack([-sin, sin], -1).reshape(T, DH0)
    for name, tab in (("rope0_c", c0), ("rope0_s", s0)):
        both = np.stack([tab * f(SCALE0), tab], 1)
        c[name] = np.ascontiguousarray(both.reshape(NT, P, 2, DH0).transpose(1, 0, 2, 3)).astype(f)
    cos, sin = tables(10000.0, DH1 // 2)
    c["rope1_c"] = np.ascontiguousarray(np.concatenate([cos, cos], 1).T)
    c["rope1_s"] = np.ascontiguousarray(np.concatenate([-sin, sin], 1).T)
    b, e = np.meshgrid(np.arange(E1), np.arange(E1))
    c["earlier"] = np.broadcast_to((b < e).astype(f).reshape(1, -1), (P, E1 * E1)).copy()
    sel = np.zeros((FT1 + 1, P, P), f)
    for tile in range(FT1):
        for j in range(P):
            row = tile * P + j
            x = row // F1 if row < E1 * F1 else E1
            sel[tile, x, j] = sel[tile, 32 + x, j] = 1.0
    return c, sel


def _rows(w):
    return np.ascontiguousarray(w.reshape(w.shape[0] // P, P, w.shape[1]).transpose(1, 0, 2))


def _ffn_tiles(wg, wu, wd, tiles):
    def pad(w):
        out = np.zeros(((tiles + 1) * P, D), w.dtype)
        out[:w.shape[0]] = w
        return out.reshape(tiles + 1, P, D)
    def up(w):
        return pad(w).reshape(tiles + 1, P, NK, P).transpose(0, 3, 2, 1).reshape(tiles + 1, P, NK * P)
    return np.ascontiguousarray(np.concatenate([pad(wd.T), up(wg), up(wu)], 2))


def kernel(**inputs):
    import concourse.bacc as _bacc
    from concourse.bass_utils import run_bass_kernel_spmd as _run
    x = {k: np.asarray(v) for k, v in inputs.items()}
    arrays, sel = _constants()
    x0 = x["L0_attn_x"].reshape(T, D)
    arrays["x_tok"] = np.ascontiguousarray(x0.reshape(NT, P, D).transpose(1, 0, 2))
    arrays["xT"] = _rows(x0.T)
    arrays["w0"] = _rows(np.concatenate([x["L0_attn_Wq"].T, x["L0_attn_Wk"].T, x["L0_attn_Wv"].T], 1))
    arrays["wo0"] = _rows(x["L0_attn_Wo"].T)
    arrays["bias0"] = np.concatenate([x["L0_attn_bq"], x["L0_attn_bk"], x["L0_attn_bv"]])
    arrays["bo"] = np.ascontiguousarray(x["L0_attn_bo"].reshape(NK, P).T)
    arrays["s_down"] = np.ascontiguousarray(x["L0_ffn_s_down"].reshape(NK, P).T)
    arrays["wf0"] = _ffn_tiles(x["L0_ffn_wq_gate"], x["L0_ffn_wq_up"], x["L0_ffn_wq_down"], FT0)
    sf = np.zeros((2, (FT0 + 1) * P), np.float32)
    sf[0, :HID0], sf[1, :HID0] = x["L0_ffn_s_gate"], x["L0_ffn_s_up"]
    arrays["sf0"] = np.ascontiguousarray(sf.reshape(2, FT0 + 1, P).transpose(1, 2, 0))
    arrays["wr"] = _rows(x["L1_ffn_Wr"].T)
    wg = np.concatenate([x["L1_ffn_Wg"].reshape(E1 * F1, D), x["L1_ffn_Wsg"]])
    wu = np.concatenate([x["L1_ffn_Wu"].reshape(E1 * F1, D), x["L1_ffn_Wsu"]])
    wd = np.concatenate([x["L1_ffn_Wd"].transpose(1, 0, 2).reshape(D, E1 * F1), x["L1_ffn_Wsd"]], 1)
    arrays["wf1"] = np.concatenate([_ffn_tiles(wg, wu, wd, FT1), sel], 2)
    q = x["L1_attn_Wq"].reshape(NK, P, KV1, GH1 * DH1)
    k = x["L1_attn_Wk"].reshape(NK, P, KV1, DH1)
    v = x["L1_attn_Wv"].reshape(NK, P, KV1, DH1)
    arrays["wqkv1"] = np.zeros((KV1 + 1, P, GWCOLS1), q.dtype)
    arrays["wqkv1"][:KV1] = np.concatenate([q, k, v], 3).transpose(2, 1, 0, 3).reshape(KV1, P, GWCOLS1)
    arrays["wo1"] = np.ascontiguousarray(
        x["L1_attn_Wo"].reshape(KV1, GH1, P, D).transpose(0, 2, 1, 3).reshape(KV1, P, GH1 * D))

    nc = _bacc.Bacc("TRN2", target_bir_lowering=False, num_devices=1)
    a = {n: nc.dram_tensor(f"in_{n}", v.shape, mybir.dt.from_np(v.dtype), kind="ExternalInput").ap()
         for n, v in arrays.items()}
    a["out"] = nc.dram_tensor("out_x", (NK, P, T), F32, kind="ExternalOutput").ap()
    build(nc, a)
    r = _run(nc, [{f"in_{n}": v for n, v in arrays.items()}], core_ids=[0])
    out = np.asarray(r.results[0]["out_x"])
    return np.ascontiguousarray(out.reshape(D, T).T).reshape(1, T, D)
```

```python
from contextlib import ExitStack

import numpy as np

import concourse.bass as bass
from concourse import mybir

F32, F32R = mybir.dt.float32, mybir.dt.float32r
F16, BF16, I32 = mybir.dt.float16, mybir.dt.bfloat16, mybir.dt.int32
ALU = mybir.AluOpType
ACT = mybir.ActivationFunctionType
AX = mybir.AxisListType

P = 128
T = 1024
D = 256
NT = T // P
NK = D // P
HALF = 512
NC = T // HALF
EPS = 1e-5
MASKED = -3.0e38

H0, DH0 = 16, 16
GROUPS0, GH0 = 4, 4
PARTS0 = 3
VW0 = PARTS0 * DH0
SCALE0 = DH0 ** -0.5
FT0, HID0 = 6, 704

KV1, GH1, DH1 = 4, 4, 128
SCALE1 = DH1 ** -0.5
E1, F1, FS1 = 8, 176, 352
FT1 = (E1 * F1 + 384) // P
TOPK = 2
ZERO_POINT = 128.0
WCOLS = 2 * NK * P + D
GWCOLS1 = NK * (GH1 * P + P + P)


def chunks_of(i):
    return (i * P + P + HALF - 1) // HALF


def chunks_before(units, tile_of):
    before = [0]
    for u in range(units):
        before.append(before[-1] + chunks_of(tile_of(u)))
    return before


class Scope:

    def __init__(self, nc, tag=""):
        self.nc, self.tag, self.stack = nc, tag, ExitStack()

    def __enter__(self):
        self.stack.__enter__()
        return self

    def __exit__(self, *a):
        return self.stack.__exit__(*a)

    def sb(self, name, shape, dt):
        return self.stack.enter_context(self.nc.sbuf_tensor(self.tag + name, shape, dt))

    def ps(self, name, shape, dt=F32):
        return self.stack.enter_context(self.nc.psum_tensor(self.tag + name, shape, dt))

    def sem(self, name):
        return self.stack.enter_context(self.nc.semaphore(self.tag + name))


class Count:

    def __init__(self, sem, per):
        self.sem, self.per = sem, per

    def prime(self, eng):
        eng.sem_inc(self.sem, self.per)

    def at(self, g, n):
        return g * self.per + (self.per + n)


def f32(ap):
    return ap.bitcast(F32)


def three_pass(pe, out, terms, start=True, stop=True, check=True):
    n, last = 0, None
    for a_hi, a_lo, b_hi, b_lo in terms:
        for a, b in ((a_hi, b_hi), (a_hi, b_lo), (a_lo, b_hi)):
            last = pe.matmul(out, a, b, start=start and n == 0,
                             stop=stop and n == 3 * len(terms) - 1, skip_group_check=not check)
            n += 1
    return last


def layer_norm(nc, tag, x_tok, xn_hi, xn_lo, ident, loads=(), act_jobs=None, pool_jobs=None):
    with Scope(nc, tag) as s:
        xn = s.sb("xn_tok", [P, NT, D], F32)
        stats = s.sb("ln_stats", [P, NT, 6], F32)
        mv = s.sb("ln_mv", [P, NT, 2], F32)
        ve = s.sb("ln_ve", [P, NT], F32)
        sd = s.sb("ln_sd", [P, NT], F32)
        y = s.sb("ln_y", [P, 3, NT], F32)
        rstd = s.sb("ln_rstd", [P, NT], F32)
        xT = [s.ps(f"ln_xT{k}", [P, T]) for k in range(NK)]
        stats_done, small_done = s.sem("ln_stats_done"), s.sem("ln_small_done")
        sd_done, norm_done = s.sem("ln_sd_done"), s.sem("ln_norm_done")
        xT_ready, hi_done, lo_done = s.sem("ln_xT_ready"), s.sem("ln_hi_done"), s.sem("ln_lo_done")
        with nc.Block() as block:

            @block.sync
            def _(sp):
                for sem, group in loads:
                    for out, src in group:
                        sp.dma_start(out, src).then_inc(sem, 16)
                for sem, group in loads:
                    sp.wait_ge(sem, 16 * len(group))

            if pool_jobs:
                @block.gpsimd
                def _(pool):
                    pool_jobs(pool)

            @block.vector
            def _(dve):
                if loads:
                    dve.wait_ge(loads[0][0], 16 * len(loads[0][1]))
                for t in range(NT):
                    dve.bn_stats(stats[:, t, :], x_tok[:, t, :]).then_inc(stats_done, 1)
                for t in range(NT):
                    dve.wait_ge(stats_done, t + 1)
                    dve.bn_aggr(mv[:, t, :], stats[:, t, :]).then_inc(stats_done, 1)
                dve.wait_ge(stats_done, 2 * NT)
                dve.tensor_scalar(ve[:, :], mv[:, :, 1], EPS, None, ALU.add).then_inc(small_done, 1)
                dve.wait_ge(sd_done, 1)
                dve.reciprocal(y[:, 0, :], sd[:, :]).then_inc(small_done, 1)
                dve.wait_ge(small_done, 2)
                dve.tensor_tensor(y[:, 1, :], y[:, 0, :], y[:, 0, :], ALU.mult).then_inc(small_done, 1)
                dve.wait_ge(small_done, 3)
                dve.tensor_tensor(y[:, 2, :], y[:, 1, :], ve[:, :], ALU.mult).then_inc(small_done, 1)
                dve.wait_ge(small_done, 4)
                dve.tensor_scalar(y[:, 1, :], y[:, 2, :], -0.5, 1.5, ALU.mult, ALU.add)\
                   .then_inc(small_done, 1)
                dve.wait_ge(small_done, 5)
                dve.tensor_tensor(rstd[:, :], y[:, 0, :], y[:, 1, :], ALU.mult).then_inc(small_done, 1)
                dve.wait_ge(small_done, 6)
                for t in range(NT):
                    dve.tensor_scalar(xn[:, t, :], x_tok[:, t, :], mv[:, t, 0:1], rstd[:, t:t + 1],
                                      ALU.subtract, ALU.mult).then_inc(norm_done, 1)
                n = 0
                for c in range(NC):
                    for k in range(NK):
                        n += 1
                        sl = slice(c * HALF, c * HALF + HALF)
                        dve.wait_ge(hi_done, n)
                        dve.tensor_tensor(xn_lo[:, k, sl], xT[k][:, sl], f32(xn_hi[:, k, sl]),
                                          ALU.subtract).then_inc(lo_done, 1)

            @block.tensor
            def _(pe):
                if loads:
                    pe.wait_ge(loads[1][0], 16 * len(loads[1][1]))
                for t in range(NT):
                    pe.wait_ge(norm_done, t + 1)
                    for k in range(NK):
                        last = pe.transpose(xT[k][:, t * P:t * P + P], xn[:, t, k * P:k * P + P],
                                            ident[:, :])
                    last.then_inc(xT_ready, 1)

            @block.scalar
            def _(act):
                act.wait_ge(small_done, 1)
                act.activation(sd[:, :], ve[:, :], ACT.Sqrt).then_inc(sd_done, 1)
                if act_jobs:
                    act_jobs(act)
                for c in range(NC):
                    for k in range(NK):
                        sl = slice(c * HALF, c * HALF + HALF)
                        act.wait_ge(xT_ready, (c + 1) * NT // NC)
                        act.activation(xn_hi[:, k, sl], xT[k][:, sl], ACT.Copy).then_inc(hi_done, 1)


def project0(nc, xn_hi, xn_lo, w_hi, w_lo, bias, rope_c, rope_s, ident, qT, kT, v3):
    QK = 2 * H0 * DH0
    with Scope(nc) as s:
        qkv = s.sb("p0_qkv", [P, 2, 3 * D], F32)
        t1 = s.sb("p0_t1", [P, QK], F32)
        t2 = s.sb("p0_t2", [P, QK], F32)
        rot = s.sb("p0_rot", [P, 2, QK], F32)
        zq = s.sb("p0_zq", [P, 2, H0, 4, DH0], F32R)
        zk = s.sb("p0_zk", [P, 2, H0, 4, DH0], F32R)
        vr = s.sb("p0_vr", [P, 2, D], F32)
        proj = [s.ps(f"p0_proj{i}", [P, 2 * HALF]) for i in range(2)]
        tp = [s.ps(f"p0_tp{i}", [P, HALF]) for i in range(4)]
        proj_ready, qkv_done, terms_done = s.sem("p0_proj_ready"), s.sem("p0_qkv_done"), s.sem("p0_terms_done")
        rot_done, z_hi_done, z_lo_done = s.sem("p0_rot_done"), s.sem("p0_z_hi_done"), s.sem("p0_z_lo_done")
        tp_ready, tp_taken = s.sem("p0_tp_ready"), s.sem("p0_tp_taken")
        v_part, v_rest = s.sem("p0_v_part"), s.sem("p0_v_rest")

        def pairs(z):
            return z.rearrange("p h r d -> p (h r d)").rearrange("p (a c) -> p a c", c=P)

        def rotated(t, a):
            return rot[:, t % 2, a * D:a * D + D].rearrange("p (h d) -> p h d", h=H0)\
                .unsqueeze(2).broadcast_to([P, H0, 2, DH0])

        def halves(t, a):
            z = (zq, zk)[a][:, t % 2]
            return (z[:, :, 0:2, :], z[:, :, 2:4, :]) if a == 0 else (z[:, :, 0::2, :], z[:, :, 1::2, :])

        def v_of(t):
            return qkv[:, t % 2, QK:3 * D].rearrange("p (h d) -> p h d", h=H0)

        def left(t):
            return vr[:, t % 2, :].rearrange("p (h d) -> p h d", h=H0)

        with nc.Block() as block:

            @block.tensor
            def _(pe):
                for t in range(NT + 2):
                    if t < NT:
                        if t >= 2:
                            pe.wait_ge(qkv_done, t - 1)
                        tok = slice(t * P, t * P + P)
                        for a, b in ((0, HALF), (HALF, 3 * D)):
                            last = three_pass(pe, proj[t % 2][:, a:b],
                                              [(xn_hi[:, k, tok], xn_lo[:, k, tok],
                                                w_hi[:, k, a:b], w_lo[:, k, a:b]) for k in range(NK)])
                        last.then_inc(proj_ready, 1)
                    if t >= 2:
                        u = t - 2
                        pe.wait_ge(z_hi_done, 2 * u + 2)
                        pe.wait_ge(z_lo_done, 2 * u + 2)
                        for b in range(4):
                            if u >= 1:
                                pe.wait_ge(tp_taken, 4 * (u - 1) + b + 1)
                            z = pairs((zq if b < 2 else zk)[:, u % 2])
                            for j in range(4):
                                pe_in = f32(z[:, 4 * (b % 2) + j, :])
                                last = pe.transpose(tp[b][:, j * P:j * P + P], pe_in, ident[:, :])
                            last.then_inc(tp_ready, 1)

            @block.vector
            def _(dve):
                for t in range(NT + 1):
                    if t < NT:
                        dve.wait_ge(proj_ready, t + 1)
                        if t >= 2:
                            dve.wait_ge(v_rest, 2 * (t - 2) + 1)
                        dve.tensor_tensor(qkv[:, t % 2, :], proj[t % 2][:, 0:3 * D], bias[:, :],
                                          ALU.add).then_inc(qkv_done, 1)
                        dve.wait_ge(qkv_done, t + 1)
                        if t >= 1:
                            dve.wait_ge(rot_done, t)
                        x = qkv[:, t % 2, 0:QK].rearrange("p (a h d) -> p a h d", a=2, h=H0)
                        y1 = t1[:, :].rearrange("p (a h d) -> p a h d", a=2, h=H0)
                        y2 = t2[:, :].rearrange("p (a h d) -> p a h d", a=2, h=H0)

                        def table(tab, lo):
                            v = tab[:, t, :, lo::2] if lo is not None else tab[:, t, :, :]
                            n = DH0 // 2 if lo is not None else DH0
                            return v.unsqueeze(2).broadcast_to([P, 2, H0, n])
                        dve.tensor_tensor(y1, x, table(rope_c, None), ALU.mult).then_inc(terms_done, 1)
                        dve.tensor_tensor(y2[:, :, :, 0::2], x[:, :, :, 1::2], table(rope_s, 0),
                                          ALU.mult).then_inc(terms_done, 1)
                        dve.tensor_tensor(y2[:, :, :, 1::2], x[:, :, :, 0::2], table(rope_s, 1),
                                          ALU.mult).then_inc(terms_done, 1)
                    if t >= 1:
                        for a in range(2):
                            hi, lo = halves(t - 1, a)
                            dve.wait_ge(z_hi_done, 2 * (t - 1) + 1 + a)
                            dve.tensor_tensor(lo, rotated(t - 1, a), f32(hi), ALU.subtract).then_inc(z_lo_done, 1)

            @block.gpsimd
            def _(pool):
                for t in range(NT):
                    part = [v3[:, t, :, n, :] for n in range(PARTS0)]
                    pool.wait_ge(v_part, 2 * t + 1)
                    if t >= 2:
                        pool.wait_ge(v_rest, 2 * (t - 1))
                    pool.tensor_tensor(left(t), v_of(t), part[0], ALU.subtract).then_inc(v_rest, 1)
                    pool.wait_ge(terms_done, 3 * t + 3)
                    if t >= 2:
                        pool.wait_ge(z_lo_done, 2 * (t - 1))
                    pool.tensor_tensor(rot[:, t % 2, :], t1[:, :], t2[:, :], ALU.add).then_inc(rot_done, 1)
                    pool.wait_ge(v_part, 2 * t + 2)
                    pool.tensor_tensor(part[2], left(t), part[1], ALU.subtract).then_inc(v_rest, 1)

            @block.scalar
            def _(act):
                for t in range(NT + 2):
                    if t < NT:
                        act.wait_ge(qkv_done, t + 1)
                        act.activation(v3[:, t, :, 0, :], v_of(t), ACT.Copy).then_inc(v_part, 1)
                    if t >= 2:
                        u = t - 2
                        for b in range(4):
                            act.wait_ge(tp_ready, 4 * u + b + 1)
                            dst = (qT if b < 2 else kT)[:, 4 * (b % 2):4 * (b % 2) + 4, u * P:u * P + P]
                            act.activation(dst, tp[b][:, :].rearrange("p (a c) -> p a c", a=4),
                                           ACT.Copy).then_inc(tp_taken, 1)
                    if t < NT:
                        act.wait_ge(v_rest, 2 * t + 1)
                        act.activation(v3[:, t, :, 1, :], left(t), ACT.Copy).then_inc(v_part, 1)
                        act.wait_ge(rot_done, t + 1)
                        if t >= 2:
                            act.wait_ge(tp_ready, 4 * (t - 1))
                        for a in range(2):
                            act.activation(halves(t, a)[0], rotated(t, a), ACT.Copy).then_inc(z_hi_done, 1)


def attention0(nc, qT, kT, v3, ident, ident_bf, mask, att):
    PER = 2 * NT * GH0
    tile_of = lambda u: u // GH0 % NT
    before = chunks_before(PER, tile_of)
    CH = before[-1]
    RING = 3
    with Scope(nc) as s:
        qs = [s.sb(f"a0_q{b}", [P, GH0, T], F32R) for b in range(2)]
        ks = [s.sb(f"a0_k{b}", [P, GH0 // 2, T], F32R) for b in range(2)]
        vs = [s.sb(f"a0_v{b}", [P, NT, GH0 * VW0], BF16) for b in range(2)]
        prob = s.sb("a0_prob", [P, RING, T], F32)
        p_hi = s.sb("a0_p_hi", [P, RING, NT, P], F16)
        p_lo = s.sb("a0_p_lo", [P, RING, NT, P], F16)
        neg_max = s.sb("a0_neg_max", [P, 8], F32)
        sums = s.sb("a0_sums", [P, 4, GH0], F32)
        rinv = s.sb("a0_rinv", [P, 2, GH0], F32)
        osum = s.sb("a0_osum", [P, 2, GH0, DH0], F32)
        copied = s.sb("a0_copied", [P, 2, GH0 * VW0], F32)
        S = [s.ps(f"a0_S{b}", [P, 2 * HALF]) for b in range(2)]
        X = [s.ps(f"a0_X{b}", [P, HALF]) for b in range(3)]
        O = s.ps("a0_O", [P, HALF])
        zeroed = [s.sem(f"a0_zeroed{e}") for e in range(2)]
        PIECES = NC
        TILES = NT // PIECES
        staged = [[s.sem(f"a0_staged{b}_{c}") for c in range(PIECES)] for b in range(2)]
        scores_ready, max_done, exp_done = s.sem("a0_scores_ready"), s.sem("a0_max_done"), s.sem("a0_exp_done")
        pT_ready, hi_done, lo_done = s.sem("a0_pT_ready"), s.sem("a0_hi_done"), s.sem("a0_lo_done")
        ROWS = PER // GH0
        o_ready, rinv_done, added = s.sem("a0_o_ready"), s.sem("a0_rinv_done"), s.sem("a0_added")
        o_taken, out_done = Count(s.sem("a0_o_taken"), ROWS), Count(s.sem("a0_out_done"), ROWS)
        NSTAGE = 2 * (GH0 // 2) + 1 + 1

        def zero_rows(engine, e):
            for b in range(2):
                engine.memset(f32(qs[b][64 - 64 * e:128 - 64 * e, e::2, :]), 0.0).then_inc(zeroed[e], 1)

        with nc.Block() as block:

            @block.sync
            def _(sp):
                for n in range(GROUPS0):
                    b = n % 2
                    if n >= 2:
                        sp.wait_ge(scores_ready, (n - 1) * PER // 2)
                        sp.wait_ge(o_ready, (n - 1) * PER // 2)
                    for c in range(PIECES):
                        ts = slice(c * TILES, c * TILES + TILES)
                        sl = slice(ts.start * P, ts.stop * P)
                        for a in range(GH0 // 2):
                            pair = n * (GH0 // 2) + a
                            for e in range(2):
                                rows = slice(64 * e, 64 * e + 64)
                                sp.dma_start(f32(qs[b][rows, 2 * a + e, sl]), f32(qT[rows, pair, sl]))\
                                  .then_inc(staged[b][c], 16)
                        sp.dma_start(f32(ks[b][:, :, sl]), f32(kT[:, n * 2:n * 2 + 2, sl])).then_inc(staged[b][c], 16)
                        sp.dma_start(vs[b][:, ts, :],
                                     v3[:, ts, n * GH0:n * GH0 + GH0].rearrange("p t h r d -> p t (h r d)"))\
                          .then_inc(staged[b][c], 16)
                for b in range(2):
                    for c in range(PIECES):
                        sp.wait_ge(staged[b][c], 2 * NSTAGE * 16)

            @block.gpsimd
            def _(pool):
                zero_rows(pool, 1)
                out_done.prime(pool)
                with pool.Fori(0, 2, 1) as g:
                    for r in range(ROWS):
                        i, b = r % NT, r // NT
                        part = [copied[:, r % 2, :].rearrange("p (h r d) -> p h r d", h=GH0, r=PARTS0)[:, :, n, :]
                                for n in range(PARTS0)]
                        pool.wait_ge(o_taken.sem, o_taken.at(g, r + 1))
                        pool.wait_ge(out_done.sem, out_done.at(g, r))
                        pool.tensor_tensor(osum[:, 0, :, :], part[0], part[1], ALU.add).then_inc(added, 1)
                        pool.wait_ge(added, g * 2 * ROWS + 2 * r + 1)
                        pool.tensor_tensor(osum[:, 1, :, :], osum[:, 0, :, :], part[2], ALU.add).then_inc(added, 1)
                        pool.wait_ge(added, g * 2 * ROWS + 2 * r + 2)
                        pool.wait_ge(rinv_done, g * ROWS + (r + 1))
                        pool.tensor_tensor(att[:, i, bass.ds(g * (2 * GH0 * DH0) + b * GH0 * DH0, GH0 * DH0)]
                                           .rearrange("p (h d) -> p h d", h=GH0), osum[:, 1, :, :],
                                           rinv[:, r % 2, :].unsqueeze(2).broadcast_to([P, GH0, DH0]),
                                           ALU.mult).then_inc(out_done.sem, 1)

            @block.tensor
            def _(pe):
                with pe.Fori(0, 2, 1) as g:
                    for step in range(PER + 5):
                        if step < PER:
                            u = step
                            i, h, b = tile_of(u), u % GH0, u // (PER // 2)
                            n = (i + 1) * P
                            if h == 0 and i % TILES == 0:
                                pe.wait_ge(staged[b][i // TILES], g * (NSTAGE * 16) + NSTAGE * 16)
                            if u % (PER // 2) == 0:
                                for e in range(2):
                                    pe.wait_ge(zeroed[e], 2)
                            if u >= 2:
                                pe.wait_ge(exp_done, g * PER + (u - 1))
                            for a in range(0, n, HALF):
                                e = min(a + HALF, n)
                                diag = e == n
                                pe.matmul(S[u % 2][:, a:e], qs[b][:, h, i * P:i * P + P],
                                          ks[b][:, h // 2, a:e], start=True, stop=not diag)
                            pe.matmul(S[u % 2][:, n - P:n], ident_bf[:, :], mask[:, :],
                                      start=False, stop=True).then_inc(scores_ready, 1)
                        if 3 <= step < PER + 3:
                            u = step - 3
                            i = tile_of(u)
                            pe.wait_ge(exp_done, g * PER + (u + 1))
                            for c in range(chunks_of(i)):
                                m = before[u] + c
                                if m >= 3:
                                    pe.wait_ge(lo_done, g * CH + (m - 2))
                                js = range(4 * c, min(4 * c + 4, i + 1))
                                for j in js:
                                    last = pe.transpose(X[m % 3][:, (j % 4) * P:(j % 4) * P + P],
                                                        prob[:, u % RING, j * P:j * P + P], ident[:, :])
                                last.then_inc(pT_ready, 1)
                        if step >= 5:
                            u = step - 5
                            i, h, b = tile_of(u), u % GH0, u // (PER // 2)
                            r = u // GH0
                            pe.wait_ge(lo_done, g * CH + before[u + 1])
                            if h == 0:
                                pe.wait_ge(o_taken.sem, o_taken.at(g, r))
                            n, count = 0, 2 * (i + 1)
                            for j in range(i + 1):
                                for half in (p_hi, p_lo):
                                    last = pe.matmul(O[:, h * VW0:h * VW0 + VW0],
                                                     half[:, u % RING, j, :],
                                                     vs[b][:, j, h * VW0:h * VW0 + VW0],
                                                     start=n == 0, stop=n == count - 1)
                                    n += 1
                            last.then_inc(o_ready, 1)

            @block.scalar
            def _(act):
                o_taken.prime(act)
                with act.Fori(0, 2, 1) as g:
                    for step in range(PER + 6):
                        if 1 <= step < PER + 1:
                            u = step - 1
                            i = tile_of(u)
                            n = (i + 1) * P
                            act.wait_ge(max_done, g * PER + (u + 1))
                            if u >= RING:
                                act.wait_ge(pT_ready, g * CH + before[u - RING + 1])
                            act.activation(prob[:, u % RING, 0:n], S[u % 2][:, 0:n], ACT.Exp,
                                           bias=neg_max[:, u % 8:u % 8 + 1],
                                           accum_out=sums[:, u // GH0 % 4, u % GH0:u % GH0 + 1])\
                               .then_inc(exp_done, 1)
                        if step >= 9 and step % GH0 == 1:
                            r = step // GH0 - 2
                            act.wait_ge(o_ready, g * PER + (r + 1) * GH0)
                            act.wait_ge(out_done.sem, out_done.at(g, r - 1))
                            act.activation(copied[:, r % 2, :], O[:, 0:GH0 * VW0], ACT.Copy).then_inc(o_taken.sem, 1)
                        if 3 <= step < PER + 3:
                            u = step - 3
                            i = tile_of(u)
                            if u >= RING:
                                act.wait_ge(o_ready, g * PER + (u - RING + 1))
                            for c in range(chunks_of(i)):
                                m = before[u] + c
                                js = slice(4 * c, min(4 * c + 4, i + 1))
                                n = (js.stop - js.start) * P
                                act.wait_ge(pT_ready, g * CH + (m + 1))
                                act.activation(p_hi[:, u % RING, js, :].rearrange("p a c -> p (a c)"),
                                               X[m % 3][:, 0:n], ACT.Copy).then_inc(hi_done, 1)

            @block.vector
            def _(dve):
                zero_rows(dve, 0)
                with dve.Fori(0, 2, 1) as g:
                    for step in range(PER + 3):
                        if step < PER:
                            u = step
                            n = (tile_of(u) + 1) * P
                            dve.wait_ge(scores_ready, g * PER + (u + 1))
                            dve.tensor_reduce(neg_max[:, u % 8:u % 8 + 1], S[u % 2][:, 0:n], AX.X,
                                              ALU.max, negate=True).then_inc(max_done, 1)
                        if step >= GH0 + 2 and step % GH0 == 2:
                            r = (step - 2) // GH0 - 1
                            dve.wait_ge(exp_done, g * PER + (r + 1) * GH0)
                            dve.wait_ge(out_done.sem, out_done.at(g, r - 1))
                            dve.reciprocal(rinv[:, r % 2, :], sums[:, r % 4, :]).then_inc(rinv_done, 1)
                        if 3 <= step < PER + 3:
                            u = step - 3
                            i = tile_of(u)
                            for c in range(chunks_of(i)):
                                m = before[u] + c
                                js = slice(4 * c, min(4 * c + 4, i + 1))
                                n = (js.stop - js.start) * P
                                dve.wait_ge(hi_done, g * CH + (m + 1))
                                dve.tensor_tensor(p_lo[:, u % RING, js, :].rearrange("p a c -> p (a c)"),
                                                  X[m % 3][:, 0:n],
                                                  p_hi[:, u % RING, js, :].rearrange("p a c -> p (a c)"),
                                                  ALU.subtract).then_inc(lo_done, 1)


def project_out0(nc, att, wo_hi, wo_lo, bo, ident, sT):
    with Scope(nc) as s:
        a_hi = s.sb("o0_a_hi", [P, NK, T], F32R)
        a_lo = s.sb("o0_a_lo", [P, NK, T], F32R)
        aT = [s.ps(f"o0_aT{k}", [P, T]) for k in range(NK)]
        acc = [s.ps(f"o0_acc{c}", [P, 2 * HALF]) for c in range(NC)]
        aT_ready, hi_done, lo_done, y_ready, y_done = (
            s.sem("o0_aT_ready"), s.sem("o0_hi_done"), s.sem("o0_lo_done"), s.sem("o0_y_ready"), s.sem("o0_y_done"))
        with nc.Block() as block:

            @block.tensor
            def _(pe):
                for c in range(NC):
                    for k in range(NK):
                        for t in range(4 * c, 4 * c + 4):
                            last = pe.transpose(aT[k][:, t * P:t * P + P], att[:, t, k * P:k * P + P],
                                                ident[:, :])
                        last.then_inc(aT_ready, 1)
                for c in range(NC):
                    pe.wait_ge(lo_done, NK * (c + 1))
                    sl = slice(c * HALF, c * HALF + HALF)
                    for m in range(NK):
                        three_pass(pe, acc[c][:, m * HALF:m * HALF + HALF],
                                   [(wo_hi[:, k, m * P:m * P + P], wo_lo[:, k, m * P:m * P + P],
                                     a_hi[:, k, sl], a_lo[:, k, sl]) for k in range(NK)])\
                            .then_inc(y_ready, 1)

            @block.scalar
            def _(act):
                n = 0
                for c in range(NC):
                    for k in range(NK):
                        n += 1
                        sl = slice(c * HALF, c * HALF + HALF)
                        act.wait_ge(aT_ready, n)
                        act.activation(a_hi[:, k, sl], aT[k][:, sl], ACT.Copy).then_inc(hi_done, 1)

            @block.vector
            def _(dve):
                n = 0
                for c in range(NC):
                    for k in range(NK):
                        n += 1
                        sl = slice(c * HALF, c * HALF + HALF)
                        dve.wait_ge(hi_done, n)
                        dve.tensor_tensor(a_lo[:, k, sl], aT[k][:, sl], f32(a_hi[:, k, sl]),
                                          ALU.subtract).then_inc(lo_done, 1)
                n = 0
                for c in range(NC):
                    for m in range(NK):
                        n += 1
                        dve.wait_ge(y_ready, n)
                        dve.tensor_scalar(sT[:, m, c * HALF:c * HALF + HALF],
                                          acc[c][:, m * HALF:m * HALF + HALF],
                                          bo[:, m:m + 1], None, ALU.add).then_inc(y_done, 1)


def gated_ffn(nc, tag, tiles, weights, cols, offset, scales, down_scale, xn_hi, xn_lo, gate_hi, gT,
              side_loads=None, side_jobs=None):
    routed = gate_hi is not None
    with Scope(nc) as s:
        raw = [s.sb(f"{tag}_raw{b}", [P, cols], weights.dtype) for b in range(2)]
        wx_hi = [s.sb(f"{tag}_wx_hi{b}", [P, cols - D], F32R) for b in range(2)]
        wx_lo = [s.sb(f"{tag}_wx_lo{b}", [P, 2 * NK * P], F32R) for b in range(2)]
        wd_hi = [s.sb(f"{tag}_wd_hi{b}", [P, D], F32R) for b in range(2)]
        wd_lo = [s.sb(f"{tag}_wd_lo{b}", [P, D], F32R) for b in range(2)]
        sc = [s.sb(f"{tag}_sc{b}", [P, 2], F32) for b in range(2)]
        sg = s.sb(f"{tag}_sg", [P, NC, HALF], F32)
        h1 = s.sb(f"{tag}_h1", [P, NC, HALF], F32)
        hh = s.sb(f"{tag}_hh", [P, NC, HALF], F32)
        h_hi = [s.sb(f"{tag}_h_hi{b}", [P, T], F32R) for b in range(2)]
        h_lo = [s.sb(f"{tag}_h_lo{b}", [P, T], F32R) for b in range(2)]
        G = [s.ps(f"{tag}_G{c}", [P, HALF]) for c in range(NC)]
        U = [s.ps(f"{tag}_U{c}", [P, HALF]) for c in range(NC)]
        acc = [s.ps(f"{tag}_acc{c}", [P, HALF]) for c in range(NK * NC)]
        two = lambda name: [s.sem(f"{tag}_{name}{b}") for b in range(2)]
        counts = lambda name, per: [Count(x, per) for x in two(name)]
        loaded, wx_hi_done, wx_lo_done = two("loaded"), two("wx_hi_done"), two("wx_lo_done")
        wd_hi_done, wd_lo_done = two("wd_hi_done"), counts("wd_lo_done", 1)
        gate_ready, up_ready, silu_done = two("gate_ready"), two("up_ready"), two("silu_done")
        mix_ready, h1_done, h_done = two("mix_ready"), two("h1_done"), counts("h_done", NC)
        h_hi_done, h_lo_done = counts("h_hi_done", NC), counts("h_lo_done", NC)
        down_done = counts("down_done", 1)
        zeroed, opened, all_down, g_done = (s.sem(f"{tag}_zeroed"), s.sem(f"{tag}_opened"),
                                            s.sem(f"{tag}_all_down"), s.sem(f"{tag}_g_done"))
        NL = 2 if scales is not None else 1
        passes = tiles // 2
        half = lambda c: slice(c * HALF, c * HALF + HALF)

        def w(t, part, k):
            at = (part * NK + k) * P
            return t[:, at:at + P]

        def down(pe, b, stop):
            for c in range(NC):
                for m in range(NK):
                    cut = slice(m * P, m * P + P)
                    last = three_pass(pe, acc[m * NC + c][:, :],
                                      [(wd_hi[b][:, cut], wd_lo[b][:, cut], h_hi[b][:, half(c)], h_lo[b][:, half(c)])],
                                      start=False, stop=stop, check=False)
            return last

        with nc.Block() as block:

            @block.sync
            def _(sp):
                sp.dma_start(raw[0][:, :], weights[0, :, :]).then_inc(loaded[0], 16)
                if scales is not None:
                    sp.dma_start(sc[0][:, :], scales[0, :, :]).then_inc(loaded[0], 16)
                if side_loads:
                    side_loads(sp)
                with sp.Fori(0, passes, 1) as g:
                    for b in range(2):
                        n = 1 - b
                        sp.wait_ge(wd_lo_done[n].sem, wd_lo_done[n].at(g, b))
                        sp.dma_start(raw[n][:, :], weights[g * 2 + (b + 1), :, :]).then_inc(loaded[n], 16)
                        if scales is not None:
                            sp.wait_ge(h_done[n].sem, h_done[n].at(g, NC * b))
                            sp.dma_start(sc[n][:, :], scales[g * 2 + (b + 1), :, :]).then_inc(loaded[n], 16)

            @block.gpsimd
            def _(pool):
                for t in (h_hi, h_lo, wd_hi, wd_lo):
                    pool.memset(f32(t[1][:, :]), 0.0).then_inc(zeroed, 1)
                if side_jobs:
                    side_jobs(pool)

            @block.tensor
            def _(pe):
                pe.wait_ge(zeroed, 4)
                for b in range(2):
                    down_done[b].prime(pe)
                for a in acc:
                    last = pe.matmul(a[:, :], wd_hi[1][:, 0:P], h_hi[1][:, 0:HALF], start=True,
                                     stop=False, skip_group_check=True)
                last.then_inc(opened, 1)
                with pe.Fori(0, passes, 1) as g:
                    for b in range(2):
                        def mix(c):
                            pe.wait_ge(silu_done[b], g * NC + (c + 1))
                            pe.matmul(G[c][:, :], wx_hi[b][:, 2 * NK * P:2 * NK * P + P],
                                      gate_hi[:, half(c)], start=True, stop=True).then_inc(mix_ready[b], 1)
                        pe.wait_ge(wx_hi_done[b], g + 1)
                        pe.wait_ge(wx_lo_done[b], g + 1)
                        for c in range(NC):
                            pe.wait_ge(h_done[1 - b].sem, h_done[1 - b].at(g, c + 1 if b else 0))
                            x = [(xn_hi[:, k, half(c)], xn_lo[:, k, half(c)]) for k in range(NK)]
                            three_pass(pe, G[c][:, :], [(w(wx_hi[b], 0, k), w(wx_lo[b], 0, k), *x[k])
                                                        for k in range(NK)]).then_inc(gate_ready[b], 1)
                            if routed and c:
                                mix(c - 1)
                            three_pass(pe, U[c][:, :], [(w(wx_hi[b], 1, k), w(wx_lo[b], 1, k), *x[k])
                                                        for k in range(NK)]).then_inc(up_ready[b], 1)
                        if routed:
                            mix(NC - 1)
                        pe.wait_ge(wd_lo_done[1 - b].sem, wd_lo_done[1 - b].at(g, b))
                        pe.wait_ge(h_lo_done[1 - b].sem, h_lo_done[1 - b].at(g, NC * b))
                        down(pe, 1 - b, False).then_inc(down_done[1 - b].sem, 1)
                pe.wait_ge(wd_lo_done[1].sem, wd_lo_done[1].at(passes - 1, 1))
                pe.wait_ge(h_lo_done[1].sem, h_lo_done[1].at(passes - 1, NC))
                down(pe, 1, True).then_inc(all_down, 1)

            @block.scalar
            def _(act):
                for b in range(2):
                    h_hi_done[b].prime(act)
                act.wait_ge(loaded[0], 16 * NL)
                act.activation(wx_hi[0][:, :], raw[0][:, D:cols], ACT.Copy, bias=offset)\
                   .then_inc(wx_hi_done[0], 1)
                with act.Fori(0, passes, 1) as g:
                    for b in range(2):
                        for c in range(NC):
                            act.wait_ge(gate_ready[b], g * NC + (c + 1))
                            act.wait_ge(h_done[1 - b].sem, h_done[1 - b].at(g, c + 1 if b else 0))
                            act.activation(sg[:, c, :], G[c][:, :], ACT.Silu,
                                           **({"scale": sc[b][:, 0:1]} if scales is not None else {}))\
                               .then_inc(silu_done[b], 1)
                            if c == 0:
                                act.wait_ge(down_done[b].sem, down_done[b].at(g, b))
                                act.activation(wd_hi[b][:, :], raw[b][:, 0:D], ACT.Copy, bias=offset)\
                                   .then_inc(wd_hi_done[b], 1)
                                act.wait_ge(loaded[1 - b], g * (16 * NL) + 16 * NL * (b + 1))
                                act.activation(wx_hi[1 - b][:, :], raw[1 - b][:, D:cols], ACT.Copy, bias=offset)\
                                   .then_inc(wx_hi_done[1 - b], 1)
                        for c in range(NC):
                            act.wait_ge(h_done[b].sem, h_done[b].at(g, c + 1))
                            act.activation(h_hi[b][:, half(c)], hh[:, c, :], ACT.Copy)\
                               .then_inc(h_hi_done[b].sem, 1)
                act.wait_ge(all_down, 1)
                for m in range(NK):
                    for c in range(NC):
                        act.activation(gT[:, m, half(c)], acc[m * NC + c][:, :], ACT.Silu,
                                       **({"scale": down_scale[:, m:m + 1]} if down_scale is not None else {}))\
                           .then_inc(g_done, 1)

            @block.vector
            def _(dve):
                def split_lo(lo, source, hi, count):
                    dve.scalar_tensor_tensor(lo, source, offset, f32(hi), ALU.add, ALU.subtract).then_inc(count, 1)
                for b in range(2):
                    for count in (wd_lo_done[b], h_done[b], h_lo_done[b]):
                        count.prime(dve)
                gate_up = slice(D, D + 2 * NK * P)
                dve.wait_ge(wx_hi_done[0], 1)
                split_lo(wx_lo[0][:, :], raw[0][:, gate_up], wx_hi[0][:, 0:2 * NK * P], wx_lo_done[0])
                with dve.Fori(0, passes, 1) as g:
                    for b in range(2):
                        for c in range(NC):
                            if c == NC - 1:
                                dve.wait_ge(wd_hi_done[b], g + 1)
                                split_lo(wd_lo[b][:, :], raw[b][:, 0:D], wd_hi[b][:, :], wd_lo_done[b].sem)
                                dve.wait_ge(wx_hi_done[1 - b], g + (1 + b))
                                split_lo(wx_lo[1 - b][:, :], raw[1 - b][:, gate_up],
                                         wx_hi[1 - b][:, 0:2 * NK * P], wx_lo_done[1 - b])
                            dve.wait_ge(silu_done[b], g * NC + (c + 1))
                            dve.wait_ge(up_ready[b], g * NC + (c + 1))
                            dve.wait_ge(h_hi_done[1 - b].sem, h_hi_done[1 - b].at(g, c + 1 if b else 0))
                            dve.wait_ge(h_lo_done[1 - b].sem, h_lo_done[1 - b].at(g, c + 1 if b else 0))
                            if routed:
                                dve.tensor_tensor(h1[:, c, :], U[c][:, :], sg[:, c, :], ALU.mult)\
                                   .then_inc(h1_done[b], 1)
                                dve.wait_ge(h1_done[b], g * NC + (c + 1))
                                dve.wait_ge(mix_ready[b], g * NC + (c + 1))
                                dve.tensor_tensor(hh[:, c, :], G[c][:, :], h1[:, c, :], ALU.mult)\
                                   .then_inc(h_done[b].sem, 1)
                            else:
                                dve.scalar_tensor_tensor(hh[:, c, :], U[c][:, :], sc[b][:, 1:2], sg[:, c, :],
                                                         ALU.mult, ALU.mult).then_inc(h_done[b].sem, 1)
                        for c in range(NC):
                            dve.wait_ge(h_hi_done[b].sem, h_hi_done[b].at(g, c + 1))
                            dve.tensor_tensor(h_lo[b][:, half(c)], hh[:, c, :], f32(h_hi[b][:, half(c)]),
                                              ALU.subtract).then_inc(h_lo_done[b].sem, 1)


def combine0(nc, xT, sT, gT, ident, x_tok):
    with Scope(nc) as s:
        prod = s.sb("c0_prod", [P, NK, T], F32)
        tp = [s.ps(f"c0_tp{b}", [P, HALF]) for b in range(4)]
        prod_done, x_done, tp_ready, taken = (s.sem("c0_prod_done"), s.sem("c0_x_done"),
                                              s.sem("c0_tp_ready"), s.sem("c0_taken"))
        with nc.Block() as block:

            @block.vector
            def _(dve):
                for c in range(NC):
                    sl = slice(c * HALF, c * HALF + HALF)
                    dve.tensor_tensor(prod[:, :, sl], sT[:, :, sl], gT[:, :, sl], ALU.mult)\
                       .then_inc(prod_done, 1)
                    dve.wait_ge(prod_done, c + 1)
                    dve.tensor_tensor(xT[:, :, sl], xT[:, :, sl], prod[:, :, sl], ALU.add)\
                       .then_inc(x_done, 1)

            @block.tensor
            def _(pe):
                for n in range(NT // 2):
                    pe.wait_ge(x_done, n // 2 + 1)
                    for j in range(2):
                        for k in range(NK):
                            t = 2 * n + j
                            last = pe.transpose(tp[n][:, (j * NK + k) * P:(j * NK + k) * P + P],
                                                xT[:, k, t * P:t * P + P], ident[:, :])
                    last.then_inc(tp_ready, 1)

            @block.scalar
            def _(act):
                for n in range(NT // 2):
                    act.wait_ge(tp_ready, n + 1)
                    act.activation(x_tok[:, 2 * n:2 * n + 2, :],
                                   tp[n][:, :].rearrange("p (t d) -> p t d", t=2),
                                   ACT.Copy).then_inc(taken, 1)


def route1(nc, xn_hi, xn_lo, wr, earlier, ident, gate_hi):
    E = 16
    with Scope(nc) as s:
        wr_hi = s.sb("r1_wr_hi", [P, NK, E1], F32R)
        wr_lo = s.sb("r1_wr_lo", [P, NK, E1], F32R)
        lg = s.sb("r1_lg", [E1, T], F32)
        sm = s.sb("r1_sm", [P, NT], F32)
        e = s.sb("r1_e", [P, 3, NT, E1], F32)
        cmp = s.sb("r1_cmp", [P, 3, NT, E1 * E1], F32)
        rank = s.sb("r1_rank", [P, 2, NT * E1], F32)
        wt = s.sb("r1_wt", [P, NT, E], F32)
        L = [s.ps(f"r1_L{c}", [P, HALF]) for c in range(NC)]
        LT = s.ps("r1_LT", [P, HALF])
        WT = [s.ps(f"r1_WT{c}", [P, HALF]) for c in range(NC)]
        wr_hi_done, step, act_step = s.sem("r1_wr_hi_done"), s.sem("r1_step"), s.sem("r1_act_step")
        logits_ready, lt_ready, wt_ready = s.sem("r1_logits_ready"), s.sem("r1_lt_ready"), s.sem("r1_wt_ready")
        zeroed, g_hi_done = s.sem("r1_zeroed"), s.sem("r1_g_hi_done")
        with nc.Block() as block:

            @block.gpsimd
            def _(pool):
                pool.memset(f32(gate_hi[:, :]), 0.0).then_inc(zeroed, 1)
                pool.memset(wt[:, :, E1:E1 + 1], 1.0).then_inc(zeroed, 1)
                pool.memset(wt[:, :, E1 + 1:E], 0.0).then_inc(zeroed, 1)

            @block.scalar
            def _(act):
                act.activation(wr_hi[:, :, :], wr[:, :, :], ACT.Copy).then_inc(wr_hi_done, 1)
                for c in range(NC):
                    act.wait_ge(logits_ready, c + 1)
                    act.activation(lg[:, c * HALF:c * HALF + HALF], L[c][0:E1, :], ACT.Copy)\
                       .then_inc(act_step, 1)
                act.wait_ge(step, 3)
                act.activation(e[:, 1, :, :], e[:, 0, :, :], ACT.Exp).then_inc(act_step, 1)
                act.wait_ge(zeroed, 3)
                for c in range(NC):
                    act.wait_ge(wt_ready, c + 1)
                    act.activation(gate_hi[0:E, c * HALF:c * HALF + HALF], WT[c][0:E, :], ACT.Copy)\
                       .then_inc(g_hi_done, 1)

            @block.tensor
            def _(pe):
                pe.wait_ge(step, 1)
                for c in range(NC):
                    sl = slice(c * HALF, c * HALF + HALF)
                    three_pass(pe, L[c][0:E1, :], [(wr_hi[:, k, :], wr_lo[:, k, :], xn_hi[:, k, sl],
                                                    xn_lo[:, k, sl]) for k in range(NK)])\
                        .then_inc(logits_ready, 1)
                for t in range(NT):
                    pe.wait_ge(act_step, t // 4 + 1)
                    last = pe.transpose(LT[:, t * E1:t * E1 + E1], lg[0:E1, t * P:t * P + P],
                                        ident[0:E1, 0:E1])
                last.then_inc(lt_ready, 1)
                pe.wait_ge(step, 13)
                pe.wait_ge(zeroed, 3)
                for c in range(NC):
                    for j in range(4):
                        last = pe.transpose(WT[c][0:E, j * P:j * P + P], wt[:, 4 * c + j, :], ident[:, :])
                    last.then_inc(wt_ready, 1)

            @block.vector
            def _(dve):
                def done(n):
                    dve.wait_ge(step, n)

                dve.wait_ge(wr_hi_done, 1)
                dve.tensor_tensor(wr_lo[:, :, :], wr[:, :, :], f32(wr_hi[:, :, :]), ALU.subtract)\
                   .then_inc(step, 1)
                dve.wait_ge(lt_ready, 1)
                lt = LT[:, 0:NT * E1].rearrange("p (t e) -> p t e", t=NT)
                wide = lambda v: v.unsqueeze(2).broadcast_to([P, NT, E1])
                dve.tensor_reduce(sm[:, :], lt, AX.X, ALU.max).then_inc(step, 1)
                done(2)
                dve.tensor_tensor(e[:, 0, :, :], lt, wide(sm[:, :]), ALU.subtract).then_inc(step, 1)
                dve.wait_ge(act_step, NC + 1)
                done(3)
                dve.tensor_reduce(sm[:, :], e[:, 1, :, :], AX.X, ALU.add).then_inc(step, 1)
                done(4)
                dve.reciprocal(rank[:, 0, 0:NT], sm[:, :]).then_inc(step, 1)
                done(5)
                dve.tensor_tensor(e[:, 2, :, :], e[:, 1, :, :], wide(rank[:, 0, 0:NT]), ALU.mult)\
                   .then_inc(step, 1)
                done(6)
                this = e[:, 2, :, :].unsqueeze(3).broadcast_to([P, NT, E1, E1])
                other = e[:, 2, :, :].unsqueeze(2).broadcast_to([P, NT, E1, E1])
                c4 = lambda n: cmp[:, n, :, :].rearrange("p t (a b) -> p t a b", a=E1)
                dve.tensor_tensor(c4(0), other, this, ALU.is_gt).then_inc(step, 1)
                dve.tensor_tensor(c4(1), other, this, ALU.is_equal).then_inc(step, 1)
                done(8)
                dve.tensor_tensor(cmp[:, 2, :, :], cmp[:, 1, :, :],
                                  earlier[:, :].unsqueeze(1).broadcast_to([P, NT, E1 * E1]), ALU.mult)\
                   .then_inc(step, 1)
                done(9)
                dve.tensor_tensor(cmp[:, 1, :, :], cmp[:, 0, :, :], cmp[:, 2, :, :], ALU.add)\
                   .then_inc(step, 1)
                done(10)
                dve.tensor_reduce(rank[:, 0, :].rearrange("p (t e) -> p t e", t=NT), c4(1), AX.X, ALU.add)\
                   .then_inc(step, 1)
                done(11)
                dve.tensor_scalar(rank[:, 1, :], rank[:, 0, :], float(TOPK) - 0.5, None, ALU.is_lt)\
                   .then_inc(step, 1)
                done(12)
                dve.tensor_tensor(wt[:, :, 0:E1], e[:, 2, :, :],
                                  rank[:, 1, :].rearrange("p (t e) -> p t e", t=NT), ALU.mult)\
                   .then_inc(step, 1)
                for c in range(NC):
                    sl = slice(c * HALF, c * HALF + HALF)
                    dve.wait_ge(g_hi_done, c + 1)
                    dve.tensor_tensor(gate_hi[32:32 + E, sl], WT[c][0:E, :], f32(gate_hi[0:E, sl]),
                                      ALU.subtract).then_inc(step, 1)


def attention1(nc, xn_hi, xn_lo, raw, w_hi, w_lo, wo_hi, wo_lo, o_hi, o_lo, w_qkv, w_out, rope_c, rope_s, ident, ident_bf, mask, acc):
    PER = NT * GH1
    PAIRS = PER // 2
    tile_of = lambda u: u // GH1
    FIRST = NT // NC * GH1
    NH = GH1 + 2
    NP = NH * NC
    RH = GH1 + 1
    QC = RH * NC
    head_of = lambda n: (GH1, *range(GH1), GH1 + 1)[n % NH]
    bank_of = lambda n: n if n < 4 else 1 + 2 * (n % 2)
    chunk_at = lambda u: chunks_before(PER, tile_of)[u] + (1 if u < FIRST else NC)
    CH = chunk_at(PER)
    V_CHUNK = (0, chunk_at(FIRST) - 1)
    chunk_in_step = lambda step: NH + step // 2 if step % 2 == 0 and 0 <= step < 2 * NH else None
    by_dve = lambda u: u >= FIRST and u % 2 == 0
    divided = lambda u, who: sum(by_dve(v) == who for v in range(u + 1))
    RP, RX = 3, 2
    with Scope(nc) as s:
        zero = s.sb("a1_zero", [P, 1], F32)
        q_hi = s.sb("a1_q_hi", [P, GH1 + 1, T], F32R)
        q_lo = s.sb("a1_q_lo", [P, GH1 + 1, T], F32R)
        vT = s.sb("a1_vT", [P, T], F32)
        v_hi = s.sb("a1_v_hi", [P, T], F32R)
        v_lo = s.sb("a1_v_lo", [P, T], F32R)
        swapped = s.sb("a1_swapped", [P, 2, HALF], F32)
        t1 = s.sb("a1_t1", [P, 2, HALF], F32)
        t2 = s.sb("a1_t2", [P, 2, HALF], F32)
        rot = s.sb("a1_rot", [P, 2, HALF], F32)
        prob = s.sb("a1_prob", [P, RP, T], F32)
        p_hi = s.sb("a1_p_hi", [P, RX, NT, 2, P], F32R)
        p_lo = s.sb("a1_p_lo", [P, RX, NT, 2, P], F32R)
        neg_max = s.sb("a1_neg_max", [P, 8], F32)
        sums = s.sb("a1_sums", [P, 8], F32)
        rinv = s.sb("a1_rinv", [P, 8], F32)
        S = [s.ps(f"a1_S{b}", [P, 2 * HALF]) for b in range(2)]
        X = [s.ps(f"a1_X{b}", [P, HALF]) for b in range(2)]
        O = [s.ps(f"a1_O{b}", [P, HALF]) for b in range(2)]
        proj = [S[n // 2][:, (n % 2) * HALF:(n % 2) * HALF + HALF] for n in range(4)]

        loaded, w_step = s.sem("a1_loaded"), Count(s.sem("a1_w_step"), 4)
        proj_ready, swap_done, terms_done, rot_done = (Count(s.sem("a1_proj_ready"), NP), s.sem("a1_swap_done"),
                                                       s.sem("a1_terms_done"), s.sem("a1_rot_done"))
        q_hi_done, q_lo_done = s.sem("a1_q_hi_done"), s.sem("a1_q_lo_done")
        vT_done = s.sem("a1_vT_done")
        scores_ready, max_done, exp_done = s.sem("a1_scores_ready"), s.sem("a1_max_done"), s.sem("a1_exp_done")
        rinv_done, norm_done = s.sem("a1_rinv_done"), {True: s.sem("a1_dve_norm_done"), False: s.sem("a1_act_norm_done")}
        x_ready, hi_done, lo_done = s.sem("a1_x_ready"), s.sem("a1_hi_done"), s.sem("a1_lo_done")
        o_ready, o_hi_done, o_lo_done = s.sem("a1_o_ready"), s.sem("a1_o_hi_done"), Count(s.sem("a1_o_lo_done"), PAIRS)
        y_ready, y_done = Count(s.sem("a1_y_ready"), NC * NK), Count(s.sem("a1_y_done"), NC * NK)
        zero_done = s.sem("a1_zero_done")

        with nc.Block() as block:

            @block.sync
            def _(sp):
                with sp.Fori(0, KV1, 1) as g:
                    sp.wait_ge(w_step.sem, w_step.at(g, 0))
                    sp.dma_start(raw[:, 0:GH1 * D], w_out[g, :, :]).then_inc(loaded, 16)
                    sp.wait_ge(w_step.sem, w_step.at(g, 2))
                    sp.dma_start(raw[:, :], w_qkv[g + 1, :, :]).then_inc(loaded, 16)

            @block.gpsimd
            def _(pool):
                pool.memset(zero[:, :], 0.0).then_inc(zero_done, 1)
                pool.wait_ge(zero_done, 1)
                w_step.prime(pool)
                flat = lambda v: v.rearrange("p a b -> p (a b)")

                def split(hi, lo, n, done):
                    pool.tensor_tensor(hi, raw[:, 0:n], zero[:, :].broadcast_to([P, n]), ALU.add)\
                        .then_inc(w_step.sem, 1)
                    pool.wait_ge(w_step.sem, w_step.at(g, done + 1))
                    pool.tensor_tensor(lo, raw[:, 0:n], f32(hi), ALU.subtract).then_inc(w_step.sem, 1)

                with pool.Fori(0, KV1, 1) as g:
                    def rope_sum(r):
                        pool.wait_ge(terms_done, g * 2 * QC + 2 * r + 2)
                        if r >= 2:
                            pool.wait_ge(q_lo_done, g * QC + (r - 1))
                        pool.tensor_tensor(rot[:, r % 2, :], t1[:, r % 2, :], t2[:, r % 2, :], ALU.add)\
                            .then_inc(rot_done, 1)

                    for r in range(QC):
                        rope_sum(r)
                    pool.wait_ge(loaded, g * 32 + 16)
                    pool.wait_ge(y_ready.sem, y_ready.at(g, NK))
                    split(flat(wo_hi[:, :, :]), flat(wo_lo[:, :, :]), GH1 * D, 0)
                    pool.wait_ge(loaded, g * 32 + 32)
                    pool.wait_ge(proj_ready.sem, proj_ready.at(g, NP))
                    split(flat(w_hi[:, :, :]), flat(w_lo[:, :, :]), GWCOLS1, 2)

            @block.tensor
            def _(pe):
                proj_ready.prime(pe)
                y_ready.prime(pe)

                def project(n):
                    m, sl = head_of(n), slice(n // NH * HALF, n // NH * HALF + HALF)
                    three_pass(pe, proj[bank_of(n)],
                               [(w_hi[:, k, m * P:m * P + P], w_lo[:, k, m * P:m * P + P],
                                 xn_hi[:, k, sl], xn_lo[:, k, sl]) for k in range(NK)])\
                        .then_inc(proj_ready.sem, 1)

                def transpose_v(c):
                    pe.wait_ge(vT_done, g * NC + (c + 1))
                    if c:
                        pe.wait_ge(lo_done, g * CH + (V_CHUNK[c] - 1))
                    for j in range(4):
                        t = 4 * c + j
                        last = pe.transpose(X[V_CHUNK[c] % 2][:, j * P:j * P + P], vT[:, t * P:t * P + P],
                                            ident[:, :])
                    last.then_inc(x_ready, 1)

                def project_out(m):
                    three_pass(pe, O[m][:, :],
                               [(wo_hi[:, h, m * P:m * P + P], wo_lo[:, h, m * P:m * P + P],
                                 o_hi[:, h, :], o_lo[:, h, :]) for h in range(GH1)])\
                        .then_inc(y_ready.sem, 1)

                for n in range(4):
                    project(n)
                with pe.Fori(0, KV1, 1) as g:
                    pe.wait_ge(o_lo_done.sem, o_lo_done.at(g, 0))
                    project_out(0)
                    for n in range(4, NH):
                        pe.wait_ge(terms_done, g * 2 * QC + 2 * bank_of(n) + 1)
                        project(n)
                    project_out(1)
                    for step in range(PER + 6):
                        if step < PER:
                            u = step
                            i, h = tile_of(u), u % GH1
                            n, rows = (i + 1) * P, slice(i * P, i * P + P)
                            if u >= 2:
                                pe.wait_ge(exp_done, g * PER + (u - 1))
                            if u < GH1:
                                pe.wait_ge(q_lo_done, g * QC + (u + 2))
                            if u == FIRST:
                                pe.wait_ge(q_lo_done, g * QC + QC)
                                pe.wait_ge(vT_done, g * NC + NC)
                            for a in range(0, n, HALF):
                                e = min(a + HALF, n)
                                three_pass(pe, S[u % 2][:, a:e],
                                           [(q_hi[:, h, rows], q_lo[:, h, rows],
                                             q_hi[:, GH1, a:e], q_lo[:, GH1, a:e])], stop=e != n)
                            pe.matmul(S[u % 2][:, n - P:n], ident_bf[:, :], mask[:, :], start=False,
                                      stop=True).then_inc(scores_ready, 1)
                        if step == 0:
                            transpose_v(0)
                        if step == FIRST + 3:
                            transpose_v(1)
                        if 3 <= step < PER + 3:
                            u = step - 3
                            i = tile_of(u)
                            who = by_dve(u)
                            pe.wait_ge(norm_done[who], g * divided(PER - 1, who) + divided(u, who))
                            for c in range(chunks_of(i)):
                                m = chunk_at(u) + c
                                if m >= 2:
                                    pe.wait_ge(lo_done, g * CH + (m - 1))
                                for j in range(4 * c, min(4 * c + 4, i + 1)):
                                    last = pe.transpose(X[m % 2][:, (j % 4) * P:(j % 4) * P + P],
                                                        prob[:, u % RP, j * P:j * P + P], ident[:, :])
                                last.then_inc(x_ready, 1)
                        if step == FIRST + 5:
                            pe.wait_ge(o_lo_done.sem, o_lo_done.at(g, PAIRS // 2))
                            pe.wait_ge(w_step.sem, w_step.at(g, 2))
                            for m in range(NK):
                                project_out(m)
                        if step == PER + 3:
                            pe.wait_ge(w_step.sem, w_step.at(g, 4))
                            pe.wait_ge(exp_done, g * PER + PER)
                            project(0)
                        if 5 <= step < PER + 5 and step % 2 == 1:
                            p = (step - 5) // 2
                            i = tile_of(2 * p)
                            pe.wait_ge(lo_done, g * CH + chunk_at(2 * p + 1) + chunks_of(i))
                            if p % 8 >= 2:
                                pe.wait_ge(o_lo_done.sem, o_lo_done.at(g, p - 1))
                            else:
                                pe.wait_ge(y_done.sem, y_done.at(g, p % 8 + 1 + (NK if p >= 8 else 0)))
                            three_pass(pe, O[p % 2][:, 0:2 * P],
                                       [(v_hi[:, j * P:j * P + P], v_lo[:, j * P:j * P + P],
                                         p_hi[:, p % RX, j].rearrange("p h c -> p (h c)"),
                                         p_lo[:, p % RX, j].rearrange("p h c -> p (h c)"))
                                        for j in range(i + 1)]).then_inc(o_ready, 1)
                        n = chunk_in_step(step)
                        if n is not None:
                            if n == NH + 1:
                                pe.wait_ge(vT_done, g * NC + 1)
                            else:
                                r = n - 2 - (n - 2) // NH
                                pe.wait_ge(terms_done, g * 2 * QC + 2 * r + 1)
                            project(n)
                    for n in (1, 2, 3):
                        project(n)
                pe.wait_ge(o_lo_done.sem, o_lo_done.at(KV1, 0))
                for m in range(NK):
                    project_out(m)

            @block.scalar
            def _(act):
                def exchange(n):
                    act.wait_ge(proj_ready.sem, proj_ready.at(g, n + 1))
                    c, r = n // NH, n - n // NH
                    if head_of(n) > GH1:
                        act.activation(vT[:, c * HALF:c * HALF + HALF], proj[bank_of(n)], ACT.Copy)\
                           .then_inc(vT_done, 1)
                        return
                    if r >= 2:
                        act.wait_ge(terms_done, g * 2 * QC + 2 * (r - 2) + 2)
                    for e in range(2):
                        act.activation(swapped[64 * e:64 * e + 64, r % 2, :],
                                       proj[bank_of(n)][64 - 64 * e:128 - 64 * e, :], ACT.Copy)\
                           .then_inc(swap_done, 1)

                def q_high(n):
                    m, c, r = head_of(n), n // NH, n - n // NH
                    if m > GH1:
                        return
                    act.wait_ge(rot_done, g * QC + (r + 1))
                    act.activation(q_hi[:, m, c * HALF:c * HALF + HALF], rot[:, r % 2, :],
                                   ACT.Copy, scale=SCALE1 if m < GH1 else 1.0).then_inc(q_hi_done, 1)

                def v_high(c):
                    act.wait_ge(x_ready, g * CH + (V_CHUNK[c] + 1))
                    act.activation(v_hi[:, c * HALF:c * HALF + HALF], X[V_CHUNK[c] % 2][:, :], ACT.Copy)\
                       .then_inc(hi_done, 1)

                with act.Fori(0, KV1, 1) as g:
                    for n in range(NH + 1):
                        if n < NH:
                            exchange(n)
                        if n >= 2:
                            q_high(n - 2)
                    for step in range(PER + 5):
                        if step == 1:
                            v_high(0)
                        if step == FIRST + 3:
                            v_high(1)
                        if 1 <= step < PER + 1:
                            u = step - 1
                            n = (tile_of(u) + 1) * P
                            act.wait_ge(max_done, g * PER + (u + 1))
                            if u >= RP:
                                act.wait_ge(x_ready, g * CH + chunk_at(u - RP) + chunks_of(tile_of(u - RP)))
                            act.activation(prob[:, u % RP, 0:n], S[u % 2][:, 0:n], ACT.Exp,
                                           bias=neg_max[:, u % 8:u % 8 + 1],
                                           accum_out=sums[:, u % 8:u % 8 + 1]).then_inc(exp_done, 1)
                        if 3 <= step < PER + 3:
                            u = step - 3
                            i, p = tile_of(u), u // 2
                            if p >= RX:
                                act.wait_ge(o_ready, g * PAIRS + (p - RX + 1))
                            for c in range(chunks_of(i)):
                                m = chunk_at(u) + c
                                js = slice(4 * c, min(4 * c + 4, i + 1))
                                act.wait_ge(x_ready, g * CH + (m + 1))
                                act.activation(p_hi[:, p % RX, js, u % 2, :],
                                               X[m % 2][:, 0:(js.stop - js.start) * P]
                                               .rearrange("p (a c) -> p a c", c=P),
                                               ACT.Copy).then_inc(hi_done, 1)
                        if 2 <= step < PER + 2 and not by_dve(step - 2):
                            u = step - 2
                            n = (tile_of(u) + 1) * P
                            act.wait_ge(rinv_done, g * PER + (u + 1))
                            act.activation(prob[:, u % RP, 0:n], prob[:, u % RP, 0:n], ACT.Copy,
                                           scale=rinv[:, u % 8:u % 8 + 1]).then_inc(norm_done[False], 1)
                        if step >= 6 and step % 2 == 0:
                            p = (step - 6) // 2
                            i, h = tile_of(2 * p), 2 * p % GH1
                            act.wait_ge(o_ready, g * PAIRS + (p + 1))
                            if p % 8 == 0:
                                act.wait_ge(y_ready.sem, y_ready.at(g, NC * NK if p else NK))
                            act.activation(o_hi[:, h:h + 2, (i % 4) * P:(i % 4) * P + P],
                                           O[p % 2][:, 0:2 * P].rearrange("p (h c) -> p h c", h=2),
                                           ACT.Copy).then_inc(o_hi_done, 1)
                        if chunk_in_step(step - 1) is not None:
                            exchange(chunk_in_step(step - 1))
                        if chunk_in_step(step - 4) is not None:
                            q_high(chunk_in_step(step - 4))

            @block.vector
            def _(dve):
                y_done.prime(dve)
                o_lo_done.prime(dve)
                def rope_terms(n):
                    m, c, r = head_of(n), n // NH, n - n // NH
                    if m > GH1:
                        return
                    sl, b = slice(c * HALF, c * HALF + HALF), r % 2
                    dve.wait_ge(swap_done, g * 2 * QC + 2 * r + 2)
                    if r >= 2:
                        dve.wait_ge(rot_done, g * QC + (r - 1))
                    dve.tensor_tensor(t1[:, b, :], proj[bank_of(n)], rope_c[:, sl], ALU.mult)\
                       .then_inc(terms_done, 1)
                    dve.tensor_tensor(t2[:, b, :], swapped[:, b, :], rope_s[:, sl], ALU.mult)\
                       .then_inc(terms_done, 1)

                def add_y(g, c, m):
                    n = (NK if c == 0 else 0) + m
                    at = acc[:, m, c * HALF:c * HALF + HALF]
                    dve.wait_ge(y_ready.sem, y_ready.at(g, n + 1))
                    dve.wait_ge(y_done.sem, y_done.at(g, n))
                    dve.tensor_tensor(at, O[m][:, :], at, ALU.add).then_inc(y_done.sem, 1)

                def q_low(n):
                    m, c, r = head_of(n), n // NH, n - n // NH
                    if m > GH1:
                        return
                    sl = slice(c * HALF, c * HALF + HALF)
                    dve.wait_ge(q_hi_done, g * QC + (r + 1))
                    dve.scalar_tensor_tensor(q_lo[:, m, sl], rot[:, r % 2, :],
                                             SCALE1 if m < GH1 else 1.0, f32(q_hi[:, m, sl]),
                                             ALU.mult, ALU.subtract).then_inc(q_lo_done, 1)

                def v_low(c):
                    sl = slice(c * HALF, c * HALF + HALF)
                    dve.wait_ge(hi_done, g * CH + (V_CHUNK[c] + 1))
                    dve.tensor_tensor(v_lo[:, sl], X[V_CHUNK[c] % 2][:, :], f32(v_hi[:, sl]), ALU.subtract)\
                       .then_inc(lo_done, 1)

                with dve.Fori(0, KV1, 1) as g:
                    for n in range(NH + 1):
                        if n < NH:
                            rope_terms(n)
                        if n >= 2:
                            q_low(n - 2)
                    for step in range(PER + 6):
                        if 2 <= step < PER + 2:
                            u = step - 2
                            dve.wait_ge(exp_done, g * PER + (u + 1))
                            dve.reciprocal(rinv[:, u % 8:u % 8 + 1], sums[:, u % 8:u % 8 + 1])\
                               .then_inc(rinv_done, 1)
                            if by_dve(u):
                                n = (tile_of(u) + 1) * P
                                dve.wait_ge(rinv_done, g * PER + (u + 1))
                                dve.tensor_scalar(prob[:, u % RP, 0:n], prob[:, u % RP, 0:n],
                                                  rinv[:, u % 8:u % 8 + 1], None, ALU.mult)\
                                   .then_inc(norm_done[True], 1)
                        if step < PER:
                            u = step
                            n = (tile_of(u) + 1) * P
                            dve.wait_ge(scores_ready, g * PER + (u + 1))
                            dve.tensor_reduce(neg_max[:, u % 8:u % 8 + 1], S[u % 2][:, 0:n], AX.X,
                                              ALU.max, negate=True).then_inc(max_done, 1)
                        if chunk_in_step(step - 2) is not None:
                            rope_terms(chunk_in_step(step - 2))
                        if chunk_in_step(step - 5) is not None:
                            q_low(chunk_in_step(step - 5))
                        if step == 1:
                            v_low(0)
                        if step == FIRST + 3:
                            v_low(1)
                        if 3 <= step < PER + 3:
                            u = step - 3
                            i, p = tile_of(u), u // 2
                            for c in range(chunks_of(i)):
                                m = chunk_at(u) + c
                                js = slice(4 * c, min(4 * c + 4, i + 1))
                                dve.wait_ge(hi_done, g * CH + (m + 1))
                                dve.tensor_tensor(p_lo[:, p % RX, js, u % 2, :],
                                                  X[m % 2][:, 0:(js.stop - js.start) * P]
                                                  .rearrange("p (a c) -> p a c", c=P),
                                                  f32(p_hi[:, p % RX, js, u % 2, :]),
                                                  ALU.subtract).then_inc(lo_done, 1)
                        if 6 <= step < PER + 5 and step % 2 == 0:
                            p = (step - 6) // 2
                            i, h = tile_of(2 * p), 2 * p % GH1
                            sl = slice((i % 4) * P, (i % 4) * P + P)
                            dve.wait_ge(o_hi_done, g * PAIRS + (p + 1))
                            dve.tensor_tensor(o_lo[:, h:h + 2, sl],
                                              O[p % 2][:, 0:2 * P].rearrange("p (h c) -> p h c", h=2),
                                              f32(o_hi[:, h:h + 2, sl]), ALU.subtract)\
                               .then_inc(o_lo_done.sem, 1)
                        if step < NK:
                            add_y(g, 1, step)
                        if step == FIRST + 5:
                            for m in range(NK):
                                add_y(g, 0, m)
                for m in range(NK):
                    add_y(KV1, 1, m)


def combine1(nc, xT, sT, gT, out):
    PIECES = [(k, slice(c * HALF, c * HALF + HALF)) for c in range(NC) for k in range(NK)]
    with Scope(nc) as s:
        prod = s.sb("c1_prod", [P, NK, T], F32)
        res = s.sb("c1_res", [P, NK, T], F32)
        step, stored = s.sem("c1_step"), s.sem("c1_stored")
        with nc.Block() as block:

            @block.vector
            def _(dve):
                for n, (k, sl) in enumerate(PIECES):
                    dve.tensor_tensor(prod[:, k, sl], sT[:, k, sl], gT[:, k, sl], ALU.mult)\
                       .then_inc(step, 1)
                    dve.wait_ge(step, 2 * n + 1)
                    dve.tensor_tensor(res[:, k, sl], xT[:, k, sl], prod[:, k, sl], ALU.add)\
                       .then_inc(step, 1)

            @block.sync
            def _(sp):
                for n, (k, sl) in enumerate(PIECES):
                    sp.wait_ge(step, 2 * n + 2)
                    sp.dma_start(out[k, :, sl], res[:, k, sl]).then_inc(stored, 16)
                sp.wait_ge(stored, 16 * len(PIECES))


def build(nc, a):
    with Scope(nc) as s:
        ident = s.sb("ident", [P, P], F32)
        ident_bf = s.sb("ident_bf", [P, P], BF16)
        mask = s.sb("mask", [P, P], BF16)
        xT = s.sb("xT", [P, NK, T], F32)
        xn_hi = s.sb("xn_hi", [P, NK, T], F32R)
        xn_lo = s.sb("xn_lo", [P, NK, T], F32R)
        sT = s.sb("sT", [P, NK, T], F32)
        bo = s.sb("bo", [P, NK], F32)
        s_down = s.sb("s_down", [P, NK], F32)
        wr = s.sb("wr", [P, NK, E1], F32)
        earlier = s.sb("earlier", [P, E1 * E1], F32)
        wo_hi = s.sb("wo_hi", [P, NK, D], F32R)
        wo_lo = s.sb("wo_lo", [P, NK, D], F32R)

        with Scope(nc) as s0:
            qT = s0.sb("qT", [P, H0 // 2, T], F32R)
            kT = s0.sb("kT", [P, H0 // 2, T], F32R)
            v3 = s0.sb("v3", [P, NT, H0, PARTS0, DH0], BF16)
            with Scope(nc) as s1:
                x_tok = s1.sb("x_tok", [P, NT, D], F32)
                w0 = s1.sb("w0", [P, NK, 3 * D], F32)
                w0_hi = s1.sb("w0_hi", [P, NK, 3 * D], F32R)
                w0_lo = s1.sb("w0_lo", [P, NK, 3 * D], F32R)
                wo = s1.sb("wo", [P, NK, D], F32)
                bias = s1.sb("bias", [P, 3 * D], F32)
                mask_f32 = s1.sb("mask_f32", [P, P], F32)
                rope_c = s1.sb("rope0_c", [P, NT, 2, DH0], F32)
                rope_s = s1.sb("rope0_s", [P, NT, 2, DH0], F32)
                x_loaded, ident_loaded, w0_loaded, rest_loaded = (s1.sem("x_loaded"), s1.sem("ident_loaded"),
                                                                  s1.sem("w0_loaded"), s1.sem("rest_loaded"))
                w_hi_done, w_lo_done, mask_done = s1.sem("w0_hi_done"), s1.sem("w0_lo_done"), s1.sem("mask_done")
                rest = [(wo[:, :, :], a["wo0"]), (bias[:, :], a["bias0"].partition_broadcast(P)),
                        (rope_c[:, :, :, :], a["rope0_c"]), (rope_s[:, :, :, :], a["rope0_s"]),
                        (mask_f32[:, :], a["mask"]), (xT[:, :, :], a["xT"]), (bo[:, :], a["bo"]),
                        (s_down[:, :], a["s_down"]), (wr[:, :, :], a["wr"]), (earlier[:, :], a["earlier"])]
                loads = [(x_loaded, [(x_tok[:, :, :], a["x_tok"])]), (ident_loaded, [(ident[:, :], a["ident"])]),
                         (w0_loaded, [(w0[:, :, :], a["w0"])]), (rest_loaded, rest)]
                splits = ((w0, w0_hi, w0_lo, w0_loaded, 16), (wo, wo_hi, wo_lo, rest_loaded, 16 * len(rest)))

                def weights_hi(act):
                    for src, hi, _, sem, value in splits:
                        act.wait_ge(sem, value)
                        act.activation(hi[:, :, :], src[:, :, :], ACT.Copy).then_inc(w_hi_done, 1)

                def weights_lo(pool):
                    for n, (src, hi, lo, _, _) in enumerate(splits):
                        pool.wait_ge(w_hi_done, n + 1)
                        pool.tensor_tensor(lo[:, :, :], src[:, :, :], f32(hi[:, :, :]),
                                           ALU.subtract).then_inc(w_lo_done, 1)
                    pool.tensor_copy(mask[:, :], mask_f32[:, :]).then_inc(mask_done, 1)
                    pool.tensor_copy(ident_bf[:, :], ident[:, :]).then_inc(mask_done, 1)
                layer_norm(nc, "l0_", x_tok, xn_hi, xn_lo, ident, loads, weights_hi, weights_lo)
                project0(nc, xn_hi, xn_lo, w0_hi, w0_lo, bias, rope_c, rope_s, ident, qT, kT, v3)
            att = s0.sb("att", [P, NT, D], F32)
            attention0(nc, qT, kT, v3, ident, ident_bf, mask, att)
            project_out0(nc, att, wo_hi, wo_lo, bo, ident, sT)
        gT = s.sb("gT", [P, NK, T], F32)
        gated_ffn(nc, "f0", FT0, a["wf0"], WCOLS, -ZERO_POINT, a["sf0"], s_down, xn_hi, xn_lo, None, gT)
        with Scope(nc) as s1:
            x_tok = s1.sb("x1_tok", [P, NT, D], F32)
            combine0(nc, xT, sT, gT, ident, x_tok)
            layer_norm(nc, "l1_", x_tok, xn_hi, xn_lo, ident)
        with Scope(nc) as s1:
            raw = s1.sb("wqkv_raw", [P, GWCOLS1], F32)
            w_hi = s1.sb("wqkv_hi", [P, NK, (GH1 + 2) * P], F32R)
            w_lo = s1.sb("wqkv_lo", [P, NK, (GH1 + 2) * P], F32R)
            rope_c = s1.sb("rope1_c", [P, T], F32)
            rope_s = s1.sb("rope1_s", [P, T], F32)
            wo1_hi = s1.sb("wo1_hi", [P, GH1, D], F32R)
            wo1_lo = s1.sb("wo1_lo", [P, GH1, D], F32R)
            o_hi = s1.sb("o1_hi", [P, GH1, HALF], F32R)
            o_lo = s1.sb("o1_lo", [P, GH1, HALF], F32R)
            wqkv_loaded, wqkv_split = s1.sem("wqkv_loaded"), s1.sem("wqkv_split")

            def load_first_head(sp):
                sp.dma_start(raw[:, :], a["wqkv1"][0, :, :]).then_inc(wqkv_loaded, 16)
                sp.dma_start(rope_c[:, :], a["rope1_c"]).then_inc(wqkv_loaded, 16)
                sp.dma_start(rope_s[:, :], a["rope1_s"]).then_inc(wqkv_loaded, 16)

            def split_first_head(pool):
                flat = lambda v: v.rearrange("p a b -> p (a b)")
                pool.memset(sT[:, :, :], 0.0).then_inc(wqkv_split, 1)
                for t in (wo1_hi, wo1_lo, o_hi, o_lo):
                    pool.memset(f32(t[:, :, :]), 0.0).then_inc(wqkv_split, 1)
                pool.wait_ge(wqkv_loaded, 48)
                pool.tensor_copy(flat(w_hi[:, :, :]), raw[:, :]).then_inc(wqkv_split, 1)
                pool.wait_ge(wqkv_split, 6)
                pool.tensor_tensor(flat(w_lo[:, :, :]), raw[:, :], f32(flat(w_hi[:, :, :])),
                                   ALU.subtract).then_inc(wqkv_split, 1)
            with Scope(nc) as s2:
                gate_hi = s2.sb("gate_hi", [P, T], F32R)
                route1(nc, xn_hi, xn_lo, wr, earlier, ident, gate_hi)
                gated_ffn(nc, "f1", FT1, a["wf1"], WCOLS + P, 0.0, None, None, xn_hi, xn_lo, gate_hi, gT,
                          load_first_head, split_first_head)
            attention1(nc, xn_hi, xn_lo, raw, w_hi, w_lo, wo1_hi, wo1_lo, o_hi, o_lo, a["wqkv1"], a["wo1"], rope_c, rope_s,
                       ident, ident_bf, mask, sT)
        combine1(nc, xT, sT, gT, a["out"])


def _constants():
    f = np.float32
    c = {"ident": np.eye(P, dtype=f), "mask": np.triu(np.full((P, P), MASKED, f), 1)}
    pos = np.arange(T, dtype=f)

    def tables(base, half):
        inv = f(1.0) / f(base) ** (np.arange(half, dtype=f) / f(half))
        ang = (pos[:, None] * inv[None, :]).astype(f)
        return np.cos(ang.astype(np.float64)).astype(f), np.sin(ang.astype(np.float64)).astype(f)
    cos, sin = tables(10000.0, DH0 // 2)
    c0 = np.repeat(cos, 2, 1)
    s0 = np.stack([-sin, sin], -1).reshape(T, DH0)
    for name, tab in (("rope0_c", c0), ("rope0_s", s0)):
        both = np.stack([tab * f(SCALE0), tab], 1)
        c[name] = np.ascontiguousarray(both.reshape(NT, P, 2, DH0).transpose(1, 0, 2, 3)).astype(f)
    cos, sin = tables(10000.0, DH1 // 2)
    c["rope1_c"] = np.ascontiguousarray(np.concatenate([cos, cos], 1).T)
    c["rope1_s"] = np.ascontiguousarray(np.concatenate([-sin, sin], 1).T)
    b, e = np.meshgrid(np.arange(E1), np.arange(E1))
    c["earlier"] = np.broadcast_to((b < e).astype(f).reshape(1, -1), (P, E1 * E1)).copy()
    sel = np.zeros((FT1 + 1, P, P), f)
    for tile in range(FT1):
        for j in range(P):
            row = tile * P + j
            x = row // F1 if row < E1 * F1 else E1
            sel[tile, x, j] = sel[tile, 32 + x, j] = 1.0
    return c, sel


def _rows(w):
    return np.ascontiguousarray(w.reshape(w.shape[0] // P, P, w.shape[1]).transpose(1, 0, 2))


def _ffn_tiles(wg, wu, wd, tiles):
    def pad(w):
        out = np.zeros(((tiles + 1) * P, D), w.dtype)
        out[:w.shape[0]] = w
        return out.reshape(tiles + 1, P, D)
    def up(w):
        return pad(w).reshape(tiles + 1, P, NK, P).transpose(0, 3, 2, 1).reshape(tiles + 1, P, NK * P)
    return np.ascontiguousarray(np.concatenate([pad(wd.T), up(wg), up(wu)], 2))


def kernel(**inputs):
    import concourse.bacc as _bacc
    from concourse.bass_utils import run_bass_kernel_spmd as _run
    x = {k: np.asarray(v) for k, v in inputs.items()}
    arrays, sel = _constants()
    x0 = x["L0_attn_x"].reshape(T, D)
    arrays["x_tok"] = np.ascontiguousarray(x0.reshape(NT, P, D).transpose(1, 0, 2))
    arrays["xT"] = _rows(x0.T)
    arrays["w0"] = _rows(np.concatenate([x["L0_attn_Wq"].T, x["L0_attn_Wk"].T, x["L0_attn_Wv"].T], 1))
    arrays["wo0"] = _rows(x["L0_attn_Wo"].T)
    arrays["bias0"] = np.concatenate([x["L0_attn_bq"], x["L0_attn_bk"], x["L0_attn_bv"]])
    arrays["bo"] = np.ascontiguousarray(x["L0_attn_bo"].reshape(NK, P).T)
    arrays["s_down"] = np.ascontiguousarray(x["L0_ffn_s_down"].reshape(NK, P).T)
    arrays["wf0"] = _ffn_tiles(x["L0_ffn_wq_gate"], x["L0_ffn_wq_up"], x["L0_ffn_wq_down"], FT0)
    sf = np.zeros((2, (FT0 + 1) * P), np.float32)
    sf[0, :HID0], sf[1, :HID0] = x["L0_ffn_s_gate"], x["L0_ffn_s_up"]
    arrays["sf0"] = np.ascontiguousarray(sf.reshape(2, FT0 + 1, P).transpose(1, 2, 0))
    arrays["wr"] = _rows(x["L1_ffn_Wr"].T)
    wg = np.concatenate([x["L1_ffn_Wg"].reshape(E1 * F1, D), x["L1_ffn_Wsg"]])
    wu = np.concatenate([x["L1_ffn_Wu"].reshape(E1 * F1, D), x["L1_ffn_Wsu"]])
    wd = np.concatenate([x["L1_ffn_Wd"].transpose(1, 0, 2).reshape(D, E1 * F1), x["L1_ffn_Wsd"]], 1)
    arrays["wf1"] = np.concatenate([_ffn_tiles(wg, wu, wd, FT1), sel], 2)
    q = x["L1_attn_Wq"].reshape(NK, P, KV1, GH1 * DH1)
    k = x["L1_attn_Wk"].reshape(NK, P, KV1, DH1)
    v = x["L1_attn_Wv"].reshape(NK, P, KV1, DH1)
    arrays["wqkv1"] = np.zeros((KV1 + 1, P, GWCOLS1), q.dtype)
    arrays["wqkv1"][:KV1] = np.concatenate([q, k, v], 3).transpose(2, 1, 0, 3).reshape(KV1, P, GWCOLS1)
    arrays["wo1"] = np.ascontiguousarray(
        x["L1_attn_Wo"].reshape(KV1, GH1, P, D).transpose(0, 2, 1, 3).reshape(KV1, P, GH1 * D))

    nc = _bacc.Bacc("TRN2", target_bir_lowering=False, num_devices=1)
    a = {n: nc.dram_tensor(f"in_{n}", v.shape, mybir.dt.from_np(v.dtype), kind="ExternalInput").ap()
         for n, v in arrays.items()}
    a["out"] = nc.dram_tensor("out_x", (NK, P, T), F32, kind="ExternalOutput").ap()
    build(nc, a)
    r = _run(nc, [{f"in_{n}": v for n, v in arrays.items()}], core_ids=[0])
    out = np.asarray(r.results[0]["out_x"])
    return np.ascontiguousarray(out.reshape(D, T).T).reshape(1, T, D)
```
